# Optimizing a Trainium2 kernel written in Bass

```python
import numpy as np
import jax
import jax.numpy as jnp

def _softmax(x, axis=-1):
    return jax.nn.softmax(x, axis=axis)

def _gelu(x):
    return jax.nn.gelu(x, approximate=True)

def _silu(x):
    return jax.nn.silu(x)

def _sigmoid(x):
    return jax.nn.sigmoid(x)

def _layernorm(x, axis=-1, eps=1e-05):
    m = jnp.mean(x, axis=axis, keepdims=True)
    v = jnp.var(x, axis=axis, keepdims=True)
    return (x - m) / jnp.sqrt(v + eps)

def _scatter_add(tgt, idx, src, axis=0):
    return tgt.at[idx].add(src)

def _segment_sum(src, seg, n):
    return jax.ops.segment_sum(src, seg, n)
kernel_name = 'mk_adaln_d4_jaxref_r8_73f7c4'

def setup_inputs(seed: int=0):
    np.random.seed(seed)
    _w = jnp.asarray

    def _L0_attn_setup():
        import jax, jax.numpy as jnp
        import numpy as np
        D_MODEL = 128
        NUM_HEADS = 16
        HEAD_DIM = D_MODEL // NUM_HEADS
        EPS = 1e-08
        key = jax.random.key(seed)
        ks = jax.random.split(key, 6)
        B, T = (4, 256)
        s = 0.02
        return {'x': jax.random.normal(ks[0], (B, T, D_MODEL), dtype=jnp.float32), 'Wq': jax.random.normal(ks[1], (D_MODEL, D_MODEL), dtype=jnp.float32) * s, 'Wk': jax.random.normal(ks[2], (D_MODEL, D_MODEL), dtype=jnp.float32) * s, 'Wv': jax.random.normal(ks[3], (D_MODEL, D_MODEL), dtype=jnp.float32) * s, 'Wo': jax.random.normal(ks[4], (D_MODEL, D_MODEL), dtype=jnp.float32) * s, 'bo': jnp.zeros((D_MODEL,), dtype=jnp.float32)}
    _L0_attn_in = _L0_attn_setup()

    def _L0_ffn_setup():
        import jax, jax.numpy as jnp
        import numpy as np
        D_MODEL = 128
        FF = 512
        E = 8
        TOP_K = 2
        CAP_FACTOR = 1.25
        B, T = (4, 256)

        def _moe_forward(x, gate_w, gate_b, w1, b1, w2, b2):
            Bb, Tt, d = x.shape
            S = Bb * Tt
            C = int(CAP_FACTOR * S / E)
            xf = x.reshape(S, d)
            logits = xf @ gate_w + gate_b
            probs = jax.nn.softmax(logits, axis=1)
            topk_p, topk_i = jax.lax.top_k(probs, TOP_K)
            topk_pn = topk_p / jnp.sum(topk_p, axis=1, keepdims=True)
            rows = jnp.arange(S)
            w_te = jnp.zeros((S, E), xf.dtype).at[rows[:, None], topk_i].set(topk_pn)
            mask = jnp.zeros((S, E), bool).at[rows[:, None], topk_i].set(True)
            rank = jnp.cumsum(mask.astype(jnp.int32), axis=0)
            slot = jnp.where(mask & (rank <= C), rank - 1, C)
            e_grid = jnp.broadcast_to(jnp.arange(E), (S, E))
            t_grid = jnp.broadcast_to(rows[:, None], (S, E))
            buf = jnp.full((E, C + 1), S, jnp.int32).at[e_grid, slot].set(t_grid)
            idx = buf[:, :C]
            valid = idx < S
            x_pad = jnp.concatenate([xf, jnp.zeros((1, d), xf.dtype)], axis=0)
            xin = x_pad[idx]
            h = jax.nn.relu(jnp.einsum('ecd,edh->ech', xin, w1) + b1[:, None, :])
            out = jnp.einsum('ech,ehd->ecd', h, w2) + b2[:, None, :]
            w_pad = jnp.concatenate([w_te, jnp.zeros((1, E), xf.dtype)], axis=0)
            tok_w = w_pad[idx, jnp.arange(E)[:, None]]
            out = out * jnp.where(valid, tok_w, 0.0)[:, :, None]
            final = jnp.zeros((S + 1, d), xf.dtype).at[idx.reshape(-1)].add(out.reshape(-1, d))[:S]
            return final.reshape(Bb, Tt, d)
        key = jax.random.key(seed)
        ks = jax.random.split(key, 7)
        s = 0.02
        return {'x': jax.random.normal(ks[0], (B, T, D_MODEL), jnp.float32), 'gate_w': jax.random.normal(ks[1], (D_MODEL, E), jnp.float32) * s, 'gate_b': jnp.zeros((E,), jnp.float32), 'w1': jax.random.normal(ks[2], (E, D_MODEL, FF), jnp.float32) * s, 'b1': jnp.zeros((E, FF), jnp.float32), 'w2': jax.random.normal(ks[3], (E, FF, D_MODEL), jnp.float32) * s, 'b2': jnp.zeros((E, D_MODEL), jnp.float32)}
    _L0_ffn_in = _L0_ffn_setup()
    _L0_c = _w((lambda *s: np.random.randn(*s).astype(np.float32) * 0.05)(4, 128))
    _L0_wmod = _w((lambda *s: np.random.randn(*s).astype(np.float32) * 0.05)(128, 6 * 128) * 128 ** (-0.5))

    def _L1_attn_setup():
        import jax, jax.numpy as jnp
        import numpy as np
        from math import log2, floor
        HEADS = 16
        DIM_HEAD = 64
        SCALE = DIM_HEAD ** (-0.5)

        def _get_slopes(heads):

            def pow2_slopes(n):
                start = 2 ** (-2 ** (-(log2(n) - 3)))
                return [start * start ** i for i in range(n)]
            if log2(heads).is_integer():
                return pow2_slopes(heads)
            c = 2 ** floor(log2(heads))
            return pow2_slopes(c) + pow2_slopes(2 * c)[0::2][:heads - c]
        key = jax.random.key(seed)
        k1, k2, k3 = jax.random.split(key, 3)
        b, n, dim = (2, 256, 128)
        inner = HEADS * DIM_HEAD
        x = jax.random.normal(k1, (b, n, dim), dtype=jnp.float32)
        w_qkv = jax.random.normal(k2, (dim, 3 * inner), dtype=jnp.float32) * dim ** (-0.5)
        w_out = jax.random.normal(k3, (inner, dim), dtype=jnp.float32) * inner ** (-0.5)
        b_out = jnp.zeros((dim,), dtype=jnp.float32)
        return {'x': x, 'w_qkv': w_qkv, 'w_out': w_out, 'b_out': b_out}
    _L1_attn_in = _L1_attn_setup()

    def _L1_ffn_setup():
        import jax, jax.numpy as jnp
        import numpy as np
        DIM = 128
        INTER = 256
        E = 8
        TOPK = 2
        ROUTE_SCALE = 1.0

        def _mlp(x, w1, w2, w3):
            h = jax.nn.silu(x @ w1.T) * (x @ w3.T)
            return h @ w2.T
        key = jax.random.key(seed)
        ks = jax.random.split(key, 10)
        s_in = 0.02
        return {'x': jax.random.normal(ks[0], (4, 256, DIM), dtype=jnp.float32), 'gate_w': jax.random.normal(ks[1], (E, DIM), dtype=jnp.float32) * s_in, 'gate_bias': jax.random.normal(ks[2], (E,), dtype=jnp.float32) * 0.01, 'w1': jax.random.normal(ks[3], (E, INTER, DIM), dtype=jnp.float32) * s_in, 'w2': jax.random.normal(ks[4], (E, DIM, INTER), dtype=jnp.float32) * s_in, 'w3': jax.random.normal(ks[5], (E, INTER, DIM), dtype=jnp.float32) * s_in, 'sw1': jax.random.normal(ks[6], (INTER, DIM), dtype=jnp.float32) * s_in, 'sw2': jax.random.normal(ks[7], (DIM, INTER), dtype=jnp.float32) * s_in, 'sw3': jax.random.normal(ks[8], (INTER, DIM), dtype=jnp.float32) * s_in}
    _L1_ffn_in = _L1_ffn_setup()
    _L1_c = _w((lambda *s: np.random.randn(*s).astype(np.float32) * 0.05)(4, 128))
    _L1_wmod = _w((lambda *s: np.random.randn(*s).astype(np.float32) * 0.05)(128, 6 * 128) * 128 ** (-0.5))

    def _L2_attn_setup():
        import jax, jax.numpy as jnp
        import numpy as np
        import math
        EMBED_DIM = 128
        NUM_HEADS = 16
        DEPTH = 12
        HEAD_DIM = EMBED_DIM // NUM_HEADS // 2
        LAMBDA_INIT = 0.8 - 0.6 * math.exp(-0.3 * DEPTH)
        SCALE = HEAD_DIM ** (-0.5)
        RMS_EPS = 1e-05
        BATCH, SEQ = (2, 256)

        def _freqs(seq_len):
            angle = 1.0 / 10000.0 ** jnp.linspace(0.0, 1.0, HEAD_DIM // 2)
            idx = jnp.arange(seq_len, dtype=jnp.float32)
            f = idx[:, None] * angle[None, :]
            return (jnp.cos(f), jnp.sin(f))

        def _rope_interleaved(x, cos, sin):
            x1, x2 = (x[..., 0::2], x[..., 1::2])
            c = cos[None, :, None, :]
            s = sin[None, :, None, :]
            o1 = x1 * c - x2 * s
            o2 = x1 * s + x2 * c
            return jnp.stack([o1, o2], axis=-1).reshape(x.shape)

        def _forward(x, Wq, Wk, Wv, Wo, lambda_q1, lambda_k1, lambda_q2, lambda_k2, rms_weight):
            b, t, _ = x.shape
            q = (x @ Wq.T).reshape(b, t, 2 * NUM_HEADS, HEAD_DIM)
            k = (x @ Wk.T).reshape(b, t, 2 * NUM_HEADS, HEAD_DIM)
            v = (x @ Wv.T).reshape(b, t, NUM_HEADS, 2, HEAD_DIM)
            cos, sin = _freqs(t)
            q = _rope_interleaved(q, cos, sin)
            k = _rope_interleaved(k, cos, sin)
            q = q.reshape(b, t, NUM_HEADS, 2, HEAD_DIM)
            k = k.reshape(b, t, NUM_HEADS, 2, HEAD_DIM)
            q1, q2 = (q[..., 0, :], q[..., 1, :])
            k1, k2 = (k[..., 0, :], k[..., 1, :])
            v12 = v.reshape(b, t, NUM_HEADS, 2 * HEAD_DIM)

            def attend(qh, kh):
                scores = jnp.einsum('bthd,bshd->bhts', qh, kh) * SCALE
                p = jax.nn.softmax(scores, axis=-1)
                return jnp.einsum('bhts,bshe->bthe', p, v12)
            attn1 = attend(q1, k1)
            attn2 = attend(q2, k2)
            lam = jnp.exp(jnp.sum(lambda_q1 * lambda_k1)) - jnp.exp(jnp.sum(lambda_q2 * lambda_k2)) + LAMBDA_INIT
            a = attn1 - lam * attn2
            a = a * jax.lax.rsqrt(jnp.mean(a * a, axis=-1, keepdims=True) + RMS_EPS) * rms_weight
            a = a * (1.0 - LAMBDA_INIT)
            a = a.reshape(b, t, NUM_HEADS * 2 * HEAD_DIM)
            return a @ Wo.T
        key = jax.random.key(seed)
        ks = jax.random.split(key, 9)
        std = EMBED_DIM ** (-0.5)
        return {'x': jax.random.normal(ks[0], (BATCH, SEQ, EMBED_DIM), jnp.float32), 'Wq': jax.random.normal(ks[1], (EMBED_DIM, EMBED_DIM), jnp.float32) * std, 'Wk': jax.random.normal(ks[2], (EMBED_DIM, EMBED_DIM), jnp.float32) * std, 'Wv': jax.random.normal(ks[3], (EMBED_DIM, EMBED_DIM), jnp.float32) * std, 'Wo': jax.random.normal(ks[4], (EMBED_DIM, EMBED_DIM), jnp.float32) * std, 'lambda_q1': jax.random.normal(ks[5], (HEAD_DIM,), jnp.float32) * 0.1, 'lambda_k1': jax.random.normal(ks[6], (HEAD_DIM,), jnp.float32) * 0.1, 'lambda_q2': jax.random.normal(ks[7], (HEAD_DIM,), jnp.float32) * 0.1, 'lambda_k2': jax.random.normal(ks[8], (HEAD_DIM,), jnp.float32) * 0.1, 'rms_weight': jnp.ones((2 * HEAD_DIM,), jnp.float32)}
    _L2_attn_in = _L2_attn_setup()

    def _L2_ffn_setup():
        import jax, jax.numpy as jnp
        import numpy as np
        D_MODEL = 128
        key = jax.random.key(seed)
        k_x, k_w, k_a1, k_a2 = jax.random.split(key, 4)
        x = jax.random.normal(k_x, (4, 256, D_MODEL), dtype=jnp.float32)
        weight = jax.random.normal(k_w, (D_MODEL, D_MODEL), dtype=jnp.float32) * 0.02
        aux_weight1 = jax.random.normal(k_a1, (D_MODEL, D_MODEL), dtype=jnp.float32) * 0.02
        aux_weight2 = jax.random.normal(k_a2, (D_MODEL, D_MODEL), dtype=jnp.float32) * 0.02
        bias = jnp.zeros((D_MODEL,), dtype=jnp.float32)
        return {'x': x, 'weight': weight, 'aux_weight1': aux_weight1, 'aux_weight2': aux_weight2, 'bias': bias}
    _L2_ffn_in = _L2_ffn_setup()
    _L2_c = _w((lambda *s: np.random.randn(*s).astype(np.float32) * 0.05)(4, 128))
    _L2_wmod = _w((lambda *s: np.random.randn(*s).astype(np.float32) * 0.05)(128, 6 * 128) * 128 ** (-0.5))

    def _L3_attn_setup():
        import jax, jax.numpy as jnp
        import numpy as np
        B, N, D = (4, 512, 128)
        H, F = (16, 32)
        HD = D // H
        EPS_ATTN = 1e-08
        EPS_LN = 1e-05

        def _layernorm(x, gamma, beta):
            mu = jnp.mean(x, axis=-1, keepdims=True)
            var = jnp.var(x, axis=-1, keepdims=True)
            return (x - mu) * jax.lax.rsqrt(var + EPS_LN) * gamma + beta
        key = jax.random.key(seed)
        ks = jax.random.split(key, 10)

        def kaiming(k, shape):
            fan_in = shape[1]
            return jax.random.normal(k, shape, jnp.float32) * jnp.sqrt(2.0 / fan_in)
        pm = jax.random.normal(ks[0], (H, HD, F), jnp.float32)
        return {'x': jax.random.normal(ks[1], (B, N, D), jnp.float32), 'proj': pm, 'w_qkv': kaiming(ks[2], (3 * D, D)), 'w_out': kaiming(ks[3], (D, D)), 'b_out': jnp.zeros((D,), jnp.float32), 'gamma': jnp.ones((D,), jnp.float32), 'beta': jnp.zeros((D,), jnp.float32), 'w1': kaiming(ks[4], (4 * D, D)), 'b1': jnp.zeros((4 * D,), jnp.float32), 'w2': kaiming(ks[5], (D, 4 * D)), 'b2': jnp.zeros((D,), jnp.float32)}
    _L3_attn_in = _L3_attn_setup()

    def _L3_ffn_setup():
        import jax, jax.numpy as jnp
        import numpy as np
        NUM_EXPERTS = 8
        TOP_K = 2
        CAPACITY_FACTOR = 1.25
        key = jax.random.key(seed)
        ks = jax.random.split(key, 5)
        B, S, D, H, E = (4, 256, 128, 256, NUM_EXPERTS)
        scale = 0.02
        return {'x': jax.random.normal(ks[0], (B, S, D), dtype=jnp.float32), 'gate_w': jax.random.normal(ks[1], (E, D), dtype=jnp.float32) * scale, 'gate_proj_w': jax.random.normal(ks[2], (E, H, D), dtype=jnp.float32) * scale, 'up_proj_w': jax.random.normal(ks[3], (E, H, D), dtype=jnp.float32) * scale, 'down_proj_w': jax.random.normal(ks[4], (E, D, H), dtype=jnp.float32) * scale}
    _L3_ffn_in = _L3_ffn_setup()
    _L3_c = _w((lambda *s: np.random.randn(*s).astype(np.float32) * 0.05)(4, 128))
    _L3_wmod = _w((lambda *s: np.random.randn(*s).astype(np.float32) * 0.05)(128, 6 * 128) * 128 ** (-0.5))
    _d = {'L0_attn_x': _L0_attn_in['x'], 'L0_attn_Wq': _L0_attn_in['Wq'], 'L0_attn_Wk': _L0_attn_in['Wk'], 'L0_attn_Wv': _L0_attn_in['Wv'], 'L0_attn_Wo': _L0_attn_in['Wo'], 'L0_attn_bo': _L0_attn_in['bo'], 'L0_ffn_gate_w': _L0_ffn_in['gate_w'], 'L0_ffn_gate_b': _L0_ffn_in['gate_b'], 'L0_ffn_w1': _L0_ffn_in['w1'], 'L0_ffn_b1': _L0_ffn_in['b1'], 'L0_ffn_w2': _L0_ffn_in['w2'], 'L0_ffn_b2': _L0_ffn_in['b2'], 'L0_c': _L0_c, 'L0_wmod': _L0_wmod, 'L1_attn_w_qkv': _L1_attn_in['w_qkv'], 'L1_attn_w_out': _L1_attn_in['w_out'], 'L1_attn_b_out': _L1_attn_in['b_out'], 'L1_ffn_gate_w': _L1_ffn_in['gate_w'], 'L1_ffn_gate_bias': _L1_ffn_in['gate_bias'], 'L1_ffn_w1': _L1_ffn_in['w1'], 'L1_ffn_w2': _L1_ffn_in['w2'], 'L1_ffn_w3': _L1_ffn_in['w3'], 'L1_ffn_sw1': _L1_ffn_in['sw1'], 'L1_ffn_sw2': _L1_ffn_in['sw2'], 'L1_ffn_sw3': _L1_ffn_in['sw3'], 'L1_c': _L1_c, 'L1_wmod': _L1_wmod, 'L2_attn_Wq': _L2_attn_in['Wq'], 'L2_attn_Wk': _L2_attn_in['Wk'], 'L2_attn_Wv': _L2_attn_in['Wv'], 'L2_attn_Wo': _L2_attn_in['Wo'], 'L2_attn_lambda_q1': _L2_attn_in['lambda_q1'], 'L2_attn_lambda_k1': _L2_attn_in['lambda_k1'], 'L2_attn_lambda_q2': _L2_attn_in['lambda_q2'], 'L2_attn_lambda_k2': _L2_attn_in['lambda_k2'], 'L2_attn_rms_weight': _L2_attn_in['rms_weight'], 'L2_ffn_weight': _L2_ffn_in['weight'], 'L2_ffn_aux_weight1': _L2_ffn_in['aux_weight1'], 'L2_ffn_aux_weight2': _L2_ffn_in['aux_weight2'], 'L2_ffn_bias': _L2_ffn_in['bias'], 'L2_c': _L2_c, 'L2_wmod': _L2_wmod, 'L3_attn_proj': _L3_attn_in['proj'], 'L3_attn_w_qkv': _L3_attn_in['w_qkv'], 'L3_attn_w_out': _L3_attn_in['w_out'], 'L3_attn_b_out': _L3_attn_in['b_out'], 'L3_attn_gamma': _L3_attn_in['gamma'], 'L3_attn_beta': _L3_attn_in['beta'], 'L3_attn_w1': _L3_attn_in['w1'], 'L3_attn_b1': _L3_attn_in['b1'], 'L3_attn_w2': _L3_attn_in['w2'], 'L3_attn_b2': _L3_attn_in['b2'], 'L3_ffn_gate_w': _L3_ffn_in['gate_w'], 'L3_ffn_gate_proj_w': _L3_ffn_in['gate_proj_w'], 'L3_ffn_up_proj_w': _L3_ffn_in['up_proj_w'], 'L3_ffn_down_proj_w': _L3_ffn_in['down_proj_w'], 'L3_c': _L3_c, 'L3_wmod': _L3_wmod}
    _x0 = _d['L0_attn_x']
    _d['L0_attn_x'] = jax.random.normal(jax.random.fold_in(jax.random.key(seed), 1), (4, 512, 128), dtype=_x0.dtype)
    del _x0
    return _d

def reference(L0_attn_x, L0_attn_Wq, L0_attn_Wk, L0_attn_Wv, L0_attn_Wo, L0_attn_bo, L0_ffn_gate_w, L0_ffn_gate_b, L0_ffn_w1, L0_ffn_b1, L0_ffn_w2, L0_ffn_b2, L0_c, L0_wmod, L1_attn_w_qkv, L1_attn_w_out, L1_attn_b_out, L1_ffn_gate_w, L1_ffn_gate_bias, L1_ffn_w1, L1_ffn_w2, L1_ffn_w3, L1_ffn_sw1, L1_ffn_sw2, L1_ffn_sw3, L1_c, L1_wmod, L2_attn_Wq, L2_attn_Wk, L2_attn_Wv, L2_attn_Wo, L2_attn_lambda_q1, L2_attn_lambda_k1, L2_attn_lambda_q2, L2_attn_lambda_k2, L2_attn_rms_weight, L2_ffn_weight, L2_ffn_aux_weight1, L2_ffn_aux_weight2, L2_ffn_bias, L2_c, L2_wmod, L3_attn_proj, L3_attn_w_qkv, L3_attn_w_out, L3_attn_b_out, L3_attn_gamma, L3_attn_beta, L3_attn_w1, L3_attn_b1, L3_attn_w2, L3_attn_b2, L3_ffn_gate_w, L3_ffn_gate_proj_w, L3_ffn_up_proj_w, L3_ffn_down_proj_w, L3_c, L3_wmod):

    def _L0_attn_ref(x, Wq, Wk, Wv, Wo, bo):
        import jax, jax.numpy as jnp
        import numpy as np
        D_MODEL = 128
        NUM_HEADS = 16
        HEAD_DIM = D_MODEL // NUM_HEADS
        EPS = 1e-08
        B, T, _ = x.shape
        H, D = (NUM_HEADS, HEAD_DIM)
        scale = jnp.sqrt(jnp.asarray(D, dtype=x.dtype))
        q = (x @ Wq.T).reshape(B, T, H, D).transpose(0, 2, 1, 3)
        k = (x @ Wk.T).reshape(B, T, H, D).transpose(0, 2, 1, 3)
        v = (x @ Wv.T).reshape(B, T, H, D).transpose(0, 2, 1, 3)
        s = jnp.einsum('bhtd,bhsd->bhts', q, k) / scale
        m = jnp.max(s, axis=-1, keepdims=True)
        e = jnp.exp(s - m)
        num = jnp.einsum('bhts,bhsd->bhtd', e, v)
        den = jnp.sum(e, axis=-1, keepdims=True) + EPS
        out = (num / den).transpose(0, 2, 1, 3).reshape(B, T, H * D)
        return out @ Wo.T + bo

    def _L0_ffn_ref(x, gate_w, gate_b, w1, b1, w2, b2):
        import jax, jax.numpy as jnp
        import numpy as np
        D_MODEL = 128
        FF = 512
        E = 8
        TOP_K = 2
        CAP_FACTOR = 1.25
        B, T = (4, 256)

        def _moe_forward(x, gate_w, gate_b, w1, b1, w2, b2):
            Bb, Tt, d = x.shape
            S = Bb * Tt
            C = int(CAP_FACTOR * S / E)
            xf = x.reshape(S, d)
            logits = xf @ gate_w + gate_b
            probs = jax.nn.softmax(logits, axis=1)
            topk_p, topk_i = jax.lax.top_k(probs, TOP_K)
            topk_pn = topk_p / jnp.sum(topk_p, axis=1, keepdims=True)
            rows = jnp.arange(S)
            w_te = jnp.zeros((S, E), xf.dtype).at[rows[:, None], topk_i].set(topk_pn)
            mask = jnp.zeros((S, E), bool).at[rows[:, None], topk_i].set(True)
            rank = jnp.cumsum(mask.astype(jnp.int32), axis=0)
            slot = jnp.where(mask & (rank <= C), rank - 1, C)
            e_grid = jnp.broadcast_to(jnp.arange(E), (S, E))
            t_grid = jnp.broadcast_to(rows[:, None], (S, E))
            buf = jnp.full((E, C + 1), S, jnp.int32).at[e_grid, slot].set(t_grid)
            idx = buf[:, :C]
            valid = idx < S
            x_pad = jnp.concatenate([xf, jnp.zeros((1, d), xf.dtype)], axis=0)
            xin = x_pad[idx]
            h = jax.nn.relu(jnp.einsum('ecd,edh->ech', xin, w1) + b1[:, None, :])
            out = jnp.einsum('ech,ehd->ecd', h, w2) + b2[:, None, :]
            w_pad = jnp.concatenate([w_te, jnp.zeros((1, E), xf.dtype)], axis=0)
            tok_w = w_pad[idx, jnp.arange(E)[:, None]]
            out = out * jnp.where(valid, tok_w, 0.0)[:, :, None]
            final = jnp.zeros((S + 1, d), xf.dtype).at[idx.reshape(-1)].add(out.reshape(-1, d))[:S]
            return final.reshape(Bb, Tt, d)
        return _moe_forward(x, gate_w, gate_b, w1, b1, w2, b2)

    def _L1_attn_ref(x, w_qkv, w_out, b_out):
        import jax, jax.numpy as jnp
        import numpy as np
        from math import log2, floor
        HEADS = 16
        DIM_HEAD = 64
        SCALE = DIM_HEAD ** (-0.5)

        def _get_slopes(heads):

            def pow2_slopes(n):
                start = 2 ** (-2 ** (-(log2(n) - 3)))
                return [start * start ** i for i in range(n)]
            if log2(heads).is_integer():
                return pow2_slopes(heads)
            c = 2 ** floor(log2(heads))
            return pow2_slopes(c) + pow2_slopes(2 * c)[0::2][:heads - c]
        b, n, _ = x.shape
        qkv = x @ w_qkv
        q, k, v = jnp.split(qkv, 3, axis=-1)

        def to_heads(t):
            return t.reshape(b, n, HEADS, DIM_HEAD).transpose(0, 2, 1, 3)
        q, k, v = map(to_heads, (q, k, v))
        q = q * SCALE
        sim = jnp.einsum('bhid,bhjd->bhij', q, k)
        slopes = jnp.asarray(_get_slopes(HEADS), dtype=sim.dtype)[:, None, None]
        i = jnp.arange(n)
        rel = -jnp.abs(i[None, :] - i[:, None]).astype(sim.dtype)
        sim = sim + rel[None, :, :] * slopes
        causal = jnp.triu(jnp.ones((n, n), dtype=bool), 1)
        mask_value = -jnp.finfo(sim.dtype).max
        sim = jnp.where(causal, mask_value, sim)
        attn = jax.nn.softmax(sim, axis=-1)
        out = jnp.einsum('bhij,bhjd->bhid', attn, v)
        out = out.transpose(0, 2, 1, 3).reshape(b, n, HEADS * DIM_HEAD)
        return out @ w_out + b_out

    def _L1_ffn_ref(x, gate_w, gate_bias, w1, w2, w3, sw1, sw2, sw3):
        import jax, jax.numpy as jnp
        import numpy as np
        DIM = 128
        INTER = 256
        E = 8
        TOPK = 2
        ROUTE_SCALE = 1.0

        def _mlp(x, w1, w2, w3):
            h = jax.nn.silu(x @ w1.T) * (x @ w3.T)
            return h @ w2.T
        shape = x.shape
        xt = x.reshape(-1, DIM)
        T = xt.shape[0]
        logits = xt @ gate_w.T
        scores = jax.nn.softmax(logits.astype(jnp.float32), axis=-1)
        original_scores = scores
        biased = scores + gate_bias
        _, indices = jax.lax.top_k(biased, TOPK)
        weights = jnp.take_along_axis(original_scores, indices, axis=1)
        weights = (weights * ROUTE_SCALE).astype(x.dtype)
        combine = (jax.nn.one_hot(indices, E, dtype=weights.dtype) * weights[..., None]).sum(axis=1)
        y = jnp.zeros_like(xt)
        for e in range(E):
            y = y + _mlp(xt, w1[e], w2[e], w3[e]) * combine[:, e:e + 1]
        z = _mlp(xt, sw1, sw2, sw3)
        return (y + z).reshape(shape)

    def _L2_attn_ref(x, Wq, Wk, Wv, Wo, lambda_q1, lambda_k1, lambda_q2, lambda_k2, rms_weight):
        import jax, jax.numpy as jnp
        import numpy as np
        import math
        EMBED_DIM = 128
        NUM_HEADS = 16
        DEPTH = 12
        HEAD_DIM = EMBED_DIM // NUM_HEADS // 2
        LAMBDA_INIT = 0.8 - 0.6 * math.exp(-0.3 * DEPTH)
        SCALE = HEAD_DIM ** (-0.5)
        RMS_EPS = 1e-05
        BATCH, SEQ = (2, 256)

        def _freqs(seq_len):
            angle = 1.0 / 10000.0 ** jnp.linspace(0.0, 1.0, HEAD_DIM // 2)
            idx = jnp.arange(seq_len, dtype=jnp.float32)
            f = idx[:, None] * angle[None, :]
            return (jnp.cos(f), jnp.sin(f))

        def _rope_interleaved(x, cos, sin):
            x1, x2 = (x[..., 0::2], x[..., 1::2])
            c = cos[None, :, None, :]
            s = sin[None, :, None, :]
            o1 = x1 * c - x2 * s
            o2 = x1 * s + x2 * c
            return jnp.stack([o1, o2], axis=-1).reshape(x.shape)

        def _forward(x, Wq, Wk, Wv, Wo, lambda_q1, lambda_k1, lambda_q2, lambda_k2, rms_weight):
            b, t, _ = x.shape
            q = (x @ Wq.T).reshape(b, t, 2 * NUM_HEADS, HEAD_DIM)
            k = (x @ Wk.T).reshape(b, t, 2 * NUM_HEADS, HEAD_DIM)
            v = (x @ Wv.T).reshape(b, t, NUM_HEADS, 2, HEAD_DIM)
            cos, sin = _freqs(t)
            q = _rope_interleaved(q, cos, sin)
            k = _rope_interleaved(k, cos, sin)
            q = q.reshape(b, t, NUM_HEADS, 2, HEAD_DIM)
            k = k.reshape(b, t, NUM_HEADS, 2, HEAD_DIM)
            q1, q2 = (q[..., 0, :], q[..., 1, :])
            k1, k2 = (k[..., 0, :], k[..., 1, :])
            v12 = v.reshape(b, t, NUM_HEADS, 2 * HEAD_DIM)

            def attend(qh, kh):
                scores = jnp.einsum('bthd,bshd->bhts', qh, kh) * SCALE
                p = jax.nn.softmax(scores, axis=-1)
                return jnp.einsum('bhts,bshe->bthe', p, v12)
            attn1 = attend(q1, k1)
            attn2 = attend(q2, k2)
            lam = jnp.exp(jnp.sum(lambda_q1 * lambda_k1)) - jnp.exp(jnp.sum(lambda_q2 * lambda_k2)) + LAMBDA_INIT
            a = attn1 - lam * attn2
            a = a * jax.lax.rsqrt(jnp.mean(a * a, axis=-1, keepdims=True) + RMS_EPS) * rms_weight
            a = a * (1.0 - LAMBDA_INIT)
            a = a.reshape(b, t, NUM_HEADS * 2 * HEAD_DIM)
            return a @ Wo.T
        return _forward(x, Wq, Wk, Wv, Wo, lambda_q1, lambda_k1, lambda_q2, lambda_k2, rms_weight)

    def _L2_ffn_ref(x, weight, aux_weight1, aux_weight2, bias):
        import jax, jax.numpy as jnp
        import numpy as np
        D_MODEL = 128
        h = jnp.einsum('btc,cd->btd', x, weight)
        h = jnp.einsum('btc,cd->btd', h, aux_weight1)
        h = jnp.einsum('btc,cd->btd', h, aux_weight2)
        return jnp.tanh(h + bias)

    def _L3_attn_ref(x, proj, w_qkv, w_out, b_out, gamma, beta, w1, b1, w2, b2):
        import jax, jax.numpy as jnp
        import numpy as np
        B, N, D = (4, 512, 128)
        H, F = (16, 32)
        HD = D // H
        EPS_ATTN = 1e-08
        EPS_LN = 1e-05

        def _layernorm(x, gamma, beta):
            mu = jnp.mean(x, axis=-1, keepdims=True)
            var = jnp.var(x, axis=-1, keepdims=True)
            return (x - mu) * jax.lax.rsqrt(var + EPS_LN) * gamma + beta
        residual = x
        b, n, d = x.shape
        qkv = x @ w_qkv.T
        q, k, v = jnp.split(qkv, 3, axis=-1)

        def to_heads(t):
            return t.reshape(b, n, H, HD).transpose(0, 2, 1, 3)
        q, k, v = (to_heads(q), to_heads(k), to_heads(v))
        q_f = jax.nn.elu(jnp.einsum('bhnd,hdf->bhnf', q, proj)) + 1.0
        k_f = jax.nn.elu(jnp.einsum('bhnd,hdf->bhnf', k, proj)) + 1.0
        kv = jnp.einsum('bhnf,bhnd->bhfd', k_f, v)
        attn = jnp.einsum('bhnf,bhfd->bhnd', q_f, kv)
        k_sum = jnp.sum(k_f, axis=2)
        z = 1.0 / (jnp.einsum('bhnf,bhf->bhn', q_f, k_sum) + EPS_ATTN)
        attn = attn * z[..., None]
        attn = attn.transpose(0, 2, 1, 3).reshape(b, n, d)
        x = residual + attn @ w_out.T + b_out
        x = _layernorm(x, gamma, beta)
        h = jax.nn.gelu(x @ w1.T + b1, approximate=False)
        x = x + h @ w2.T + b2
        x = _layernorm(x, gamma, beta)
        return x

    def _L3_ffn_ref(x, gate_w, gate_proj_w, up_proj_w, down_proj_w):
        import jax, jax.numpy as jnp
        import numpy as np
        NUM_EXPERTS = 8
        TOP_K = 2
        CAPACITY_FACTOR = 1.25
        B, S, D = x.shape
        E, K = (NUM_EXPERTS, TOP_K)
        T = B * S
        xf = x.reshape(T, D)
        logits = xf @ gate_w.T
        probs = jax.nn.softmax(logits, axis=-1)
        top_p, top_i = jax.lax.top_k(probs, K)
        w = top_p / (jnp.sum(top_p, axis=-1, keepdims=True) + 1e-09)
        capacity = int(CAPACITY_FACTOR * T / E)
        oh = jax.nn.one_hot(top_i, E, dtype=jnp.int32)
        rank = jnp.cumsum(oh, axis=0) - 1
        my_rank = jnp.sum(rank * oh, axis=-1)
        keep = (my_rank < capacity).astype(w.dtype)
        comb = jnp.einsum('tk,tke->te', w * keep, oh.astype(w.dtype))
        out = jnp.zeros_like(xf)
        for e in range(E):
            g = jax.nn.silu(xf @ gate_proj_w[e].T)
            u = xf @ up_proj_w[e].T
            y = g * u @ down_proj_w[e].T
            out = out + comb[:, e:e + 1] * y
        return out.reshape(B, S, D)
    x = L0_attn_x
    mod = (_silu(L0_c) @ L0_wmod).reshape(L0_c.shape[0], 6, 1, -1)
    sa, ca, ga, sb, cb, gb = (mod[:, 0], mod[:, 1], mod[:, 2], mod[:, 3], mod[:, 4], mod[:, 5])
    ga = (2 * (ga >= 0) - 1) * jnp.maximum(jnp.abs(ga), 0.25)
    gb = (2 * (gb >= 0) - 1) * jnp.maximum(jnp.abs(gb), 0.25)
    h = _layernorm(x, axis=-1) * (1 + ca) + sa
    x = x + ga * _L0_attn_ref(h, L0_attn_Wq, L0_attn_Wk, L0_attn_Wv, L0_attn_Wo, L0_attn_bo)
    h = _layernorm(x, axis=-1) * (1 + cb) + sb
    x = x + gb * _L0_ffn_ref(h, L0_ffn_gate_w, L0_ffn_gate_b, L0_ffn_w1, L0_ffn_b1, L0_ffn_w2, L0_ffn_b2)
    mod = (_silu(L1_c) @ L1_wmod).reshape(L1_c.shape[0], 6, 1, -1)
    sa, ca, ga, sb, cb, gb = (mod[:, 0], mod[:, 1], mod[:, 2], mod[:, 3], mod[:, 4], mod[:, 5])
    ga = (2 * (ga >= 0) - 1) * jnp.maximum(jnp.abs(ga), 0.25)
    gb = (2 * (gb >= 0) - 1) * jnp.maximum(jnp.abs(gb), 0.25)
    h = _layernorm(x, axis=-1) * (1 + ca) + sa
    x = x + ga * _L1_attn_ref(h, L1_attn_w_qkv, L1_attn_w_out, L1_attn_b_out)
    h = _layernorm(x, axis=-1) * (1 + cb) + sb
    x = x + gb * _L1_ffn_ref(h, L1_ffn_gate_w, L1_ffn_gate_bias, L1_ffn_w1, L1_ffn_w2, L1_ffn_w3, L1_ffn_sw1, L1_ffn_sw2, L1_ffn_sw3)
    mod = (_silu(L2_c) @ L2_wmod).reshape(L2_c.shape[0], 6, 1, -1)
    sa, ca, ga, sb, cb, gb = (mod[:, 0], mod[:, 1], mod[:, 2], mod[:, 3], mod[:, 4], mod[:, 5])
    ga = (2 * (ga >= 0) - 1) * jnp.maximum(jnp.abs(ga), 0.25)
    gb = (2 * (gb >= 0) - 1) * jnp.maximum(jnp.abs(gb), 0.25)
    h = _layernorm(x, axis=-1) * (1 + ca) + sa
    x = x + ga * _L2_attn_ref(h, L2_attn_Wq, L2_attn_Wk, L2_attn_Wv, L2_attn_Wo, L2_attn_lambda_q1, L2_attn_lambda_k1, L2_attn_lambda_q2, L2_attn_lambda_k2, L2_attn_rms_weight)
    h = _layernorm(x, axis=-1) * (1 + cb) + sb
    x = x + gb * _L2_ffn_ref(h, L2_ffn_weight, L2_ffn_aux_weight1, L2_ffn_aux_weight2, L2_ffn_bias)
    mod = (_silu(L3_c) @ L3_wmod).reshape(L3_c.shape[0], 6, 1, -1)
    sa, ca, ga, sb, cb, gb = (mod[:, 0], mod[:, 1], mod[:, 2], mod[:, 3], mod[:, 4], mod[:, 5])
    ga = (2 * (ga >= 0) - 1) * jnp.maximum(jnp.abs(ga), 0.25)
    gb = (2 * (gb >= 0) - 1) * jnp.maximum(jnp.abs(gb), 0.25)
    h = _layernorm(x, axis=-1) * (1 + ca) + sa
    x = x + ga * _L3_attn_ref(h, L3_attn_proj, L3_attn_w_qkv, L3_attn_w_out, L3_attn_b_out, L3_attn_gamma, L3_attn_beta, L3_attn_w1, L3_attn_b1, L3_attn_w2, L3_attn_b2)
    h = _layernorm(x, axis=-1) * (1 + cb) + sb
    x = x + gb * _L3_ffn_ref(h, L3_ffn_gate_w, L3_ffn_gate_proj_w, L3_ffn_up_proj_w, L3_ffn_down_proj_w)
    return x

_drawn_inputs = setup_inputs


def setup_inputs(seed=0):
    import zlib

    import numpy as np

    out = dict(_drawn_inputs(seed))
    spreads = {'L0_attn_bo': (0.0, 0.277),
     'L0_ffn_gate_b': (0.0, 0.516),
     'L0_ffn_b1': (0.0, 0.8),
     'L0_ffn_b2': (0.0, 0.578),
     'L1_attn_b_out': (0.0, 0.294),
     'L2_attn_rms_weight': (1.0, 0.6),
     'L2_ffn_bias': (0.0, 0.333),
     'L3_attn_b_out': (0.0, 0.315),
     'L3_attn_gamma': (1.0, 0.2),
     'L3_attn_beta': (0.0, 0.1),
     'L3_attn_b1': (0.0, 0.555),
     'L3_attn_b2': (0.0, 0.592)}
    factors = {'L0_attn_Wq': 8.0,
     'L0_attn_Wk': 8.0,
     'L0_attn_Wv': 8.0,
     'L0_attn_Wo': 8.0,
     'L0_ffn_gate_w': 3.736,
     'L0_ffn_w1': 6.761,
     'L0_ffn_w2': 5.234,
     'L1_ffn_gate_w': 8.0,
     'L1_ffn_gate_bias': 8.0,
     'L1_ffn_w1': 8.0,
     'L1_ffn_w2': 8.0,
     'L1_ffn_w3': 8.0,
     'L1_ffn_sw1': 8.0,
     'L1_ffn_sw2': 8.0,
     'L1_ffn_sw3': 8.0,
     'L2_attn_lambda_q1': 8.0,
     'L2_attn_lambda_k1': 8.0,
     'L2_attn_lambda_q2': 8.0,
     'L2_attn_lambda_k2': 8.0,
     'L2_ffn_weight': 8.0,
     'L2_ffn_aux_weight1': 8.0,
     'L2_ffn_aux_weight2': 8.0,
     'L3_attn_proj': 3.951,
     'L3_ffn_gate_w': 8.0,
     'L3_ffn_gate_proj_w': 8.0,
     'L3_ffn_up_proj_w': 8.0,
     'L3_ffn_down_proj_w': 8.0}
    for name, (base, spread) in spreads.items():
        noise = np.random.default_rng([zlib.crc32(name.encode()), seed]).standard_normal(out[name].shape)
        drawn = base * np.exp(spread * noise) if base else spread * noise
        out[name] = jnp.asarray(drawn.astype(out[name].dtype))
    for name, factor in factors.items():
        out[name] = (out[name] * factor).astype(out[name].dtype)
    return out
```

```python
import concourse.bass as bass
from concourse import mybir
import numpy as np

F32 = mybir.dt.float32
F32R = mybir.dt.float32r
BF16 = mybir.dt.bfloat16
ACT = mybir.ActivationFunctionType
ALU = mybir.AluOpType
X = mybir.AxisListType.X

P = 128
B, T = 4, 512
N = B * T
LN_EPS = 1e-5
EXPERTS = 8
CAPACITY = int(1.25 * N / EXPERTS)
LAMBDA_INIT = 0.8 - 0.6 * float(np.exp(-0.3 * 12))
MAX_ROW = 96
START = 64

SQUARES = ["L0_Wq", "L0_Wk", "L0_Wv", "L0_Wo",
           "L2_Wq", "L2_Wqs", "L2_Wk", "L2_Wks", "L2_Wv", "L2_Wo", "L2_f0", "L2_f1", "L2_f2",
           "L3_Wq", "L3_Wk", "L3_Wv", "L3_Wo"]
COLUMNS = ["L0_bo", "L1_bo", "L2_rms", "L2_bias", "L3_bo", "L3_gamma", "L3_beta", "L3_b2",
           "L3_b1_0", "L3_b1_1", "L3_b1_2", "L3_b1_3"]
SHIFT_A, SCALE_A, GATE_A, SHIFT_B, SCALE_B, GATE_B = range(6)


class Signal:

    def __init__(self, nc, name):
        self.sem = nc.alloc_semaphore(name)
        self.base = START

    def at(self, n):
        return n + self.base

    def end(self, n):
        self.base += n


def cols(c):
    return slice(c * T, (c + 1) * T)


def setup_phase(nc, g):
    D, s = g.dram, g.s
    with g.sb("wmod", [P, 4, 6 * P], F32) as wmod, \
         g.sb("cond", [P, 16], F32) as cond, \
         g.sb("cond_t", [P, 3, 16], F32) as ct, \
         g.sb("lam_in", [P, 4, 4], F32) as lam_in, \
         g.sb("lam_t", [P, 2, 4], F32) as lam_t, \
         g.sb("lam_s", [P, 4], F32) as lam_s, \
         g.sb("gate_t", [P, 4, 2, 2, B], F32) as gt, \
         g.pb("mod_ps", [P, 512], F32) as mod_ps, \
         nc.Block() as block:

        @block.sync
        def _(sp):
            sp.dma_start(cond[:], D["cT"]).then_inc(s["dma"].sem, 16)
            for i in range(4):
                sp.dma_start(wmod[:, i], D[f"L{i}_wmod"]).then_inc(s["dma"].sem, 16)
            sp.dma_start(lam_in[:], D["lambdas"].partition_broadcast(P)).then_inc(s["dma"].sem, 16)
            sp.dma_start(g.xT[:], D["xT"]).then_inc(s["dma"].sem, 16)
            sp.dma_start(g.squares[:], D["squares"]).then_inc(s["dma"].sem, 16)
            sp.dma_start(g.columns[:], D["columns"]).then_inc(s["dma"].sem, 16)
            sp.dma_start(g.consts[:], D["consts"]).then_inc(s["dma"].sem, 16)
            sp.wait_ge(s["dma"].sem, s["dma"].at(16 * 10))
            sp.dma_start(g.scratch["alibi"], D["alibi"]).then_inc(s["store"].sem, 16)
            sp.wait_ge(s["store"].sem, s["store"].at(16))

        @block.scalar
        def _(act):
            act.wait_ge(s["dma"].sem, s["dma"].at(16 * 10))
            nc.scalar.activation(ct[:, 0], cond[:], ACT.Exp, scale=-1.0).then_inc(s["act"].sem, 1)
            act.wait_ge(s["vec"].sem, s["vec"].at(8))
            nc.scalar.activation(lam_s[:, 2:4], lam_s[:, 0:2], ACT.Exp).then_inc(s["act"].sem, 1)

        @block.vector
        def _(dve):
            n = 0
            dve.wait_ge(s["act"].sem, s["act"].at(1))

            def after(ins):
                nonlocal n
                n += 1
                ins.then_inc(s["vec"].sem, 1)
                dve.wait_ge(s["vec"].sem, s["vec"].at(n))

            after(nc.vector.tensor_scalar(ct[:, 1], ct[:, 0], 1.0, None, ALU.add))
            after(nc.vector.reciprocal(ct[:, 2], ct[:, 1]))
            after(nc.vector.tensor_tensor(g.cs[:], cond[:], ct[:, 2], ALU.mult))
            after(nc.vector.tensor_tensor(lam_t[:, 0], lam_in[:, 0], lam_in[:, 1], ALU.mult))
            after(nc.vector.tensor_tensor(lam_t[:, 1], lam_in[:, 2], lam_in[:, 3], ALU.mult))
            after(nc.vector.tensor_reduce(lam_s[:, 0:2], lam_t[:], X, ALU.add))
            after(nc.vector.memset(g.eps[:, 0:1], LN_EPS))
            after(nc.vector.memset(g.eps[:, 1:2], 0.0))
            dve.wait_ge(s["act"].sem, s["act"].at(2))
            after(nc.vector.tensor_scalar(lam_s[:, 0:1], lam_s[:, 3:4], -LAMBDA_INIT, None, ALU.add))
            after(nc.vector.tensor_tensor(g.neg_lam[:], lam_s[:, 0:1], lam_s[:, 2:3], ALU.subtract))
            dve.wait_ge(s["pe"].sem, s["pe"].at(1))
            after(nc.vector.tensor_copy(g.mod[:], mod_ps[:, 0:96].rearrange(
                "p (l j b) -> p l j b", l=4, j=6)))
            for j in (SCALE_A, SCALE_B):
                after(nc.vector.tensor_scalar(g.mod[:, :, j], g.mod[:, :, j], 1.0, None, ALU.add))
            for i, j in enumerate((GATE_A, GATE_B)):
                gate = g.mod[:, :, j]
                sign, size = gt[:, :, i, 0], gt[:, :, i, 1]
                after(nc.vector.tensor_scalar(sign, gate, 0.0, 2.0, ALU.is_ge, ALU.mult))
                after(nc.vector.tensor_scalar(size, gate, -1.0, 0.25, ALU.mult, ALU.max))
                after(nc.vector.tensor_tensor(size, size, gate, ALU.max))
                after(nc.vector.tensor_scalar(sign, sign, -1.0, None, ALU.add))
                after(nc.vector.tensor_tensor(gate, size, sign, ALU.mult))
            for layer, name in ((0, "L0_bo"), (1, "L1_bo")):
                after(nc.vector.tensor_scalar(g.gate_bias[:, layer], g.mod[:, layer, GATE_A],
                                              g.col(name), None, ALU.mult))
            after(nc.vector.tensor_scalar(g.rms_w[:], g.col("L2_rms"), 1.0 - LAMBDA_INIT, None, ALU.mult))
            g.n_vec = n

        @block.tensor
        def _(pe):
            pe.wait_ge(s["vec"].sem, s["vec"].at(3))
            for layer in range(4):
                for j in range(6):
                    at = (layer * 6 + j) * B
                    mm = nc.tensor.matmul(mod_ps[:, at:at + B], wmod[:, layer, j * P:(j + 1) * P],
                                          g.cs[:, layer * B:(layer + 1) * B], start=True, stop=True)
            mm.then_inc(s["pe"].sem, 1)

    s["dma"].end(160)
    s["store"].end(16)
    s["act"].end(2)
    s["vec"].end(g.n_vec)
    s["pe"].end(1)


def norm_phase(nc, g, src, scales, shifts):
    s = g.s
    with g.sb("centred", [P, N], F32) as centred, \
         g.sb("squared", [P, N], F32) as work, \
         g.pb("mean_ps", [P, B, T], F32) as mean, \
         g.pb("var_ps", [P, B, T], F32) as var, \
         nc.Block() as block:

        @block.tensor
        def _(pe):
            for c in range(B):
                nc.tensor.matmul(mean[:, c], g.mean_w, src[:, cols(c)],
                                 start=True, stop=True).then_inc(s["mean"].sem, 1)
            for c in range(B):
                pe.wait_ge(s["square"].sem, s["square"].at(c + 1))
                nc.tensor.matmul(var[:, c], g.mean_w, work[:, cols(c)],
                                 start=True, stop=True).then_inc(s["var"].sem, 1)

        @block.scalar
        def _(act):
            for c in range(B):
                act.wait_ge(s["centre"].sem, s["centre"].at(c + 1))
                nc.scalar.activation(work[:, cols(c)], centred[:, cols(c)], ACT.Square
                                     ).then_inc(s["square"].sem, 1)
            for c in range(B):
                act.wait_ge(s["var"].sem, s["var"].at(c + 1))
                nc.scalar.activation(work[:, cols(c)], var[:, c], ACT.Sqrt, bias=g.eps[:, 0:1]
                                     ).then_inc(s["std"].sem, 1)

        @block.vector
        def _(dve):
            for c in range(B):
                dve.wait_ge(s["mean"].sem, s["mean"].at(c + 1))
                nc.vector.tensor_tensor(centred[:, cols(c)], src[:, cols(c)], mean[:, c],
                                        ALU.subtract).then_inc(s["centre"].sem, 1)
            for c in range(B):
                dve.wait_ge(s["std"].sem, s["std"].at(c + 1))
                nc.vector.reciprocal(work[:, cols(c)], work[:, cols(c)]).then_inc(s["norm"].sem, 1)
                dve.wait_ge(s["norm"].sem, s["norm"].at(3 * c + 1))
                nc.vector.tensor_tensor(work[:, cols(c)], work[:, cols(c)], centred[:, cols(c)],
                                        ALU.mult).then_inc(s["norm"].sem, 1)
                dve.wait_ge(s["norm"].sem, s["norm"].at(3 * c + 2))
                nc.vector.tensor_scalar(g.hT[:, cols(c)], work[:, cols(c)], scales(c), shifts(c),
                                        ALU.mult, ALU.add).then_inc(s["norm"].sem, 1)

    for name in ("mean", "square", "var", "centre", "std"):
        s[name].end(B)
    s["norm"].end(3 * B)


def by_part(tensor, parts):
    return tensor[:].rearrange("p (i t w) -> p i t w", i=B * parts, t=T // P)


def small_head_stacks(g):
    return (g.sb("q_stack", [P, 4, 4, T], F32R), g.sb("k_stack", [P, 4, 4, T], F32R),
            g.sb("v_group", [P, 4, T // P, P], F32))


def small_head_projections(nc, g, stacks, hd, wq, wk, wv, wq_swapped=None, wk_swapped=None):
    s = g.s
    heads = P // hd
    rope = wq_swapped is not None
    per_b = [("q", wq), ("qs", wq_swapped), ("k", wk), ("ks", wk_swapped)] if rope else [("q", wq), ("k", wk)]
    tasks = [(b, kind, w) for b in range(B) for kind, w in per_b + [("v", wv)]]
    n_task = len(tasks) // B
    parts = heads // 16
    q_scr = g.scratch["q"].rearrange("(b e r) t -> b e r t", b=B, e=heads)
    k_scr = g.scratch["k"].rearrange("(b e r) t -> b e r t", b=B, e=heads)
    with g.sb("full", [P, 4 if rope else 2, N], F32) as full, \
         g.sb("hi", [P, 2, N], F32) as hi, \
         g.sb("lo", [P, 2, N], F32) as lo, \
         g.sb("rope", [P, 2, T], F32) as rope_t, \
         g.pb("proj", [P, 8, T], F32) as ps, \
         nc.Block() as block:
        slot = {"q": 0, "k": 1, "qs": 2, "ks": 3}
        hi_r = hi[:].bitcast(F32R)

        @block.gpsimd
        def _(pool):
            qs, ks, vg = stacks
            nc.gpsimd.memset(ks[:].bitcast(F32), 0.0).then_inc(s["zeros"].sem, 1)
            nc.gpsimd.memset(vg[:], 1.0).then_inc(s["zeros"].sem, 1)
            nc.gpsimd.memset(qs[:].bitcast(F32), 0.0).then_inc(s["zeros"].sem, 1)
            pool.wait_ge(s["zeros"].sem, s["zeros"].at(3))
            nc.gpsimd.memset(ks[MAX_ROW:MAX_ROW + 2].bitcast(F32), 1.0).then_inc(s["zeros"].sem, 1)

        @block.tensor
        def _(pe):
            for n, (b, kind, w) in enumerate(tasks):
                if n >= 8:
                    pe.wait_ge(s["evac"].sem, s["evac"].at(n - 7))
                if kind != "v":
                    mm = nc.tensor.matmul(ps[:, n % 8], g.square(w), g.hT[:, cols(b)], start=True, stop=True)
                else:
                    for t in range(T // P):
                        at = b * T + t * P
                        mm = nc.tensor.matmul(ps[:, n % 8, t * P:(t + 1) * P], g.hT[:, at:at + P],
                                              g.square(w), start=True, stop=True)
                mm.then_inc(s["mm"].sem, 1)

        @block.scalar
        def _(act):
            for n, (b, kind, _) in enumerate(tasks):
                act.wait_ge(s["mm"].sem, s["mm"].at(n + 1))
                if kind != "v":
                    nc.scalar.activation(full[:, slot[kind], cols(b)], ps[:, n % 8], ACT.Copy
                                         ).then_inc(s["evac"].sem, 1)
                else:
                    nc.scalar.activation(
                        by_part(g.v_tok, parts)[:, b * parts:(b + 1) * parts],
                        ps[:, n % 8].rearrange("p (t i w) -> p i t w", t=T // P, i=parts), ACT.Copy
                    ).then_inc(s["evac"].sem, 1)

        @block.vector
        def _(dve):
            step = s["vec"]
            n = 0

            def after(ins):
                nonlocal n
                n += 1
                ins.then_inc(step.sem, 1)
                dve.wait_ge(step.sem, step.at(n))

            if rope:
                dve.wait_ge(s["dma"].sem, s["dma"].at(16))
            for b in range(B):
                dve.wait_ge(s["evac"].sem, s["evac"].at(n_task * b + len(per_b)))
                for i in range(2):
                    f = full[:, i, cols(b)]
                    if rope:
                        f2 = full[:, 2 + i, cols(b)]
                        after(nc.vector.tensor_tensor(f, f, rope_t[:, 0], ALU.mult))
                        after(nc.vector.tensor_tensor(f2, f2, rope_t[:, 1], ALU.mult))
                        after(nc.vector.tensor_tensor(f, f, f2, ALU.add))
                    after(nc.vector.tensor_copy(hi_r[:, i, cols(b)], f))
                    nc.vector.tensor_tensor(lo[:, i, cols(b)], f, hi[:, i, cols(b)], ALU.subtract
                                            ).then_inc(s["split"].sem, 1)
            g.n_vec = n

        @block.sync
        def _(sp):
            if rope:
                sp.dma_start(rope_t[:], g.dram["rope"]).then_inc(s["dma"].sem, 16)
            for b in range(B):
                for i, (scr, parts) in enumerate(((q_scr, (hi, hi, lo)), (k_scr, (hi, lo, hi)))):
                    sp.wait_ge(s["split"].sem, s["split"].at(2 * b + i + 1))
                    for r, part in enumerate(parts):
                        sp.dma_start(scr[b, :, r * hd:(r + 1) * hd, :], part[:, i, cols(b)]
                                     ).then_inc(s["store"].sem, 16)
            sp.wait_ge(s["store"].sem, s["store"].at(16 * 6 * B))

    s["zeros"].end(4)
    s["mm"].end(len(tasks))
    s["evac"].end(len(tasks))
    s["vec"].end(g.n_vec)
    s["split"].end(2 * B)
    s["store"].end(16 * 6 * B)
    if rope:
        s["dma"].end(16)


def small_head_attention(nc, g, stacks, hd, scale, differential=False):
    s = g.s
    heads = P // hd
    NG = B * heads // 4
    K1 = 3 * hd
    KT = T // P
    TILES = 4 * KT
    DIVIDE = 5 if differential else 2
    BODY = 4
    q_scr = g.scratch["q"].rearrange("(e r) t -> e r t", r=K1)
    k_scr = g.scratch["k"].rearrange("(e r) t -> e r t", r=K1)
    HD_V = 8
    PAIR = 2 if differential else 1
    v_part, out_part = by_part(g.v_tok, heads // 16), by_part(g.att_tok, heads // 16)
    WIDTH = 4 // PAIR * HD_V
    qs, ks, vg = stacks
    with g.sb("probs", [P, KT, 4, T], F32) as probs, \
         g.sb("neg_max", [P, 2, TILES], F32) as neg_max, \
         g.sb("max_parts", [TILES, 2, 2, P], F32) as max_parts, \
         g.sb("raw", [P, 2, T], F32) as raw, \
         g.sb("recip", [P, KT, 4], F32) as recip, \
         g.sb("second", [P, 2, KT, 2, HD_V], F32) as pair_t, \
         g.pb("scores", [P, 4, T], F32) as sc_ps, \
         g.pb("scoresT", [P, 2, T], F32) as st_ps, \
         g.pb("values", [P, T], F32) as o_ps, \
         g.pb("rawT", [P, KT, 4, 32], F32) as rt_ps, \
         nc.Block() as block:
        mt_ps = rt_ps[:].rearrange("p t j r -> p (t j r)")[0:TILES, 0:P]
        SPLIT = 5

        def group(i, p, d=0):
            i, p = i + (p + d) // BODY, (p + d) % BODY
            if isinstance(i, int) and not 0 <= BODY * i + p < NG:
                return None
            return i, p, i * BODY + p

        def steps(eng, step):
            for i in (-1, 0):
                for p in range(BODY):
                    step(i, p)
            with eng.Fori(1, NG // BODY - 1) as i:
                for p in range(BODY):
                    step(i, p)
            for i in (NG // BODY - 1, NG // BODY):
                for p in range(BODY):
                    step(i, p)

        @block.sync
        def _(sp):
            def step(i, p):
                if at := group(i, p, 3):
                    gi, gp, n = at
                    sp.wait_ge(s["st"].sem, s["st"].at(TILES * (n - 3)))
                    for dst, src in ((qs, q_scr), (ks, k_scr)):
                        sp.dma_start(dst[0:K1, gp].bitcast(F32), src[bass.ds(n * 4, 4)].rearrange("e r t -> r e t")
                                     ).then_inc(s[f"load{gp}"].sem, 16)
                if at := group(i, p, 1):
                    gi, gp, n = at
                    sp.wait_ge(s["max_split"].sem, s["max_split"].at(n + 1))
                    for r in range(2):
                        sp.dma_start(qs[MAX_ROW + r:MAX_ROW + r + 1, gp].bitcast(F32)
                                     .rearrange("o j (t q) -> o (j t) q", t=KT), max_parts[:, gp % 2, r]).then_inc(s[f"rows{gp % 2}"].sem, 16)

            steps(sp, step)

        @block.gpsimd
        def _(pool):
            by_one = g.all_ones[:, 0:KT * WIDTH].rearrange("p (t j d) -> p t j d", t=KT, d=HD_V)

            def step(i, p):
                if at := group(i, p, 1):
                    gi, gp, n = at
                    pool.wait_ge(s["pv"].sem, s["pv"].at(KT * (n - 3)))
                    dst = vg[:, gp].rearrange("p t (j c r) -> p c t j r", c=PAIR, r=32)
                    for c in range(PAIR):
                        src = v_part[:, bass.ds(gi, 1), :, gp * WIDTH:(gp + 1) * WIDTH].rearrange(
                            "p i t (j d) -> p (i t) j d", d=HD_V)
                        nc.gpsimd.tensor_tensor(dst[:, c, :, :, 0:HD_V], src, by_one, ALU.mult
                                                ).then_inc(s["vg"].sem, 1)

            steps(pool, step)

        @block.scalar
        def _(act):
            def step(i, p):
                cur = group(i, p)
                for t in range(TILES):
                    if cur:
                        _, _, n = cur
                        kt, j = t // 4, t % 4
                        act.wait_ge(s["st"].sem, s["st"].at(TILES * n + t + 1))
                        if j == 0:
                            act.wait_ge(s["pv"].sem, s["pv"].at(KT * (n - 1) + kt + 1))
                        nc.scalar.activation(probs[:, kt, j], st_ps[:, t % 2], ACT.Exp, scale=scale
                                             ).then_inc(s["exp"].sem, 1)
                    if t == 4 and (at := group(i, p, -1)):
                        gi, gp, n = at
                        act.wait_ge(s["pv"].sem, s["pv"].at(KT * (n + 1)))
                        act.wait_ge(s["rawT"].sem, s["rawT"].at(n - 1))
                        nc.scalar.activation(raw[:, gp % 2], o_ps[:], ACT.Identity,
                                             bias=g.den_eps(hd)).then_inc(s["raw"].sem, 1)

            steps(act, step)

        @block.vector
        def _(dve):
            def divide(at, first):
                gi, gp, n = at
                done = lambda ins: ins.then_inc(s["divide"].sem, 1)
                dve.wait_ge(s["divide"].sem, s["divide"].at(DIVIDE * n + first))
                out = out_part[:, bass.ds(gi, 1), :, gp * WIDTH:(gp + 1) * WIDTH].rearrange(
                    "p i t (j d) -> p (i t) j d", d=HD_V)
                spread = [P, KT, 4 // PAIR, HD_V]
                if first == 0:
                    dve.wait_ge(s["rawT"].sem, s["rawT"].at(n + 1))
                    done(nc.vector.reciprocal(recip[:], rt_ps[:, :, :, HD_V]))
                elif not differential:
                    done(nc.vector.tensor_tensor(out, rt_ps[:, :, :, 0:HD_V],
                                                 recip[:].unsqueeze(3).broadcast_to(spread), ALU.mult))
                elif first == 1:
                    done(nc.vector.tensor_scalar(recip[:, :, 1::2], recip[:, :, 1::2], g.neg_lam[:], None,
                                                 ALU.mult))
                elif first < 4:
                    c = first - 2
                    done(nc.vector.tensor_tensor(pair_t[:, c], rt_ps[:, :, c::2, 0:HD_V],
                                                 recip[:, :, c::2].unsqueeze(3).broadcast_to(spread),
                                                 ALU.mult))
                else:
                    done(nc.vector.tensor_tensor(out, pair_t[:, 0], pair_t[:, 1], ALU.add))

            def step(i, p):
                ahead, next_, last = group(i, p, 2), group(i, p, 1), group(i, p, -1)
                for t in range(TILES):
                    if ahead:
                        _, gp, n = ahead
                        dve.wait_ge(s["scores"].sem, s["scores"].at(TILES * n + t + 1))
                        if t == 0:
                            dve.wait_ge(s["maxT"].sem, s["maxT"].at(n - 1))
                        nc.vector.tensor_reduce(neg_max[:, gp % 2, t:t + 1], sc_ps[:, t % 4], X, ALU.max,
                                                negate=True).then_inc(s["max"].sem, 1)
                    if t == SPLIT and next_:
                        _, gp, n = next_
                        dve.wait_ge(s["maxT"].sem, s["maxT"].at(n + 1))
                        dve.wait_ge(s[f"rows{gp % 2}"].sem, s[f"rows{gp % 2}"].at(next_[0] * 64 + 32 * (gp // 2)))
                        nc.vector.tensor_copy(max_parts[:, gp % 2, 0].bitcast(F32R), mt_ps
                                              ).then_inc(s["max_hi"].sem, 1)
                    if t == SPLIT + 1 and next_:
                        _, gp, n = next_
                        dve.wait_ge(s["max_hi"].sem, s["max_hi"].at(n + 1))
                        nc.vector.tensor_tensor(max_parts[:, gp % 2, 1], mt_ps, max_parts[:, gp % 2, 0],
                                                ALU.subtract).then_inc(s["max_split"].sem, 1)
                    if t >= TILES - 4 and last and t - (TILES - 4) < DIVIDE:
                        divide(last, t - (TILES - 4))
                if last and DIVIDE > 4:
                    divide(last, 4)

            steps(dve, step)

        @block.tensor
        def _(pe):
            def values(cur, kt):
                _, gp, n = cur
                pe.wait_ge(s["exp"].sem, s["exp"].at(TILES * n + 4 * kt + 4))
                if kt == 0:
                    pe.wait_ge(s["raw"].sem, s["raw"].at(n))
                    pe.wait_ge(s["vg"].sem, s["vg"].at((n + 1) * PAIR))
                for j in range(4):
                    mm = nc.tensor.matmul(o_ps[32 * j:32 * j + 32], vg[:, gp, kt, 32 * j:32 * j + 32],
                                          probs[:, kt, j], start=kt == 0, stop=kt == KT - 1)
                mm.then_inc(s["pv"].sem, 1)

            def step(i, p):
                ahead, cur = group(i, p, 2), group(i, p)
                if ahead:
                    gi, gp, n = ahead
                    pe.wait_ge(s[f"load{gp}"].sem, s[f"load{gp}"].at(gi * 32 + 32))
                if cur:
                    gi, gp, n = cur
                    pe.wait_ge(s[f"rows{gp % 2}"].sem, s[f"rows{gp % 2}"].at(gi * 64 + 32 * (gp // 2) + 32))
                for t in range(TILES):
                    if ahead:
                        gi, gp, n = ahead
                        j, qt = t // KT, t % KT
                        pe.wait_ge(s["max"].sem, s["max"].at(TILES * n + t - 3))
                        r = slice(0, MAX_ROW)
                        nc.tensor.matmul(sc_ps[:, t % 4], qs[r, gp, j, qt * P:(qt + 1) * P], ks[r, gp, j],
                                         start=True, stop=True).then_inc(s["scores"].sem, 1)
                    if cur:
                        gi, gp, n = cur
                        kt, j = t // 4, t % 4
                        pe.wait_ge(s["exp"].sem, s["exp"].at(TILES * n + t - 1))
                        nc.tensor.matmul(st_ps[:, t % 2], ks[:, gp, j, kt * P:(kt + 1) * P], qs[:, gp, j],
                                         start=True, stop=True).then_inc(s["st"].sem, 1)
                    if t == SPLIT - 1 and (at := group(i, p, 1)):
                        _, gp, n = at
                        pe.wait_ge(s["max"].sem, s["max"].at(TILES * (n + 1)))
                        pe.wait_ge(s["divide"].sem, s["divide"].at(DIVIDE * (n - 2)))
                        nc.tensor.transpose(mt_ps, neg_max[:, gp % 2], g.identity
                                            ).then_inc(s["maxT"].sem, 1)
                    if t == TILES - 4 and (at := group(i, p, -1)):
                        _, gp, n = at
                        pe.wait_ge(s["raw"].sem, s["raw"].at(n + 1))
                        pe.wait_ge(s["divide"].sem, s["divide"].at(DIVIDE * n))
                        if at_next := group(i, p, 1):
                            pe.wait_ge(s["max_split"].sem, s["max_split"].at(at_next[2] + 1))
                        for qt in range(KT):
                            mm = nc.tensor.transpose(rt_ps[:, qt].rearrange("p j r -> p (j r)"),
                                                     raw[:, gp % 2, qt * P:(qt + 1) * P], g.identity)
                        mm.then_inc(s["rawT"].sem, 1)
                    if t == 2 and (at := group(i, p, -1)):
                        values(at, KT - 1)
                    if cur and t % 4 == 2 and t > 4:
                        values(cur, t // 4 - 1)

            steps(pe, step)

    for name in ("st", "scores", "max", "exp"):
        s[name].end(TILES * NG)
    for name in ("max_split", "max_hi", "maxT", "raw", "rawT"):
        s[name].end(NG)
    s["divide"].end(DIVIDE * NG)
    s["pv"].end(KT * NG)
    s["vg"].end(NG * PAIR)
    for p in range(BODY):
        s[f"load{p}"].end(32 * NG // BODY)
    for q in range(2):
        s[f"rows{q}"].end(32 * NG // 2)


def attention_output(nc, g, layer, weights, biased):
    s = g.s
    att = g.att_tok[:].rearrange("p (n d) -> p n d", d=P)
    with g.sb("attn", [P, B, T], F32) as attn, \
         g.sb("update", [P, B, T], F32) as upd, \
         g.pb("turn_ps", [P, B, T], F32) as turn_ps, \
         g.pb("out_ps", [P, B, T], F32) as ps, \
         nc.Block() as block:

        @block.tensor
        def _(pe):
            for b in range(B):
                for t in range(T // P):
                    mm = nc.tensor.transpose(turn_ps[:, b, t * P:(t + 1) * P], att[:, b * (T // P) + t],
                                             g.identity)
                mm.then_inc(s["rawT"].sem, 1)
            for b in range(B):
                pe.wait_ge(s["evac"].sem, s["evac"].at(b + 1))
                nc.tensor.matmul(ps[:, b], weights, attn[:, b], start=True, stop=True
                                 ).then_inc(s["mm"].sem, 1)

        @block.scalar
        def _(act):
            for b in range(B):
                act.wait_ge(s["rawT"].sem, s["rawT"].at(b + 1))
                nc.scalar.activation(attn[:, b], turn_ps[:, b], ACT.Copy).then_inc(s["evac"].sem, 1)
            for b in range(B):
                act.wait_ge(s["mm"].sem, s["mm"].at(b + 1))
                bias = g.gate_bias[:, layer, b:b + 1] if biased else 0.0
                nc.scalar.activation(upd[:, b], ps[:, b], ACT.Identity, bias=bias,
                                     scale=g.mod[:, layer, GATE_A, b:b + 1]).then_inc(s["act"].sem, 1)

        @block.vector
        def _(dve):
            for b in range(B):
                dve.wait_ge(s["act"].sem, s["act"].at(b + 1))
                nc.vector.tensor_tensor(g.xT[:, cols(b)], g.xT[:, cols(b)], upd[:, b], ALU.add
                                        ).then_inc(s["vec"].sem, 1)

    for name in ("rawT", "evac", "mm", "act", "vec"):
        s[name].end(B)


def router_phase(nc, g, wg_name, bias_name, kind):
    s = g.s
    NT, E = N // P, EXPERTS
    with g.sb("gate_w", [P, E], F32) as gw, \
         g.sb("gate_bias", [P, E], F32) as gb, \
         g.sb("router", [P, 16, NT, E], F32) as r, \
         g.sb("router_col", [P, 16, NT], F32) as rc, \
         g.sb("comb_rows", [E, N], F32) as rows, \
         g.sb("scan_a", [P, 2, NT, E], F32) as scan_a, \
         g.sb("scan_b", [P, 2, NT, E], F32) as scan_b, \
         g.pb("logits", [P, NT, E], F32) as logits, \
         g.pb("counts", [P, 2, NT, E], F32) as counts, \
         g.pb("totals", [P, 2, NT, E], F32) as totals, \
         g.pb("rows_ps", [P, B, T], F32) as rows_ps, \
         nc.Block() as block:
        P_, SEL, EQ, OH1, OH2, V, KEEP, M, INC, ALT, COMB, T1 = range(12)
        M1, M2, I1, SUM, R1, W1, W2, T2 = range(8)
        nk = 2 if kind == "each" else 1
        big = 1e30 if kind == "open" else 4.0

        def spread(col):
            return col.unsqueeze(2).broadcast_to([P, NT, E])

        def iota():
            return g.iota.unsqueeze(1).broadcast_to([P, NT, E])

        def over_experts(t):
            return t.unsqueeze(1).broadcast_to([P, NT, E])

        @block.sync
        def _(sp):
            sp.dma_start(gw[:], g.dram[wg_name]).then_inc(s["dma"].sem, 16)
            n = 1
            if bias_name:
                sp.dma_start(gb[:], g.dram[bias_name].partition_broadcast(P)).then_inc(s["dma"].sem, 16)
                n += 1
            g.n_dma = n
            sp.wait_ge(s["evac"].sem, s["evac"].at(1))
            sp.dma_start(g.scratch["comb"][0:E, :], rows[:]).then_inc(s["store"].sem, 16)
            sp.dma_start(g.scratch["comb"][E].rearrange("(a b) -> a b", b=P), g.all_ones[0:NT, :]
                         ).then_inc(s["store"].sem, 16)
            sp.wait_ge(s["store"].sem, s["store"].at(32))

        @block.tensor
        def _(pe):
            pe.wait_ge(s["dma"].sem, s["dma"].at(16 * (2 if bias_name else 1)))
            for t in range(NT):
                mm = nc.tensor.matmul(logits[:, t], g.hT[:, t * P:(t + 1) * P], gw[:], start=True, stop=True)
            mm.then_inc(s["mm"].sem, 1)
            if kind != "open":
                pe.wait_ge(s["chosen"].sem, s["chosen"].at(1))
                chosen = r[:, M:M + nk].rearrange("p k t e -> p (k t e)")
                w = nk * NT * E
                nc.tensor.matmul(counts[:].rearrange("p k t e -> p (k t e)")[:, 0:w], g.tri, chosen,
                                 start=True, stop=True).then_inc(s["mm"].sem, 1)
                nc.tensor.matmul(totals[:].rearrange("p k t e -> p (k t e)")[:, 0:w], g.all_ones, chosen,
                                 start=True, stop=True).then_inc(s["mm"].sem, 1)
            pe.wait_ge(s["chosen"].sem, s["chosen"].at(2))
            for t in range(NT):
                mm = nc.tensor.transpose(rows_ps[0:E, t // 4, (t % 4) * P:(t % 4 + 1) * P], r[:, COMB, t],
                                         g.identity)
            mm.then_inc(s["maxT"].sem, 1)

        @block.scalar
        def _(act):
            act.wait_ge(s["centre"].sem, s["centre"].at(1))
            nc.scalar.activation(r[:, T1], r[:, P_], ACT.Exp).then_inc(s["act"].sem, 1)
            act.wait_ge(s["maxT"].sem, s["maxT"].at(1))
            nc.scalar.activation(rows[:], rows_ps[0:E].rearrange("e b t -> e (b t)"), ACT.Copy
                                 ).then_inc(s["evac"].sem, 1)

        @block.vector
        def _(dve):
            n = 0
            v = nc.vector

            def after(ins, *signals):
                nonlocal n
                n += 1
                ins.then_inc(s["vec"].sem, 1)
                dve.wait_ge(s["vec"].sem, s["vec"].at(n))

            dve.wait_ge(s["mm"].sem, s["mm"].at(1))
            source = logits[:]
            if bias_name and kind != "open":
                after(v.tensor_tensor(r[:, P_], logits[:], over_experts(gb[:]), ALU.add))
                source = r[:, P_]
            after(v.tensor_reduce(rc[:, M1], source, X, ALU.max))
            v.tensor_tensor(r[:, P_], source, spread(rc[:, M1]), ALU.subtract).then_inc(s["centre"].sem, 1)
            dve.wait_ge(s["act"].sem, s["act"].at(1))
            after(v.tensor_reduce(rc[:, SUM], r[:, T1], X, ALU.add))
            after(v.reciprocal(rc[:, R1], rc[:, SUM]))
            after(v.tensor_tensor(r[:, P_], r[:, T1], spread(rc[:, R1]), ALU.mult))
            sel = P_
            if kind == "open":
                sel = SEL
                after(v.tensor_tensor(r[:, SEL], r[:, P_], over_experts(gb[:]), ALU.add))
            for m, oh in ((M1, OH1), (M2, OH2)):
                after(v.tensor_reduce(rc[:, m], r[:, sel], X, ALU.max))
                after(v.tensor_tensor(r[:, EQ], r[:, sel], spread(rc[:, m]), ALU.is_equal))
                after(v.tensor_tensor(r[:, V], r[:, EQ], iota(), ALU.mult))
                after(v.tensor_reduce(rc[:, I1], r[:, V], X, ALU.min))
                after(v.tensor_tensor(r[:, oh], iota(), spread(rc[:, I1]), ALU.is_equal))
                if m == M1:
                    after(v.tensor_scalar(r[:, T1], r[:, oh], -big, None, ALU.mult))
                    after(v.tensor_tensor(r[:, SEL], r[:, T1], r[:, sel], ALU.add))
                    sel = SEL
            if kind == "open":
                after(v.tensor_tensor(r[:, EQ], r[:, OH1], r[:, OH2], ALU.add))
                v.tensor_tensor(r[:, COMB], r[:, EQ], r[:, P_], ALU.mult).then_inc(s["chosen"].sem, 2)
            else:
                if kind == "norm":
                    v.tensor_tensor(r[:, M], r[:, OH1], r[:, OH2], ALU.add).then_inc(s["chosen"].sem, 1)
                else:
                    after(v.tensor_copy(r[:, M], r[:, OH1]))
                    v.tensor_copy(r[:, M + 1], r[:, OH2]).then_inc(s["chosen"].sem, 1)
                after(v.tensor_tensor(rc[:, SUM], rc[:, M1], rc[:, M2], ALU.add))
                if kind == "each":
                    after(v.tensor_scalar(rc[:, SUM], rc[:, SUM], 1e-9, None, ALU.add))
                after(v.reciprocal(rc[:, R1], rc[:, SUM]))
                after(v.tensor_tensor(rc[:, W1], rc[:, M1], rc[:, R1], ALU.mult))
                after(v.tensor_tensor(rc[:, W2], rc[:, M2], rc[:, R1], ALU.mult))
                after(v.tensor_tensor(r[:, OH1], r[:, OH1], spread(rc[:, W1]), ALU.mult))
                after(v.tensor_tensor(r[:, OH2], r[:, OH2], spread(rc[:, W2]), ALU.mult))
                dve.wait_ge(s["mm"].sem, s["mm"].at(3))
                a, b_ = scan_a, scan_b
                after(v.tensor_copy(a[:, 0:nk], totals[:, 0:nk]))
                for k in range(4):
                    d = 1 << k
                    after(v.tensor_tensor(b_[:, 0:nk, d:], a[:, 0:nk, d:], a[:, 0:nk, :NT - d], ALU.add))
                    after(v.tensor_copy(b_[:, 0:nk, :d], a[:, 0:nk, :d]))
                    a, b_ = b_, a
                after(v.tensor_tensor(b_[:, 0:nk], a[:, 0:nk], totals[:, 0:nk], ALU.subtract))
                after(v.tensor_tensor(a[:, 0:nk], b_[:, 0:nk], counts[:, 0:nk], ALU.add))
                after(v.tensor_scalar(b_[:, 0:nk], a[:, 0:nk], float(CAPACITY), None, ALU.is_le))
                if kind == "norm":
                    after(v.tensor_tensor(r[:, T1], r[:, OH1], r[:, OH2], ALU.add))
                    v.tensor_tensor(r[:, COMB], r[:, T1], b_[:, 0], ALU.mult).then_inc(s["chosen"].sem, 1)
                else:
                    after(v.tensor_tensor(r[:, OH1], r[:, OH1], b_[:, 0], ALU.mult))
                    after(v.tensor_tensor(r[:, OH2], r[:, OH2], b_[:, 1], ALU.mult))
                    v.tensor_tensor(r[:, COMB], r[:, OH1], r[:, OH2], ALU.add).then_inc(s["chosen"].sem, 1)
            g.n_vec = n

    s["dma"].end(16 * g.n_dma)
    s["vec"].end(g.n_vec)
    s["mm"].end(1 if kind == "open" else 3)
    s["chosen"].end(2)
    for name, k in (("maxT", 1), ("centre", 1), ("act", 1), ("evac", 1), ("store", 32)):
        s[name].end(k)


def experts_phase(nc, g, layer, up_names, down_name, n_experts, ff, gated, b1_name=None, b2_name=None):
    s = g.s
    FT = ff // P
    NU = len(up_names)
    UPS = B * FT * NU
    HID = B * FT
    turns, odd = divmod(n_experts, 2)
    with g.sb("w_up", [P, 2, NU, ff], F32) as wu, \
         g.sb("w_down", [P, 2, FT, P], F32) as wd, \
         g.sb("b_up", [P, 2, FT], F32) as bu, \
         g.sb("weights_of", [P, 2, N], F32) as cb, \
         g.sb("hidden", [P, 2, FT, T], F32) as hid, \
         g.sb("silu", [P, 2, T], F32) as silu, \
         g.sb("weighted", [P, 2, T], F32) as wtd, \
         g.sb("acc", [P, B, T], F32) as acc, \
         g.sb("b_down", [EXPERTS, P], F32) as bd, \
         g.sb("comb_rows", [EXPERTS, N], F32) as rows, \
         g.pb("up_ps", [P, 4, T], F32) as up_ps, \
         g.pb("down_ps", [P, 2, T], F32) as dn_ps, \
         nc.Block() as block:
        per_load = 16 * (NU + 2 + (1 if b1_name else 0))

        def experts(eng, step):
            with eng.Fori(0, turns) as i:
                for q in range(2):
                    step(i * 2 + q, q, i)
            if odd:
                step(n_experts - 1, 0, turns)

        @block.sync
        def _(sp):
            if b2_name:
                sp.dma_start(bd[:], g.dram[b2_name]).then_inc(s["dma"].sem, 16)
                sp.dma_start(rows[:], g.scratch["comb"][0:EXPERTS, :]).then_inc(s["dma"].sem, 16)

            def step(e, q, i):
                sp.wait_ge(s["added"].sem, s["added"].at(B * (e - 1)))
                one = bass.ds(e, 1)
                for k, name in enumerate(up_names):
                    sp.dma_start(wu[:, q, k], g.dram[name][one].rearrange("o d f -> (o d) f")
                                 ).then_inc(s[f"load{q}"].sem, 16)
                sp.dma_start(wd[:, q], g.dram[down_name][one].rearrange("o (t p) d -> p (o t) d", p=P)
                             ).then_inc(s[f"load{q}"].sem, 16)
                sp.dma_start(cb[:, q], g.scratch["comb"][one].rearrange("o n -> (o n)").partition_broadcast(P)
                             ).then_inc(s[f"load{q}"].sem, 16)
                if b1_name:
                    sp.dma_start(bu[:, q], g.dram[b1_name][one].rearrange("o p t -> (o p) t")
                                 ).then_inc(s[f"load{q}"].sem, 16)

            experts(sp, step)

        @block.tensor
        def _(pe):
            def step(e, q, i):
                pe.wait_ge(s[f"load{q}"].sem, s[f"load{q}"].at(per_load * (i + 1)))

                def up(c):
                    for t in range(FT):
                        for k in range(NU):
                            n = (c * FT + t) * NU + k
                            if gated:
                                pe.wait_ge(s["hidden"].sem, s["hidden"].at(HID * e + (n - 2 - k) // 2))
                            else:
                                pe.wait_ge(s["hidden"].sem, s["hidden"].at(HID * e + n - 3))
                            nc.tensor.matmul(up_ps[:, n % 4], wu[:, q, k, t * P:(t + 1) * P], g.hT[:, cols(c)],
                                             start=True, stop=True).then_inc(s["up"].sem, 1)

                def down(c):
                    pe.wait_ge(s["hidden"].sem, s["hidden"].at(HID * e + (c + 1) * FT))
                    pe.wait_ge(s["weighted"].sem, s["weighted"].at(B * e + c - 1))
                    for t in range(FT):
                        mm = nc.tensor.matmul(dn_ps[:, c % 2], wd[:, q, t], hid[:, c % 2, t],
                                              start=t == 0, stop=t == FT - 1)
                    mm.then_inc(s["down"].sem, 1)

                up(0)
                for c in range(B):
                    if c + 1 < B:
                        up(c + 1)
                    down(c)

            if b2_name:
                pe.wait_ge(s["dma"].sem, s["dma"].at(32))
                for c in range(B):
                    nc.tensor.matmul(up_ps[:, c], bd[:], rows[:, cols(c)], start=True, stop=True
                                     ).then_inc(s["mm"].sem, 1)
                pe.wait_ge(s["first"].sem, s["first"].at(B))
            experts(pe, step)

        @block.scalar
        def _(act):
            def step(e, q, i):
                if b1_name:
                    act.wait_ge(s[f"load{q}"].sem, s[f"load{q}"].at(per_load * (i + 1)))
                for c in range(B):
                    act.wait_ge(s["down"].sem, s["down"].at(B * e + c - 1))
                    for t in range(FT):
                        h = c * FT + t
                        n = h * NU
                        if gated:
                            act.wait_ge(s["up"].sem, s["up"].at(UPS * e + n + 1))
                            act.wait_ge(s["hidden"].sem, s["hidden"].at(HID * e + h - 1))
                            nc.scalar.activation(silu[:, h % 2], up_ps[:, n % 4], ACT.Silu
                                                 ).then_inc(s["silu"].sem, 1)
                        else:
                            act.wait_ge(s["up"].sem, s["up"].at(UPS * e + n + 1))
                            nc.scalar.activation(hid[:, c % 2, t], up_ps[:, n % 4], ACT.Relu,
                                                 bias=bu[:, q, t:t + 1]).then_inc(s["hidden"].sem, 1)

            experts(act, step)

        @block.vector
        def _(dve):
            for c in range(B):
                if b2_name:
                    dve.wait_ge(s["mm"].sem, s["mm"].at(c + 1))
                    nc.vector.tensor_copy(acc[:, c], up_ps[:, c]).then_inc(s["first"].sem, 1)
                else:
                    nc.vector.memset(acc[:, c], 0.0).then_inc(s["first"].sem, 1)

            def step(e, q, i):
                dve.wait_ge(s[f"load{q}"].sem, s[f"load{q}"].at(per_load * (i + 1)))

                def hidden(c):
                    for t in range(FT):
                        h = c * FT + t
                        n = h * NU + 1
                        dve.wait_ge(s["up"].sem, s["up"].at(UPS * e + n + 1))
                        dve.wait_ge(s["silu"].sem, s["silu"].at(HID * e + h + 1))
                        if t == 0:
                            dve.wait_ge(s["down"].sem, s["down"].at(B * e + c - 1))
                        nc.vector.tensor_tensor(hid[:, c % 2, t], silu[:, h % 2], up_ps[:, n % 4], ALU.mult
                                                ).then_inc(s["hidden"].sem, 1)

                def weight(c):
                    dve.wait_ge(s["down"].sem, s["down"].at(B * e + c + 1))
                    dve.wait_ge(s["added"].sem, s["added"].at(B * e + c - 1))
                    nc.vector.tensor_tensor(wtd[:, c % 2], cb[:, q, cols(c)], dn_ps[:, c % 2], ALU.mult
                                            ).then_inc(s["weighted"].sem, 1)

                if gated:
                    hidden(0)
                for c in range(B):
                    if gated and c + 1 < B:
                        hidden(c + 1)
                    weight(c)

            experts(dve, step)
            dve.wait_ge(s["added"].sem, s["added"].at(B * n_experts))
            for c in range(B):
                nc.vector.scalar_tensor_tensor(g.xT[:, cols(c)], acc[:, c], g.mod[:, layer, GATE_B, c:c + 1],
                                               g.xT[:, cols(c)], ALU.mult, ALU.add).then_inc(s["vec"].sem, 1)

        @block.gpsimd
        def _(pool):
            pool.wait_ge(s["first"].sem, s["first"].at(B))

            def step(e, q, i):
                for c in range(B):
                    pool.wait_ge(s["weighted"].sem, s["weighted"].at(B * e + c + 1))
                    pool.wait_ge(s["added"].sem, s["added"].at(B * e + c - 3))
                    nc.gpsimd.tensor_tensor(acc[:, c], acc[:, c], wtd[:, c % 2], ALU.add
                                            ).then_inc(s["added"].sem, 1)

            experts(pool, step)

    if b2_name:
        s["dma"].end(32)
        s["mm"].end(B)
    s["first"].end(B)
    s["vec"].end(B)
    s["up"].end(UPS * n_experts)
    s["hidden"].end(HID * n_experts)
    if gated:
        s["silu"].end(HID * n_experts)
    for name in ("down", "weighted", "added"):
        s[name].end(B * n_experts)
    s["load0"].end(per_load * (turns + odd))
    s["load1"].end(per_load * turns)


def linear_chain_phase(nc, g):
    s = g.s
    with g.sb("chain", [P, 3, B, T], F32) as mid, \
         g.pb("chain_ps", [P, 2, B, T], F32) as ps, \
         nc.Block() as block:

        @block.tensor
        def _(pe):
            for k, w in enumerate(("L2_f0", "L2_f1", "L2_f2")):
                for c in range(B):
                    if k:
                        pe.wait_ge(s["evac"].sem, s["evac"].at(B * (k - 1) + c + 1))
                    nc.tensor.matmul(ps[:, k % 2, c], g.square(w), g.hT[:, cols(c)] if k == 0 else mid[:, k - 1, c],
                                     start=True, stop=True).then_inc(s["mm"].sem, 1)

        @block.scalar
        def _(act):
            for k in range(3):
                for c in range(B):
                    act.wait_ge(s["mm"].sem, s["mm"].at(B * k + c + 1))
                    if k < 2:
                        nc.scalar.activation(mid[:, k, c], ps[:, k % 2, c], ACT.Copy).then_inc(s["evac"].sem, 1)
                    else:
                        nc.scalar.activation(mid[:, k, c], ps[:, k % 2, c], ACT.Tanh, bias=g.col("L2_bias")
                                             ).then_inc(s["act"].sem, 1)

        @block.vector
        def _(dve):
            for c in range(B):
                dve.wait_ge(s["act"].sem, s["act"].at(c + 1))
                nc.vector.scalar_tensor_tensor(g.xT[:, cols(c)], mid[:, 2, c], g.mod[:, 2, GATE_B, c:c + 1],
                                               g.xT[:, cols(c)], ALU.mult, ALU.add).then_inc(s["vec"].sem, 1)

    s["mm"].end(3 * B)
    s["evac"].end(2 * B)
    s["act"].end(B)
    s["vec"].end(B)


def head_rms_phase(nc, g):
    s = g.s
    heads, d = 16, 8
    src = by_part(g.att_tok, 2)
    with g.sb("sq", [P, N], F32) as sq, \
         g.sb("ms", [P, N // d], F32) as ms, \
         g.sb("ordered", [P, N], F32) as ordered, \
         nc.Block() as block:

        @block.scalar
        def _(act):
            nc.scalar.activation(sq[:], g.att_tok[:], ACT.Square).then_inc(s["act"].sem, 1)
            act.wait_ge(s["vec"].sem, s["vec"].at(1))
            nc.scalar.activation(ms[:], ms[:], ACT.Sqrt, bias=g.eps[:, 0:1], scale=1.0 / d).then_inc(s["act"].sem, 1)

        @block.vector
        def _(dve):
            dve.wait_ge(s["act"].sem, s["act"].at(1))
            nc.vector.tensor_reduce(ms[:], sq[:].rearrange("p (h d) -> p h d", d=d), X, ALU.add
                                    ).then_inc(s["vec"].sem, 1)
            nc.vector.tensor_scalar(g.wo2[:], g.square("L2_Wo"), g.rms_w[:], None, ALU.mult
                                    ).then_inc(s["vec"].sem, 1)
            dve.wait_ge(s["act"].sem, s["act"].at(2))
            nc.vector.reciprocal(ms[:], ms[:]).then_inc(s["vec"].sem, 1)
            dve.wait_ge(s["vec"].sem, s["vec"].at(3))
            nc.vector.tensor_tensor(ordered[:].rearrange("p (h d) -> p h d", d=d),
                                    g.att_tok[:].rearrange("p (h d) -> p h d", d=d),
                                    ms[:].unsqueeze(2).broadcast_to([P, N // d, d]), ALU.mult
                                    ).then_inc(s["vec"].sem, 1)
            dve.wait_ge(s["vec"].sem, s["vec"].at(4))
            w = P // 2
            back = g.att_tok[:].rearrange("p (b t i w) -> p b i t w", b=B, i=2, w=w)
            o = ordered[:].rearrange("p (b i t w) -> p b i t w", b=B, i=2, w=w)
            for b in range(B):
                nc.vector.tensor_copy(back[:, b], o[:, b]).then_inc(s["vec"].sem, 1)

    s["act"].end(2)
    s["vec"].end(4 + B)


def alibi_attention(nc, g):
    s = g.s
    HEADS, HD = 16, 64
    NU = HEADS * B
    BODY = 8
    KT = T // P
    ALIBI_ROW = 64
    OUT = HD + 1
    with g.sb("w_head", [P, 2, 5, HD], F32) as wh, \
         g.sb("qa", [P, 4, T], F32R) as qa, \
         g.sb("qb", [P, 4, T], F32R) as qb, \
         g.sb("ka", [P, 4, T], F32R) as ka, \
         g.sb("kb", [P, 4, T], F32R) as kb, \
         g.sb("v_one", [P, 4, KT, OUT], F32) as vo, \
         g.sb("probs", [P, 2, KT, T], F32) as probs, \
         g.sb("neg_max", [P, 2, KT], F32) as neg_max, \
         g.sb("max_parts", [KT, 2, 2, P], F32) as max_parts, \
         g.sb("recip", [P, KT], F32) as recip, \
         g.sb("mask", [P, 3, P], BF16) as mask, \
         g.pb("proj", [P, 2, T], F32) as pj, \
         g.pb("scores", [P, 2, T], F32) as sc_ps, \
         g.pb("scoresT", [P, 2, T], F32) as st_ps, \
         g.pb("values", [P, T], F32) as o_ps, \
         g.pb("maxT", [P, T], F32) as mt_ps, \
         nc.Block() as block:
        f32 = lambda ap: ap.bitcast(F32)
        identity, above, below = mask[:, 0], mask[:, 1], mask[:, 2]

        def unit(i, p, d=0):
            i, p = i + (p + d) // BODY, (p + d) % BODY
            if isinstance(i, int) and not 0 <= BODY * i + p < NU:
                return None
            return i, p, i * BODY + p

        def steps(eng, step):
            for i in (-1, 0):
                for p in range(BODY):
                    step(i, p)
            with eng.Fori(1, NU // BODY - 1) as i:
                for p in range(BODY):
                    step(i, p)
            for i in (NU // BODY - 1, NU // BODY):
                for p in range(BODY):
                    step(i, p)

        @block.sync
        def _(sp):
            sp.dma_start(mask[:], g.dram["mask"]).then_inc(s["dma"].sem, 16)

            def step(i, p):
                if (at := unit(i, p, 4)) and at[1] % 4 == 0:
                    gi, gp, n = at
                    q = gp // 4
                    sp.wait_ge(s["mm"].sem, s["mm"].at(3 * (n - 4)))
                    sp.dma_start(wh[:, q], g.dram["L1_wqkv"][bass.ds(gi * 2 + q, 1)]
                                 .rearrange("o p c d -> (o p) c d")).then_inc(s[f"load{q}"].sem, 16)
                if at := unit(i, p, 3):
                    gi, gp, n = at
                    sp.wait_ge(s["zeros"].sem, s["zeros"].at(5))
                    sp.wait_ge(s["st"].sem, s["st"].at(KT * (n - 3)))
                    sp.dma_start(f32(kb[ALIBI_ROW:ALIBI_ROW + 2, gp % 4]),
                                 g.scratch["alibi"][bass.ds(gi * 2 + gp // 4, 1)].rearrange("o r t -> (o r) t")
                                 ).then_inc(s[f"alibi{gp % 4}"].sem, 16)
                if at := unit(i, p, 1):
                    gi, gp, n = at
                    sp.wait_ge(s["max_split"].sem, s["max_split"].at(n + 1))
                    for r in range(2):
                        row = slice(MAX_ROW + r, MAX_ROW + r + 1)
                        sp.dma_start(f32(qb[row, gp % 4]).rearrange("o (t q) -> o t q", t=KT),
                                     max_parts[:, gp % 2, r]).then_inc(s[f"rows{gp % 2}"].sem, 16)

            steps(sp, step)

        @block.gpsimd
        def _(pool):
            nc.gpsimd.memset(vo[:], 1.0).then_inc(s["ones"].sem, 1)

            def step(i, p):
                if at := unit(i, p, 3):
                    _, gp, n = at
                    pool.wait_ge(s["hi"].sem, s["hi"].at(2 * n + 2))
                    pool.wait_ge(s["st"].sem, s["st"].at(KT * (n - 3)))
                    pool.wait_ge(s["zeros"].sem, s["zeros"].at(5))
                    nc.gpsimd.tensor_tensor(kb[0:HD, gp % 4], f32(ka[0:HD, gp % 4]),
                                            g.all_ones[0:HD, 0:1].broadcast_to([HD, T]), ALU.mult).then_inc(s["kb"].sem, 1)

            steps(pool, step)

        @block.scalar
        def _(act):
            def step(i, p):
                cur, new = unit(i, p), unit(i, p, 3)
                for kt in range(KT):
                    if cur:
                        _, gp, n = cur
                        if kt == 0:
                            act.wait_ge(s["pv"].sem, s["pv"].at(n - 1))
                        act.wait_ge(s["st"].sem, s["st"].at(KT * n + kt + 1))
                        nc.scalar.activation(probs[:, gp % 2, kt, kt * P:T], st_ps[:, kt % 2, kt * P:T],
                                             ACT.Exp, scale=HD ** -0.5).then_inc(s["exp"].sem, 1)
                    if new:
                        _, gp, n = new
                        b = gp % 4
                        if kt == 0:
                            act.wait_ge(s["st"].sem, s["st"].at(KT * (n - 3)))
                            act.wait_ge(s["mm"].sem, s["mm"].at(3 * n + 1))
                            nc.scalar.activation(qa[:, b], pj[:, (3 * gp) % 2], ACT.Copy).then_inc(s["hi"].sem, 1)
                        elif kt == 1:
                            act.wait_ge(s["mm"].sem, s["mm"].at(3 * n + 2))
                            nc.scalar.activation(ka[:, b], pj[:, (3 * gp + 1) % 2], ACT.Copy
                                                 ).then_inc(s["hi"].sem, 1)
                        elif kt == 3:
                            act.wait_ge(s["mm"].sem, s["mm"].at(3 * n + 3))
                            act.wait_ge(s["ones"].sem, s["ones"].at(1))
                            act.wait_ge(s["pv"].sem, s["pv"].at(n - 3))
                            nc.scalar.activation(vo[:, b, :, 0:HD], pj[:, (3 * gp + 2) % 2, 0:KT * HD]
                                                 .rearrange("p (t d) -> p t d", d=HD), ACT.Copy
                                                 ).then_inc(s["vg"].sem, 1)

            steps(act, step)

        @block.vector
        def _(dve):
            nc.vector.memset(f32(qb[HD:P]), 0.0).then_inc(s["zeros"].sem, 1)
            nc.vector.memset(f32(kb[HD:P]), 0.0).then_inc(s["zeros"].sem, 1)
            dve.wait_ge(s["zeros"].sem, s["zeros"].at(2))
            nc.vector.memset(f32(qb[ALIBI_ROW:ALIBI_ROW + 2]), 1.0).then_inc(s["zeros"].sem, 1)
            nc.vector.memset(f32(kb[MAX_ROW:MAX_ROW + 2]), 1.0).then_inc(s["zeros"].sem, 1)
            nc.vector.memset(f32(neg_max[:]), 0.0).then_inc(s["zeros"].sem, 1)

            def step(i, p):
                ahead, next_, new, last = unit(i, p, 2), unit(i, p, 1), unit(i, p, 3), unit(i, p, -2)
                if last:
                    gi, gp, n = last
                    o = o_ps[:, 0:KT * OUT].rearrange("p (t d) -> p t d", d=OUT)
                    dve.wait_ge(s["pv"].sem, s["pv"].at(n + 1))
                    nc.vector.reciprocal(recip[:], o[:, :, HD]).then_inc(s["recip"].sem, 1)
                    dve.wait_ge(s["recip"].sem, s["recip"].at(n + 1))
                    out = g.att1[:, (gp % 4) * KT:(gp % 4) * KT + KT, bass.ds((gi * 2 + gp // 4) * HD, HD)]
                    nc.vector.tensor_tensor(out, o[:, :, 0:HD], recip[:].unsqueeze(2).broadcast_to([P, KT, HD]),
                                            ALU.mult).then_inc(s["divide"].sem, 1)
                for qt in range(KT):
                    if ahead:
                        _, gp, n = ahead
                        if qt == 0:
                            dve.wait_ge(s["maxT"].sem, s["maxT"].at(n - 1))
                        dve.wait_ge(s["scores"].sem, s["scores"].at(KT * n + qt + 1))
                        nc.vector.tensor_reduce(neg_max[:, gp % 2, qt:qt + 1], sc_ps[:, qt % 2, 0:(qt + 1) * P],
                                                X, ALU.max, negate=True).then_inc(s["max"].sem, 1)
                    if qt == 0 and next_:
                        gi, gp, n = next_
                        dve.wait_ge(s["maxT"].sem, s["maxT"].at(n + 1))
                        dve.wait_ge(s[f"rows{gp % 2}"].sem, s[f"rows{gp % 2}"].at(gi * 128 + 32 * (gp // 2)))
                        nc.vector.tensor_copy(max_parts[:, gp % 2, 0].bitcast(F32R), mt_ps[0:KT, 0:P]
                                              ).then_inc(s["max_hi"].sem, 1)
                        dve.wait_ge(s["max_hi"].sem, s["max_hi"].at(n + 1))
                        nc.vector.tensor_tensor(max_parts[:, gp % 2, 1], mt_ps[0:KT, 0:P],
                                                max_parts[:, gp % 2, 0], ALU.subtract
                                                ).then_inc(s["max_split"].sem, 1)
                    if new and qt in (0, 1):
                        _, gp, n = new
                        b = gp % 4
                        dve.wait_ge(s["hi"].sem, s["hi"].at(2 * n + qt + 1))
                        if qt == 0:
                            nc.vector.tensor_tensor(qb[0:HD, b], pj[0:HD, (3 * gp) % 2], f32(qa[0:HD, b]),
                                                    ALU.subtract).then_inc(s["lo"].sem, 1)
                        else:
                            nc.vector.tensor_tensor(ka[HD:P, b], pj[HD:P, (3 * gp + 1) % 2], f32(ka[HD:P, b]),
                                                    ALU.subtract).then_inc(s["lo"].sem, 1)

            steps(dve, step)

        @block.tensor
        def _(pe):
            def project(at, c):
                gi, gp, n = at
                b, q = gp % 4, gp // 4
                if c == 0:
                    pe.wait_ge(s[f"load{q}"].sem, s[f"load{q}"].at(gi * 16 + 16))
                    pe.wait_ge(s["lo"].sem, s["lo"].at(2 * n))
                if c == 1:
                    pe.wait_ge(s["vg"].sem, s["vg"].at(n))
                if c == 2:
                    pe.wait_ge(s["lo"].sem, s["lo"].at(2 * n + 1))
                if c < 2:
                    nc.tensor.matmul(pj[:, (3 * gp + c) % 2],
                                     wh[:, q, 2 * c:2 * c + 2].rearrange("p c d -> p (c d)"), g.hT[:, cols(b)],
                                     start=True, stop=True).then_inc(s["mm"].sem, 1)
                else:
                    for t in range(KT):
                        at_ = b * T + t * P
                        mm = nc.tensor.matmul(pj[:, (3 * gp + 2) % 2, t * HD:(t + 1) * HD], g.hT[:, at_:at_ + P],
                                              wh[:, q, 4], start=True, stop=True)
                    mm.then_inc(s["mm"].sem, 1)

            def scores(at, qt):
                gi, gp, n = at
                b, w = gp % 4, (qt + 1) * P
                tile, row = slice(qt * P, w), slice(0, MAX_ROW)
                pe.wait_ge(s["max"].sem, s["max"].at(KT * n + qt - 1))
                nc.tensor.matmul(sc_ps[:, qt % 2, 0:w], qa[:, b, tile], ka[:, b, 0:w], start=True, stop=False)
                nc.tensor.matmul(sc_ps[:, qt % 2, 0:w], qb[row, b, tile], kb[row, b, 0:w], start=False, stop=False)
                nc.tensor.matmul(sc_ps[:, qt % 2, tile], identity, above, start=False, stop=True
                                 ).then_inc(s["scores"].sem, 1)

            def scores_t(at, kt):
                gi, gp, n = at
                b, tile, right = gp % 4, slice(kt * P, (kt + 1) * P), slice(kt * P, T)
                pe.wait_ge(s["exp"].sem, s["exp"].at(KT * n + kt - 1))
                nc.tensor.matmul(st_ps[:, kt % 2, right], ka[:, b, tile], qa[:, b, right], start=True, stop=False)
                nc.tensor.matmul(st_ps[:, kt % 2, right], kb[:, b, tile], qb[:, b, right], start=False, stop=False)
                nc.tensor.matmul(st_ps[:, kt % 2, tile], identity, below, start=False, stop=True
                                 ).then_inc(s["st"].sem, 1)

            def values(at, qt):
                gi, gp, n = at
                if qt == 0:
                    pe.wait_ge(s["divide"].sem, s["divide"].at(n))
                    pe.wait_ge(s["exp"].sem, s["exp"].at(KT * (n + 1)))
                for kt in range(qt + 1):
                    mm = nc.tensor.matmul(o_ps[:, qt * OUT:(qt + 1) * OUT],
                                          probs[:, gp % 2, kt, qt * P:(qt + 1) * P], vo[:, gp % 4, kt],
                                          start=kt == 0, stop=kt == qt)
                if qt == KT - 1:
                    mm.then_inc(s["pv"].sem, 1)

            pe.wait_ge(s["dma"].sem, s["dma"].at(16))

            def step(i, p):
                cur, ahead, next_ = unit(i, p), unit(i, p, 2), unit(i, p, 1)
                new, before = unit(i, p, 3), unit(i, p, -1)
                if cur:
                    gi, gp, n = cur
                    pe.wait_ge(s[f"rows{gp % 2}"].sem, s[f"rows{gp % 2}"].at(gi * 128 + 32 * (gp // 2) + 32))
                if ahead:
                    gi, gp, n = ahead
                    pe.wait_ge(s["kb"].sem, s["kb"].at(n + 1))
                    pe.wait_ge(s["lo"].sem, s["lo"].at(2 * n + 2))
                    pe.wait_ge(s[f"alibi{gp % 4}"].sem, s[f"alibi{gp % 4}"].at(gi * 32 + 16 * (gp // 4) + 16))
                for k in range(KT):
                    if cur:
                        scores_t(cur, k)
                    if ahead:
                        scores(ahead, k)
                    if k > 0 and before:
                        if k == 1:
                            values(before, 0)
                        values(before, k)
                    if k == 0 and next_:
                        gi, gp, n = next_
                        pe.wait_ge(s["max"].sem, s["max"].at(KT * (n + 1)))
                        pe.wait_ge(s["max_split"].sem, s["max_split"].at(n))
                        nc.tensor.transpose(mt_ps[0:KT, 0:P], neg_max[:, gp % 2], g.identity
                                            ).then_inc(s["maxT"].sem, 1)
                    if new and k != 2:
                        project(new, min(k, 2))

            steps(pe, step)

    s["dma"].end(16)
    s["mm"].end(3 * NU)
    for q in range(2):
        s[f"load{q}"].end(16 * HEADS // 2)
        s[f"rows{q}"].end(32 * NU // 2)
    for b in range(B):
        s[f"alibi{b}"].end(16 * HEADS)
    s["zeros"].end(5)
    s["ones"].end(1)
    s["hi"].end(2 * NU)
    s["lo"].end(2 * NU)
    for name in ("kb", "vg", "pv", "maxT", "max_hi", "max_split", "recip", "divide"):
        s[name].end(NU)
    for name in ("scores", "st", "max", "exp"):
        s[name].end(KT * NU)


def alibi_output(nc, g):
    s = g.s
    KD = 8
    with g.sb("w_out", [P, KD, P], F32) as wo, \
         g.sb("attn", [P, 4, T], F32) as attn, \
         g.sb("update", [P, B, T], F32) as upd, \
         g.pb("turn_ps", [P, 4, T], F32) as turn_ps, \
         g.pb("out_ps", [P, B, T], F32) as ps, \
         nc.Block() as block:
        tiles = [(b, k) for b in range(B) for k in range(KD)]

        @block.sync
        def _(sp):
            sp.dma_start(wo[:], g.dram["L1_wout"]).then_inc(s["dma"].sem, 16)

        @block.tensor
        def _(pe):
            def turn(n):
                b, k = tiles[n]
                if n >= 4:
                    pe.wait_ge(s["evac"].sem, s["evac"].at(n - 3))
                for t in range(T // P):
                    mm = nc.tensor.transpose(turn_ps[:, n % 4, t * P:(t + 1) * P],
                                             g.att1[:, b * (T // P) + t, k * P:(k + 1) * P], g.identity)
                mm.then_inc(s["rawT"].sem, 1)

            pe.wait_ge(s["dma"].sem, s["dma"].at(16))
            turn(0)
            turn(1)
            for n, (b, k) in enumerate(tiles):
                if n + 2 < len(tiles):
                    turn(n + 2)
                pe.wait_ge(s["evac"].sem, s["evac"].at(n + 1))
                nc.tensor.matmul(ps[:, b], wo[:, k], attn[:, n % 4], start=k == 0, stop=k == KD - 1
                                 ).then_inc(s["mm"].sem, 1)

        @block.scalar
        def _(act):
            for n in range(len(tiles)):
                act.wait_ge(s["rawT"].sem, s["rawT"].at(n + 1))
                act.wait_ge(s["mm"].sem, s["mm"].at(n - 3))
                nc.scalar.activation(attn[:, n % 4], turn_ps[:, n % 4], ACT.Copy).then_inc(s["evac"].sem, 1)
            for b in range(B):
                act.wait_ge(s["mm"].sem, s["mm"].at(KD * (b + 1)))
                nc.scalar.activation(upd[:, b], ps[:, b], ACT.Identity, bias=g.gate_bias[:, 1, b:b + 1],
                                     scale=g.mod[:, 1, GATE_A, b:b + 1]).then_inc(s["act"].sem, 1)

        @block.vector
        def _(dve):
            for b in range(B):
                dve.wait_ge(s["act"].sem, s["act"].at(b + 1))
                nc.vector.tensor_tensor(g.xT[:, cols(b)], g.xT[:, cols(b)], upd[:, b], ALU.add
                                        ).then_inc(s["vec"].sem, 1)

    s["dma"].end(16)
    for name in ("rawT", "evac", "mm"):
        s[name].end(B * KD)
    s["act"].end(B)
    s["vec"].end(B)


def linear_attention(nc, g):
    s = g.s
    HG, KT = 4, T // P
    OUT = 9
    with g.sb("head_proj", [P, 4 * P], F32) as pm, \
         g.sb("q_k", [P, 2, 2, T], F32) as qk, \
         g.sb("v_one", [P, 2, KT, 16, OUT], F32) as vo, \
         g.sb("expd", [P, 4, T], F32) as ex, \
         g.sb("features", [P, 16, T], F32) as feat, \
         g.sb("kv", [P, 2, HG, 4, OUT], F32) as kv, \
         g.sb("kv_mask", [P, 4, OUT], F32) as kv_mask, \
         g.sb("recip", [P, 2, KT, 16], F32) as recip, \
         g.pb("proj", [P, 3, T], F32) as pj, \
         g.pb("feat_ps", [P, 2, T], F32) as f_ps, \
         g.pb("kv_ps", [P, HG, P], F32) as kv_ps, \
         g.pb("out_ps", [P, KT, 2 * P], F32) as o_ps, \
         nc.Block() as block:
        F = 2 * 4

        @block.sync
        def _(sp):
            sp.dma_start(pm[:], g.dram["L3_proj"]).then_inc(s["dma"].sem, 16)
            sp.dma_start(kv_mask[:], g.dram["kv_mask"]).then_inc(s["dma"].sem, 16)

        @block.tensor
        def _(pe):
            pe.wait_ge(s["dma"].sem, s["dma"].at(32))

            def project(b):
                pe.wait_ge(s["evac"].sem, s["evac"].at(3 * b))
                for c, w in enumerate(("L3_Wq", "L3_Wk")):
                    nc.tensor.matmul(pj[:, c], g.square(w), g.hT[:, cols(b)], start=True, stop=True
                                     ).then_inc(s["mm"].sem, 1)
                for t in range(KT):
                    at = b * T + t * P
                    mm = nc.tensor.matmul(pj[:, 2, t * P:(t + 1) * P], g.hT[:, at:at + P], g.square("L3_Wv"),
                                          start=True, stop=True)
                mm.then_inc(s["mm"].sem, 1)

            project(0)
            for b in range(B + 1):
                for f in range(F):
                    if b < B:
                        n = F * b + f
                        if f == 0:
                            pe.wait_ge(s["evac"].sem, s["evac"].at(3 * (b + 1)))
                        pe.wait_ge(s["feat"].sem, s["feat"].at(n - 1))
                        if f < 4:
                            nc.tensor.matmul(f_ps[:, n % 2], pm[:, f * P:(f + 1) * P], qk[:, b % 2, 0],
                                             start=True, stop=True).then_inc(s["up"].sem, 1)
                        else:
                            nc.tensor.matmul(f_ps[:, n % 2], qk[:, b % 2, 1, (f - 4) * P:(f - 3) * P], pm[:],
                                             start=True, stop=True).then_inc(s["up"].sem, 1)
                    if b > 0 and f < HG:
                        hg = f
                        pe.wait_ge(s["feat"].sem, s["feat"].at(F * b))
                        pe.wait_ge(s["kb"].sem, s["kb"].at(b - 1))
                        for t in range(KT):
                            mm = nc.tensor.matmul(
                                kv_ps[:, hg, 0:4 * OUT], feat[:, 8 * ((b - 1) % 2) + 4 + t, hg * P:(hg + 1) * P],
                                vo[:, (b - 1) % 2, t, 4 * hg:4 * hg + 4].rearrange("p j d -> p (j d)"),
                                start=t == 0, stop=t == KT - 1)
                        if hg == HG - 1:
                            mm.then_inc(s["pv"].sem, 1)
                    elif b > 0:
                        t = f - HG
                        pe.wait_ge(s["kb"].sem, s["kb"].at(b))
                        pe.wait_ge(s["divide"].sem, s["divide"].at(b - 1))
                        for hg in range(HG):
                            mm = nc.tensor.matmul(
                                o_ps[:, t, hg * 4 * OUT:(hg + 1) * 4 * OUT],
                                feat[:, 8 * ((b - 1) % 2) + hg, t * P:(t + 1) * P],
                                kv[:, (b - 1) % 2, hg].rearrange("p j d -> p (j d)"), start=True, stop=True)
                        if t == KT - 1:
                            mm.then_inc(s["down"].sem, 1)
                    if b + 1 < B and f == 5:
                        project(b + 1)

        @block.scalar
        def _(act):
            def evacuate(b):
                for c in range(2):
                    act.wait_ge(s["mm"].sem, s["mm"].at(3 * b + c + 1))
                    act.wait_ge(s["up"].sem, s["up"].at(F * (b - 1)))
                    nc.scalar.activation(qk[:, b % 2, c], pj[:, c], ACT.Copy).then_inc(s["evac"].sem, 1)
                act.wait_ge(s["mm"].sem, s["mm"].at(3 * b + 3))
                act.wait_ge(s["ones"].sem, s["ones"].at(1))
                act.wait_ge(s["pv"].sem, s["pv"].at(b - 1))
                nc.scalar.activation(vo[:, b % 2, :, :, 0:8], pj[:, 2].rearrange("p (t h d) -> p t h d", h=16, d=8),
                                     ACT.Copy).then_inc(s["evac"].sem, 1)

            evacuate(0)
            for b in range(B):
                for f in range(F):
                    n = F * b + f
                    act.wait_ge(s["clip"].sem, s["clip"].at(n + 1))
                    nc.scalar.activation(ex[:, n % 4], ex[:, n % 4], ACT.Exp).then_inc(s["exp"].sem, 1)
                    if b + 1 < B and f == 6:
                        evacuate(b + 1)

        @block.gpsimd
        def _(pool):
            nc.gpsimd.memset(vo[:], 1.0).then_inc(s["ones"].sem, 1)

        @block.vector
        def _(dve):
            dve.wait_ge(s["dma"].sem, s["dma"].at(32))
            def mask(b):
                dve.wait_ge(s["pv"].sem, s["pv"].at(b + 1))
                nc.vector.tensor_tensor(kv[:, b % 2], kv_mask[:].unsqueeze(1).broadcast_to([P, HG, 4, OUT]),
                                        kv_ps[:, :, 0:4 * OUT].rearrange("p g (j d) -> p g j d", d=OUT),
                                        ALU.mult).then_inc(s["kb"].sem, 1)

            def divide(b):
                o = o_ps[:, :, 0:16 * OUT].rearrange("p t (h d) -> p t h d", d=OUT)
                dve.wait_ge(s["down"].sem, s["down"].at(b + 1))
                nc.vector.tensor_scalar(recip[:, 0], o[:, :, :, 8], 1e-8, None, ALU.add
                                        ).then_inc(s["recip"].sem, 1)
                dve.wait_ge(s["recip"].sem, s["recip"].at(2 * b + 1))
                nc.vector.reciprocal(recip[:, 1], recip[:, 0]).then_inc(s["recip"].sem, 1)
                dve.wait_ge(s["recip"].sem, s["recip"].at(2 * b + 2))
                for t in range(KT):
                    done = s["divide"] if t == KT - 1 else s["vec"]
                    nc.vector.tensor_tensor(
                        g.att_tok[:].rearrange("p (n h d) -> p n h d", h=16, d=8)[:, b * KT + t],
                        o[:, t, :, 0:8], recip[:, 1, t].unsqueeze(2).broadcast_to([P, 16, 8]), ALU.mult
                    ).then_inc(done.sem, 1)

            for b in range(B + 1):
                for f in range(F + 1):
                    n = F * b + f
                    if f < F and b < B:
                        dve.wait_ge(s["up"].sem, s["up"].at(n + 1))
                        dve.wait_ge(s["feat"].sem, s["feat"].at(n - 3))
                        nc.vector.tensor_scalar(ex[:, n % 4], f_ps[:, n % 2], 0.0, None, ALU.min
                                                ).then_inc(s["clip"].sem, 1)
                    if f and b < B:
                        dve.wait_ge(s["exp"].sem, s["exp"].at(n))
                        dve.wait_ge(s["down"].sem, s["down"].at(b - 1))
                        nc.vector.scalar_tensor_tensor(feat[:, 8 * (b % 2) + f - 1], f_ps[:, (n - 1) % 2], 0.0,
                                                       ex[:, (n - 1) % 4], ALU.max, ALU.add
                                                       ).then_inc(s["feat"].sem, 1)
                    if b > 0 and f == HG:
                        mask(b - 1)
                if b > 0:
                    divide(b - 1)

    s["dma"].end(32)
    s["mm"].end(3 * B)
    s["evac"].end(3 * B)
    for name in ("up", "exp", "clip", "feat"):
        s[name].end(F * B)
    for name in ("kb", "pv", "down", "divide"):
        s[name].end(B)
    s["recip"].end(2 * B)
    s["vec"].end(3 * B)
    s["ones"].end(1)


def residual_output(nc, g):
    s = g.s
    att = g.att_tok[:].rearrange("p (n d) -> p n d", d=P)
    with g.sb("attn", [P, B, T], F32) as attn, \
         g.pb("turn_ps", [P, B, T], F32) as turn_ps, \
         g.pb("out_ps", [P, B, T], F32) as ps, \
         nc.Block() as block:

        @block.tensor
        def _(pe):
            for b in range(B):
                for t in range(T // P):
                    mm = nc.tensor.transpose(turn_ps[:, b, t * P:(t + 1) * P], att[:, b * (T // P) + t],
                                             g.identity)
                mm.then_inc(s["rawT"].sem, 1)
            for b in range(B):
                pe.wait_ge(s["evac"].sem, s["evac"].at(b + 1))
                nc.tensor.matmul(ps[:, b], g.square("L3_Wo"), attn[:, b], start=True, stop=True
                                 ).then_inc(s["mm"].sem, 1)

        @block.scalar
        def _(act):
            for b in range(B):
                act.wait_ge(s["rawT"].sem, s["rawT"].at(b + 1))
                nc.scalar.activation(attn[:, b], turn_ps[:, b], ACT.Copy).then_inc(s["evac"].sem, 1)

        @block.vector
        def _(dve):
            for b in range(B):
                dve.wait_ge(s["mm"].sem, s["mm"].at(b + 1))
                nc.vector.scalar_tensor_tensor(g.hT[:, cols(b)], ps[:, b], g.col("L3_bo"), g.hT[:, cols(b)],
                                               ALU.add, ALU.add).then_inc(s["vec"].sem, 1)

    for name in ("rawT", "evac", "mm", "vec"):
        s[name].end(B)


def gelu_ffn(nc, g):
    s = g.s
    FT = 4
    with g.sb("w1", [P, 4 * P], F32) as w1, \
         g.sb("w2", [P, FT, P], F32) as w2, \
         g.sb("hidden", [P, 2, FT, T], F32) as hid, \
         g.pb("up_ps", [P, 4, T], F32) as up_ps, \
         g.pb("down_ps", [P, 2, T], F32) as dn_ps, \
         nc.Block() as block:

        @block.sync
        def _(sp):
            sp.dma_start(w1[:], g.dram["L3_w1"]).then_inc(s["dma"].sem, 16)
            sp.dma_start(w2[:], g.dram["L3_w2"]).then_inc(s["dma"].sem, 16)

        @block.tensor
        def _(pe):
            pe.wait_ge(s["dma"].sem, s["dma"].at(32))

            def up(c):
                for t in range(FT):
                    pe.wait_ge(s["hidden"].sem, s["hidden"].at(FT * (c - 1) + t + 1))
                    nc.tensor.matmul(up_ps[:, t], w1[:, t * P:(t + 1) * P], g.hT[:, cols(c)],
                                     start=True, stop=True).then_inc(s["up"].sem, 1)

            up(0)
            for c in range(B):
                if c + 1 < B:
                    up(c + 1)
                pe.wait_ge(s["hidden"].sem, s["hidden"].at(FT * (c + 1)))
                pe.wait_ge(s["vec"].sem, s["vec"].at(c - 1))
                for t in range(FT):
                    mm = nc.tensor.matmul(dn_ps[:, c % 2], w2[:, t], hid[:, c % 2, t], start=t == 0,
                                          stop=t == FT - 1)
                mm.then_inc(s["down"].sem, 1)

        @block.scalar
        def _(act):
            for c in range(B):
                act.wait_ge(s["down"].sem, s["down"].at(c - 1))
                for t in range(FT):
                    act.wait_ge(s["up"].sem, s["up"].at(FT * c + t + 1))
                    nc.scalar.activation(hid[:, c % 2, t], up_ps[:, t], ACT.Gelu, bias=g.col(f"L3_b1_{t}")
                                         ).then_inc(s["hidden"].sem, 1)

        @block.vector
        def _(dve):
            for c in range(B):
                dve.wait_ge(s["down"].sem, s["down"].at(c + 1))
                nc.vector.scalar_tensor_tensor(g.hT[:, cols(c)], dn_ps[:, c % 2], g.col("L3_b2"), g.hT[:, cols(c)],
                                               ALU.add, ALU.add).then_inc(s["vec"].sem, 1)

    s["dma"].end(32)
    s["up"].end(B * FT)
    s["hidden"].end(B * FT)
    s["down"].end(B)
    s["vec"].end(B)


def gated_add(nc, g, layer, gate):
    s = g.s
    with nc.Block() as block:
        @block.vector
        def _(dve):
            for c in range(B):
                nc.vector.scalar_tensor_tensor(g.xT[:, cols(c)], g.hT[:, cols(c)], g.mod[:, layer, gate, c:c + 1],
                                               g.xT[:, cols(c)], ALU.mult, ALU.add).then_inc(s["vec"].sem, 1)
    s["vec"].end(B)


class Program:

    def __init__(self, nc):
        self.nc, self.count = nc, 0

    def sb(self, name, shape, dtype):
        self.count += 1
        return self.nc.sbuf_tensor(f"{name}_{self.count}", shape, dtype)

    def pb(self, name, shape, dtype):
        self.count += 1
        return self.nc.psum_tensor(f"{name}_{self.count}", shape, dtype)


def build(nc, dram, debug=None):
    g = Program(nc)
    g.dram = dram
    names = ["dma", "vec", "act", "pe", "pool", "mean", "square", "var", "centre", "std", "norm", "mm",
             "evac", "split", "store", "scores", "st", "max", "exp", "max_split", "max_hi", "maxT", "raw",
             "rawT", "divide", "pv", "vg", "ones", "zeros"]
    names += [f"load{p}" for p in range(4)] + [f"rows{q}" for q in range(2)]
    names += MORE_SIGNALS
    g.s = {n: Signal(nc, n) for n in names}
    g.scratch = {n: nc.dram_tensor(f"scratch_{n}", shape, F32, kind="Internal").ap() for n, shape in
                 (("q", (B * 16 * 24, T)), ("k", (B * 16 * 24, T)), ("comb", (9, N)),
                  ("alibi", (16, 2, T)))}
    g.xT = nc.alloc_sbuf_tensor("x_keep", [P, N], F32)
    g.hT = nc.alloc_sbuf_tensor("h_keep", [P, N], F32)
    g.squares = nc.alloc_sbuf_tensor("squares_keep", [P, len(SQUARES), P], F32)
    g.columns = nc.alloc_sbuf_tensor("columns_keep", [P, len(COLUMNS)], F32)
    g.consts = nc.alloc_sbuf_tensor("consts_keep", [P, 6 * P + 16], F32)
    g.iota = g.consts[:, 6 * P + 8:6 * P + 16]
    g.wo2 = nc.alloc_sbuf_tensor("wo2", [P, P], F32)
    g.v_tok = nc.alloc_sbuf_tensor("v_tok", [P, N], F32)
    g.att_tok = nc.alloc_sbuf_tensor("att_tok", [P, N], F32)
    g.cs = nc.alloc_sbuf_tensor("silu_c", [P, 16], F32)
    g.mod = nc.alloc_sbuf_tensor("mod", [P, 4, 6, B], F32)
    g.gate_bias = nc.alloc_sbuf_tensor("gate_bias", [P, 2, B], F32)
    g.rms_w = nc.alloc_sbuf_tensor("rms_w", [P, 1], F32)
    g.neg_lam = nc.alloc_sbuf_tensor("neg_lam", [P, 1], F32)
    g.eps = nc.alloc_sbuf_tensor("eps", [P, 2], F32)
    const = lambda n: g.consts[:, n * P:(n + 1) * P]
    g.identity, g.mean_w, g.den_sel, g.head_mean, g.tri, g.all_ones = (const(n) for n in range(6))
    g.den_eps = lambda hd: g.consts[:, 6 * P:6 * P + 1] if hd == 8 else g.eps[:, 1:2]
    g.square = lambda name: g.squares[:, SQUARES.index(name)]
    g.col = lambda name: g.columns[:, COLUMNS.index(name):COLUMNS.index(name) + 1]
    g.modcol = lambda layer, j: (lambda c: g.mod[:, layer, j, c:c + 1])

    with nc.Block() as block:
        @block.sync
        def _(sp):
            for signal in g.s.values():
                sp.sem_inc(signal.sem, START)

    def dump(name):
        if debug and name in debug:
            with nc.Block() as block:
                @block.sync
                def _(sp):
                    src = g.hT if name.startswith("h") else g.xT
                    sp.dma_start(debug[name], src[:]).then_inc(g.s["dma"].sem, 16)
                    sp.wait_ge(g.s["dma"].sem, g.s["dma"].at(16))
            g.s["dma"].end(16)

    setup_phase(nc, g)
    norm_phase(nc, g, g.xT, g.modcol(0, SCALE_A), g.modcol(0, SHIFT_A))
    dump("h0")
    q_stack, k_stack, v_group = small_head_stacks(g)
    with q_stack as qs, k_stack as ks, v_group as vg:
        small_head_projections(nc, g, (qs, ks, vg), 8, "L0_Wq", "L0_Wk", "L0_Wv")
        small_head_attention(nc, g, (qs, ks, vg), 8, float(8 ** -0.5))
    attention_output(nc, g, 0, g.square("L0_Wo"), True)
    dump("x0")
    norm_phase(nc, g, g.xT, g.modcol(0, SCALE_B), g.modcol(0, SHIFT_B))
    dump("h1")
    router_phase(nc, g, "L0_gate_w", "L0_gate_b", "norm")
    experts_phase(nc, g, 0, ["L0_w1"], "L0_w2", EXPERTS, 512, False, "L0_b1", "L0_b2")
    dump("x1")

    norm_phase(nc, g, g.xT, g.modcol(1, SCALE_A), g.modcol(1, SHIFT_A))
    dump("h2")
    with g.sb("att1", [P, N // P, 16 * 64], F32) as g.att1:
        alibi_attention(nc, g)
        alibi_output(nc, g)
    dump("x2")
    norm_phase(nc, g, g.xT, g.modcol(1, SCALE_B), g.modcol(1, SHIFT_B))
    router_phase(nc, g, "L1_gate_w", "L1_gate_b", "open")
    experts_phase(nc, g, 1, ["L1_w1", "L1_w3"], "L1_w2", EXPERTS + 1, 256, True)
    dump("x3")

    norm_phase(nc, g, g.xT, g.modcol(2, SCALE_A), g.modcol(2, SHIFT_A))
    dump("h4")
    q_stack, k_stack, v_group = small_head_stacks(g)
    with q_stack as qs, k_stack as ks, v_group as vg:
        small_head_projections(nc, g, (qs, ks, vg), 4, "L2_Wq", "L2_Wk", "L2_Wv", "L2_Wqs", "L2_Wks")
        small_head_attention(nc, g, (qs, ks, vg), 4, 0.5, differential=True)
    head_rms_phase(nc, g)
    attention_output(nc, g, 2, g.wo2[:], False)
    dump("x4")
    norm_phase(nc, g, g.xT, g.modcol(2, SCALE_B), g.modcol(2, SHIFT_B))
    linear_chain_phase(nc, g)
    dump("x5")

    norm_phase(nc, g, g.xT, g.modcol(3, SCALE_A), g.modcol(3, SHIFT_A))
    dump("h6")
    linear_attention(nc, g)
    residual_output(nc, g)
    gamma, beta = (lambda c: g.col("L3_gamma")), (lambda c: g.col("L3_beta"))
    norm_phase(nc, g, g.hT, gamma, beta)
    gelu_ffn(nc, g)
    norm_phase(nc, g, g.hT, gamma, beta)
    gated_add(nc, g, 3, GATE_A)
    dump("x6")
    norm_phase(nc, g, g.xT, g.modcol(3, SCALE_B), g.modcol(3, SHIFT_B))
    dump("h7")
    router_phase(nc, g, "L3_gate_w", None, "each")
    experts_phase(nc, g, 3, ["L3_gate", "L3_up"], "L3_down", EXPERTS, 256, True)

    with nc.Block() as block:
        @block.sync
        def _(sp):
            sp.dma_start(dram["outT"], g.xT[:]).then_inc(g.s["dma"].sem, 16)
            sp.wait_ge(g.s["dma"].sem, g.s["dma"].at(16))


MORE_SIGNALS = ["chosen", "first", "up", "hidden", "silu", "down", "weighted", "added", "hi", "lo", "kb",
                "recip", "feat", "clip", "alibi0", "alibi1", "alibi2", "alibi3"]


def host_arrays(inp):
    a = {k: np.asarray(v) for k, v in inp.items()}
    t = np.transpose
    out = {"xT": np.ascontiguousarray(a["L0_attn_x"].reshape(N, P).T)}
    out["cT"] = np.ascontiguousarray(np.concatenate([a[f"L{i}_c"] for i in range(4)]).T)
    for i in range(4):
        out[f"L{i}_wmod"] = np.ascontiguousarray(a[f"L{i}_wmod"])
    out["lambdas"] = np.stack([a[f"L2_attn_lambda_{n}"] for n in ("q1", "k1", "q2", "k2")])
    swap = np.arange(P) ^ 1
    qkv3 = np.split(a["L3_attn_w_qkv"], 3)
    squares = [a["L0_attn_Wq"].T, a["L0_attn_Wk"].T, a["L0_attn_Wv"].T, a["L0_attn_Wo"].T,
               a["L2_attn_Wq"].T, a["L2_attn_Wq"][swap].T, a["L2_attn_Wk"].T, a["L2_attn_Wk"][swap].T,
               a["L2_attn_Wv"].T, a["L2_attn_Wo"].T,
               a["L2_ffn_weight"], a["L2_ffn_aux_weight1"], a["L2_ffn_aux_weight2"],
               qkv3[0].T, qkv3[1].T, qkv3[2].T, a["L3_attn_w_out"].T]
    out["squares"] = np.ascontiguousarray(np.stack(squares, axis=1))
    out["columns"] = np.ascontiguousarray(np.stack(
        [a["L0_attn_bo"], a["L1_attn_b_out"], np.tile(a["L2_attn_rms_weight"], 16), a["L2_ffn_bias"],
         a["L3_attn_b_out"], a["L3_attn_gamma"], a["L3_attn_beta"], a["L3_attn_b2"],
         *a["L3_attn_b1"].reshape(4, P)], axis=1))
    i = np.arange(P)
    den_sel = (i[:, None] == 32 * (i[None, :] // 32) + 8)
    head_mean = (i[:, None] // 8 == i[None, :] // 8) / 8
    tri = i[:, None] <= i[None, :]
    den_eps = np.zeros((P, 16))
    den_eps[8::32, 0] = 1e-8
    den_eps[:, 8:16] = np.arange(EXPERTS) - EXPERTS
    out["consts"] = np.concatenate([np.eye(P), np.full((P, P), 1 / P), den_sel, head_mean, tri,
                                    np.ones((P, P)), den_eps], axis=1).astype(np.float32)
    angle = (1.0 / 10000.0 ** np.linspace(0.0, 1.0, 2)).astype(np.float32)
    f = np.arange(T, dtype=np.float32)[None, :] * angle[(i % 4) // 2][:, None]
    out["rope"] = np.stack([np.cos(f), np.sin(f) * np.where(i % 2, 1, -1)[:, None]], axis=1).astype(np.float32)
    bf = mybir.dt.np(BF16)
    above = np.where(i[None, :] > i[:, None], -1e30, 0.0)
    out["mask"] = np.stack([np.eye(P), above, above.T], axis=1).astype(bf)
    slope = np.array([(2 ** -0.5) ** (h + 1) for h in range(16)])
    al = (8 * slope[:, None] * np.arange(T)[None, :]).astype(np.float32)
    hi = (al.view(np.uint32) & np.uint32(0xFFFFF000)).view(np.float32)
    out["alibi"] = np.stack([hi, al - hi], axis=1)
    j = np.arange(4)
    out["kv_mask"] = np.broadcast_to((i[:, None] // 32 == j[None, :])[:, :, None], (P, 4, 9)).astype(np.float32)

    c = np.ascontiguousarray
    out["L0_gate_w"], out["L0_gate_b"] = a["L0_ffn_gate_w"], a["L0_ffn_gate_b"]
    out["L0_w1"], out["L0_w2"], out["L0_b2"] = a["L0_ffn_w1"], a["L0_ffn_w2"], a["L0_ffn_b2"]
    out["L0_b1"] = c(a["L0_ffn_b1"].reshape(EXPERTS, 4, P).transpose(0, 2, 1))
    wq = a["L1_attn_w_qkv"].reshape(P, 3, 16, 64)
    out["L1_wqkv"] = c(wq.transpose(2, 0, 1, 3)[:, :, [0, 0, 1, 1, 2]])
    out["L1_wout"] = c(a["L1_attn_w_out"].reshape(8, P, P).transpose(1, 0, 2))
    out["L1_gate_w"], out["L1_gate_b"] = c(a["L1_ffn_gate_w"].T), a["L1_ffn_gate_bias"]
    for n in ("w1", "w2", "w3"):
        both = np.concatenate([a[f"L1_ffn_{n}"], a[f"L1_ffn_s{n}"][None]])
        out[f"L1_{n}"] = c(both.transpose(0, 2, 1))
    pm = np.zeros((P, 16, 32), np.float32)
    for h in range(16):
        pm[8 * h:8 * h + 8, h] = a["L3_attn_proj"][h]
    out["L3_proj"] = pm.reshape(P, 512)
    out["L3_w1"] = c(a["L3_attn_w1"].T)
    out["L3_w2"] = c(a["L3_attn_w2"].T.reshape(4, P, P).transpose(1, 0, 2))
    out["L3_gate_w"] = c(a["L3_ffn_gate_w"].T)
    for n, m in (("gate", "gate_proj_w"), ("up", "up_proj_w"), ("down", "down_proj_w")):
        out[f"L3_{n}"] = c(a[f"L3_ffn_{m}"].transpose(0, 2, 1))
    return out


def kernel(**inputs):
    import concourse.bacc as bacc
    from concourse.bass_utils import run_bass_kernel_spmd as run

    arrays = host_arrays(inputs)
    nc = bacc.Bacc("TRN2", target_bir_lowering=False, num_devices=1)
    dram = {k: nc.dram_tensor(f"in_{k}", v.shape, mybir.dt.from_np(v.dtype), kind="ExternalInput").ap()
            for k, v in arrays.items()}
    dram["outT"] = nc.dram_tensor("outT", (P, N), F32, kind="ExternalOutput").ap()
    build(nc, dram)
    r = run(nc, [{f"in_{k}": v for k, v in arrays.items()}], core_ids=[0])
    return np.ascontiguousarray(r.results[0]["outT"].T).reshape(B, T, P)
```

```python
import concourse.bass as bass
from concourse import mybir
import numpy as np

F32 = mybir.dt.float32
F32R = mybir.dt.float32r
BF16 = mybir.dt.bfloat16
ACT = mybir.ActivationFunctionType
ALU = mybir.AluOpType
X = mybir.AxisListType.X

P = 128
B, T = 4, 512
N = B * T
LN_EPS = 1e-5
EXPERTS = 8
CAPACITY = int(1.25 * N / EXPERTS)
LAMBDA_INIT = 0.8 - 0.6 * float(np.exp(-0.3 * 12))
MAX_ROW = 96
START = 64

SQUARES = ["L0_Wq", "L0_Wk", "L0_Wv", "L0_Wo",
           "L2_Wq", "L2_Wqs", "L2_Wk", "L2_Wks", "L2_Wv", "L2_Wo", "L2_f0", "L2_f1", "L2_f2",
           "L3_Wq", "L3_Wk", "L3_Wv", "L3_Wo"]
COLUMNS = ["L0_bo", "L1_bo", "L2_rms", "L2_bias", "L3_bo", "L3_gamma", "L3_beta", "L3_b2",
           "L3_b1_0", "L3_b1_1", "L3_b1_2", "L3_b1_3"]
SHIFT_A, SCALE_A, GATE_A, SHIFT_B, SCALE_B, GATE_B = range(6)


class Signal:

    def __init__(self, nc, name):
        self.sem = nc.alloc_semaphore(name)
        self.base = START

    def at(self, n):
        return n + self.base

    def end(self, n):
        self.base += n


def cols(c):
    return slice(c * T, (c + 1) * T)


def setup_phase(nc, g):
    D, s = g.dram, g.s
    with g.sb("wmod", [P, 4, 6 * P], F32) as wmod, \
         g.sb("cond", [P, 16], F32) as cond, \
         g.sb("cond_t", [P, 3, 16], F32) as ct, \
         g.sb("lam_in", [P, 4, 4], F32) as lam_in, \
         g.sb("lam_t", [P, 2, 4], F32) as lam_t, \
         g.sb("lam_s", [P, 4], F32) as lam_s, \
         g.sb("gate_t", [P, 4, 2, 2, B], F32) as gt, \
         g.pb("mod_ps", [P, 512], F32) as mod_ps, \
         nc.Block() as block:

        @block.sync
        def _(sp):
            sp.dma_start(cond[:], D["cT"]).then_inc(s["dma"].sem, 16)
            for i in range(4):
                sp.dma_start(wmod[:, i], D[f"L{i}_wmod"]).then_inc(s["dma"].sem, 16)
            sp.dma_start(lam_in[:], D["lambdas"].partition_broadcast(P)).then_inc(s["dma"].sem, 16)
            sp.dma_start(g.xT[:], D["xT"]).then_inc(s["dma"].sem, 16)
            sp.dma_start(g.squares[:], D["squares"]).then_inc(s["dma"].sem, 16)
            sp.dma_start(g.columns[:], D["columns"]).then_inc(s["dma"].sem, 16)
            sp.dma_start(g.consts[:], D["consts"]).then_inc(s["dma"].sem, 16)
            sp.dma_start(g.gate_w[:], D["gate_w"]).then_inc(s["dma"].sem, 16)
            sp.dma_start(g.gate_b[:], D["gate_b"].partition_broadcast(P)).then_inc(s["dma"].sem, 16)
            sp.wait_ge(s["dma"].sem, s["dma"].at(16 * 12))
            sp.dma_start(g.scratch["alibi"], D["alibi"]).then_inc(s["store"].sem, 16)
            sp.wait_ge(s["store"].sem, s["store"].at(16))

        @block.scalar
        def _(act):
            act.wait_ge(s["dma"].sem, s["dma"].at(16 * 12))
            nc.scalar.activation(ct[:, 0], cond[:], ACT.Exp, scale=-1.0).then_inc(s["act"].sem, 1)
            act.wait_ge(s["vec"].sem, s["vec"].at(8))
            nc.scalar.activation(lam_s[:, 2:4], lam_s[:, 0:2], ACT.Exp).then_inc(s["act"].sem, 1)

        @block.vector
        def _(dve):
            n = 0
            dve.wait_ge(s["act"].sem, s["act"].at(1))

            def after(ins):
                nonlocal n
                n += 1
                ins.then_inc(s["vec"].sem, 1)
                dve.wait_ge(s["vec"].sem, s["vec"].at(n))

            after(nc.vector.tensor_scalar(ct[:, 1], ct[:, 0], 1.0, None, ALU.add))
            after(nc.vector.reciprocal(ct[:, 2], ct[:, 1]))
            after(nc.vector.tensor_tensor(g.cs[:], cond[:], ct[:, 2], ALU.mult))
            after(nc.vector.tensor_tensor(lam_t[:, 0], lam_in[:, 0], lam_in[:, 1], ALU.mult))
            after(nc.vector.tensor_tensor(lam_t[:, 1], lam_in[:, 2], lam_in[:, 3], ALU.mult))
            after(nc.vector.tensor_reduce(lam_s[:, 0:2], lam_t[:], X, ALU.add))
            after(nc.vector.memset(g.eps[:, 0:1], LN_EPS))
            after(nc.vector.memset(g.eps[:, 1:2], 0.0))
            dve.wait_ge(s["act"].sem, s["act"].at(2))
            after(nc.vector.tensor_scalar(lam_s[:, 0:1], lam_s[:, 3:4], -LAMBDA_INIT, None, ALU.add))
            after(nc.vector.tensor_tensor(g.neg_lam[:], lam_s[:, 0:1], lam_s[:, 2:3], ALU.subtract))
            dve.wait_ge(s["pe"].sem, s["pe"].at(1))
            after(nc.vector.tensor_copy(g.mod[:], mod_ps[:, 0:96].rearrange(
                "p (l j b) -> p l j b", l=4, j=6)))
            for j in (SCALE_A, SCALE_B):
                after(nc.vector.tensor_scalar(g.mod[:, :, j], g.mod[:, :, j], 1.0, None, ALU.add))
            for i, j in enumerate((GATE_A, GATE_B)):
                gate = g.mod[:, :, j]
                sign, size = gt[:, :, i, 0], gt[:, :, i, 1]
                after(nc.vector.tensor_scalar(sign, gate, 0.0, 2.0, ALU.is_ge, ALU.mult))
                after(nc.vector.tensor_scalar(size, gate, -1.0, 0.25, ALU.mult, ALU.max))
                after(nc.vector.tensor_tensor(size, size, gate, ALU.max))
                after(nc.vector.tensor_scalar(sign, sign, -1.0, None, ALU.add))
                after(nc.vector.tensor_tensor(gate, size, sign, ALU.mult))
            for layer, name in ((0, "L0_bo"), (1, "L1_bo")):
                after(nc.vector.tensor_scalar(g.gate_bias[:, layer], g.mod[:, layer, GATE_A],
                                              g.col(name), None, ALU.mult))
            after(nc.vector.tensor_scalar(g.rms_w[:], g.col("L2_rms"), 1.0 - LAMBDA_INIT, None, ALU.mult))
            g.n_vec = n

        @block.tensor
        def _(pe):
            pe.wait_ge(s["vec"].sem, s["vec"].at(3))
            for layer in range(4):
                for j in range(6):
                    at = (layer * 6 + j) * B
                    mm = nc.tensor.matmul(mod_ps[:, at:at + B], wmod[:, layer, j * P:(j + 1) * P],
                                          g.cs[:, layer * B:(layer + 1) * B], start=True, stop=True)
            mm.then_inc(s["pe"].sem, 1)

    s["dma"].end(192)
    s["store"].end(16)
    s["act"].end(2)
    s["vec"].end(g.n_vec)
    s["pe"].end(1)


def norm_phase(nc, g, src, scales, shifts):
    s = g.s
    with g.sb("centred", [P, N], F32) as centred, \
         g.sb("squared", [P, N], F32) as work, \
         g.pb("mean_ps", [P, B, T], F32) as mean, \
         g.pb("var_ps", [P, B, T], F32) as var, \
         nc.Block() as block:

        @block.tensor
        def _(pe):
            for c in range(B):
                nc.tensor.matmul(mean[:, c], g.mean_w, src[:, cols(c)],
                                 start=True, stop=True).then_inc(s["mean"].sem, 1)
            for c in range(B):
                pe.wait_ge(s["square"].sem, s["square"].at(c + 1))
                nc.tensor.matmul(var[:, c], g.mean_w, work[:, cols(c)],
                                 start=True, stop=True).then_inc(s["var"].sem, 1)

        @block.scalar
        def _(act):
            for c in range(B):
                act.wait_ge(s["centre"].sem, s["centre"].at(c + 1))
                nc.scalar.activation(work[:, cols(c)], centred[:, cols(c)], ACT.Square
                                     ).then_inc(s["square"].sem, 1)
            for c in range(B):
                act.wait_ge(s["var"].sem, s["var"].at(c + 1))
                nc.scalar.activation(work[:, cols(c)], var[:, c], ACT.Ln, bias=g.eps[:, 0:1]
                                     ).then_inc(s["log"].sem, 1)
                act.wait_ge(s["log"].sem, s["log"].at(c + 1))
                nc.scalar.activation(work[:, cols(c)], work[:, cols(c)], ACT.Exp, scale=-0.5
                                     ).then_inc(s["std"].sem, 1)

        @block.vector
        def _(dve):
            for c in range(B):
                dve.wait_ge(s["mean"].sem, s["mean"].at(c + 1))
                nc.vector.tensor_tensor(centred[:, cols(c)], src[:, cols(c)], mean[:, c],
                                        ALU.subtract).then_inc(s["centre"].sem, 1)
            for c in range(B):
                dve.wait_ge(s["std"].sem, s["std"].at(c + 1))
                nc.vector.tensor_tensor(work[:, cols(c)], work[:, cols(c)], centred[:, cols(c)],
                                        ALU.mult).then_inc(s["norm"].sem, 1)
                dve.wait_ge(s["norm"].sem, s["norm"].at(2 * c + 1))
                nc.vector.tensor_scalar(g.hT[:, cols(c)], work[:, cols(c)], scales(c), shifts(c),
                                        ALU.mult, ALU.add).then_inc(s["norm"].sem, 1)

    for name in ("mean", "square", "var", "centre", "std", "log"):
        s[name].end(B)
    s["norm"].end(2 * B)


def by_part(tensor, parts):
    return tensor[:].rearrange("p (i t w) -> p i t w", i=B * parts, t=T // P)


def small_head_stacks(g):
    return (g.sb("q_stack", [P, 4, 4, T], F32R), g.sb("k_stack", [P, 4, 4, T], F32R),
            g.sb("v_group", [P, 4, T // P, P], F32))


def small_head_projections(nc, g, stacks, hd, wq, wk, wv, wq_swapped=None, wk_swapped=None):
    s = g.s
    heads = P // hd
    rope = wq_swapped is not None
    per_b = [("q", wq), ("qs", wq_swapped), ("k", wk), ("ks", wk_swapped)] if rope else [("q", wq), ("k", wk)]
    tasks = [(b, kind, w) for b in range(B) for kind, w in per_b + [("v", wv)]]
    n_task = len(tasks) // B
    parts = heads // 16
    q_scr = g.scratch["q"].rearrange("(b e r) t -> b e r t", b=B, e=heads)
    k_scr = g.scratch["k"].rearrange("(b e r) t -> b e r t", b=B, e=heads)
    with g.sb("full", [P, 4 if rope else 2, N], F32) as full, \
         g.sb("hi", [P, 2, N], F32) as hi, \
         g.sb("lo", [P, 2, N], F32) as lo, \
         g.sb("rope", [P, 2, T], F32) as rope_t, \
         g.pb("proj", [P, 8, T], F32) as ps, \
         nc.Block() as block:
        slot = {"q": 0, "k": 1, "qs": 2, "ks": 3}
        hi_r = hi[:].bitcast(F32R)

        @block.gpsimd
        def _(pool):
            qs, ks, vg = stacks
            nc.gpsimd.memset(ks[:].bitcast(F32), 0.0).then_inc(s["zeros"].sem, 1)
            nc.gpsimd.memset(vg[:], 1.0).then_inc(s["zeros"].sem, 1)
            nc.gpsimd.memset(qs[:].bitcast(F32), 0.0).then_inc(s["zeros"].sem, 1)
            pool.wait_ge(s["zeros"].sem, s["zeros"].at(3))
            nc.gpsimd.memset(ks[MAX_ROW:MAX_ROW + 2].bitcast(F32), 1.0).then_inc(s["zeros"].sem, 1)

        @block.tensor
        def _(pe):
            for n, (b, kind, w) in enumerate(tasks):
                if n >= 8:
                    pe.wait_ge(s["evac"].sem, s["evac"].at(n - 7))
                if kind != "v":
                    mm = nc.tensor.matmul(ps[:, n % 8], g.square(w), g.hT[:, cols(b)], start=True, stop=True)
                else:
                    for t in range(T // P):
                        at = b * T + t * P
                        mm = nc.tensor.matmul(ps[:, n % 8, t * P:(t + 1) * P], g.hT[:, at:at + P],
                                              g.square(w), start=True, stop=True)
                mm.then_inc(s["mm"].sem, 1)

        @block.scalar
        def _(act):
            for n, (b, kind, _) in enumerate(tasks):
                act.wait_ge(s["mm"].sem, s["mm"].at(n + 1))
                if kind != "v":
                    nc.scalar.activation(full[:, slot[kind], cols(b)], ps[:, n % 8], ACT.Copy
                                         ).then_inc(s["evac"].sem, 1)
                else:
                    nc.scalar.activation(
                        by_part(g.v_tok, parts)[:, b * parts:(b + 1) * parts],
                        ps[:, n % 8].rearrange("p (t i w) -> p i t w", t=T // P, i=parts), ACT.Copy
                    ).then_inc(s["evac"].sem, 1)

        @block.vector
        def _(dve):
            step = s["vec"]
            n = 0

            def after(ins):
                nonlocal n
                n += 1
                ins.then_inc(step.sem, 1)
                dve.wait_ge(step.sem, step.at(n))

            if rope:
                dve.wait_ge(s["dma"].sem, s["dma"].at(16))
            for b in range(B):
                dve.wait_ge(s["evac"].sem, s["evac"].at(n_task * b + len(per_b)))
                for i in range(2):
                    f = full[:, i, cols(b)]
                    if rope:
                        f2 = full[:, 2 + i, cols(b)]
                        after(nc.vector.tensor_tensor(f, f, rope_t[:, 0], ALU.mult))
                        after(nc.vector.tensor_tensor(f2, f2, rope_t[:, 1], ALU.mult))
                        after(nc.vector.tensor_tensor(f, f, f2, ALU.add))
                    after(nc.vector.tensor_copy(hi_r[:, i, cols(b)], f))
                    nc.vector.tensor_tensor(lo[:, i, cols(b)], f, hi[:, i, cols(b)], ALU.subtract
                                            ).then_inc(s["split"].sem, 1)
            g.n_vec = n

        @block.sync
        def _(sp):
            if rope:
                sp.dma_start(rope_t[:], g.dram["rope"]).then_inc(s["dma"].sem, 16)
            for b in range(B):
                for i, (scr, parts) in enumerate(((q_scr, (hi, hi, lo)), (k_scr, (hi, lo, hi)))):
                    sp.wait_ge(s["split"].sem, s["split"].at(2 * b + i + 1))
                    for r, part in enumerate(parts):
                        sp.dma_start(scr[b, :, r * hd:(r + 1) * hd, :], part[:, i, cols(b)]
                                     ).then_inc(s["store"].sem, 16)
            sp.wait_ge(s["store"].sem, s["store"].at(16 * 6 * B))

    s["zeros"].end(4)
    s["mm"].end(len(tasks))
    s["evac"].end(len(tasks))
    s["vec"].end(g.n_vec)
    s["split"].end(2 * B)
    s["store"].end(16 * 6 * B)
    if rope:
        s["dma"].end(16)


def small_head_attention(nc, g, stacks, hd, scale, differential=False):
    s = g.s
    heads = P // hd
    NG = B * heads // 4
    K1 = 3 * hd
    KT = T // P
    TILES = 4 * KT
    DIVIDE = 5 if differential else 2
    BODY = 4
    q_scr = g.scratch["q"].rearrange("(e r) t -> e r t", r=K1)
    k_scr = g.scratch["k"].rearrange("(e r) t -> e r t", r=K1)
    HD_V = 8
    PAIR = 2 if differential else 1
    v_part, out_part = by_part(g.v_tok, heads // 16), by_part(g.att_tok, heads // 16)
    WIDTH = 4 // PAIR * HD_V
    qs, ks, vg = stacks
    with g.sb("probs", [P, KT, 4, T], F32) as probs, \
         g.sb("neg_max", [P, 2, TILES], F32) as neg_max, \
         g.sb("max_parts", [TILES, 2, 2, P], F32) as max_parts, \
         g.sb("raw", [P, 2, T], F32) as raw, \
         g.sb("recip", [P, KT, 4], F32) as recip, \
         g.sb("second", [P, 2, KT, 2, HD_V], F32) as pair_t, \
         g.pb("scores", [P, 4, T], F32) as sc_ps, \
         g.pb("scoresT", [P, 2, T], F32) as st_ps, \
         g.pb("values", [P, T], F32) as o_ps, \
         g.pb("rawT", [P, KT, 4, 32], F32) as rt_ps, \
         nc.Block() as block:
        mt_ps = rt_ps[:].rearrange("p t j r -> p (t j r)")[0:TILES, 0:P]
        SPLIT = 5

        def group(i, p, d=0):
            i, p = i + (p + d) // BODY, (p + d) % BODY
            if isinstance(i, int) and not 0 <= BODY * i + p < NG:
                return None
            return i, p, i * BODY + p

        def steps(eng, step):
            for i in (-1, 0):
                for p in range(BODY):
                    step(i, p)
            with eng.Fori(1, NG // BODY - 1) as i:
                for p in range(BODY):
                    step(i, p)
            for i in (NG // BODY - 1, NG // BODY):
                for p in range(BODY):
                    step(i, p)

        @block.sync
        def _(sp):
            def step(i, p):
                if at := group(i, p, 3):
                    gi, gp, n = at
                    sp.wait_ge(s["st"].sem, s["st"].at(TILES * (n - 3)))
                    for dst, src in ((qs, q_scr), (ks, k_scr)):
                        sp.dma_start(dst[0:K1, gp].bitcast(F32), src[bass.ds(n * 4, 4)].rearrange("e r t -> r e t")
                                     ).then_inc(s[f"load{gp}"].sem, 16)
                if at := group(i, p, 1):
                    gi, gp, n = at
                    sp.wait_ge(s["max_split"].sem, s["max_split"].at(n + 1))
                    for r in range(2):
                        sp.dma_start(qs[MAX_ROW + r:MAX_ROW + r + 1, gp].bitcast(F32)
                                     .rearrange("o j (t q) -> o (j t) q", t=KT), max_parts[:, gp % 2, r]).then_inc(s[f"rows{gp % 2}"].sem, 16)

            steps(sp, step)

        @block.gpsimd
        def _(pool):
            by_one = g.all_ones[:, 0:KT * WIDTH].rearrange("p (t j d) -> p t j d", t=KT, d=HD_V)

            def step(i, p):
                if at := group(i, p, 1):
                    gi, gp, n = at
                    pool.wait_ge(s["pv"].sem, s["pv"].at(KT * (n - 3)))
                    dst = vg[:, gp].rearrange("p t (j c r) -> p c t j r", c=PAIR, r=32)
                    for c in range(PAIR):
                        src = v_part[:, bass.ds(gi, 1), :, gp * WIDTH:(gp + 1) * WIDTH].rearrange(
                            "p i t (j d) -> p (i t) j d", d=HD_V)
                        nc.gpsimd.tensor_tensor(dst[:, c, :, :, 0:HD_V], src, by_one, ALU.mult
                                                ).then_inc(s["vg"].sem, 1)

            steps(pool, step)

        @block.scalar
        def _(act):
            def step(i, p):
                cur = group(i, p)
                for t in range(TILES):
                    if cur:
                        _, _, n = cur
                        kt, j = t // 4, t % 4
                        act.wait_ge(s["st"].sem, s["st"].at(TILES * n + t + 1))
                        if j == 0:
                            act.wait_ge(s["pv"].sem, s["pv"].at(KT * (n - 1) + kt + 1))
                        nc.scalar.activation(probs[:, kt, j], st_ps[:, t % 2], ACT.Exp, scale=scale
                                             ).then_inc(s["exp"].sem, 1)
                    if t == 4 and (at := group(i, p, -1)):
                        gi, gp, n = at
                        act.wait_ge(s["pv"].sem, s["pv"].at(KT * (n + 1)))
                        act.wait_ge(s["rawT"].sem, s["rawT"].at(n - 1))
                        nc.scalar.activation(raw[:, gp % 2], o_ps[:], ACT.Identity,
                                             bias=g.den_eps(hd)).then_inc(s["raw"].sem, 1)

            steps(act, step)

        @block.vector
        def _(dve):
            def divide(at, first):
                gi, gp, n = at
                done = lambda ins: ins.then_inc(s["divide"].sem, 1)
                dve.wait_ge(s["divide"].sem, s["divide"].at(DIVIDE * n + first))
                out = out_part[:, bass.ds(gi, 1), :, gp * WIDTH:(gp + 1) * WIDTH].rearrange(
                    "p i t (j d) -> p (i t) j d", d=HD_V)
                spread = [P, KT, 4 // PAIR, HD_V]
                if first == 0:
                    dve.wait_ge(s["rawT"].sem, s["rawT"].at(n + 1))
                    done(nc.vector.reciprocal(recip[:], rt_ps[:, :, :, HD_V]))
                elif not differential:
                    done(nc.vector.tensor_tensor(out, rt_ps[:, :, :, 0:HD_V],
                                                 recip[:].unsqueeze(3).broadcast_to(spread), ALU.mult))
                elif first == 1:
                    done(nc.vector.tensor_scalar(recip[:, :, 1::2], recip[:, :, 1::2], g.neg_lam[:], None,
                                                 ALU.mult))
                elif first < 4:
                    c = first - 2
                    done(nc.vector.tensor_tensor(pair_t[:, c], rt_ps[:, :, c::2, 0:HD_V],
                                                 recip[:, :, c::2].unsqueeze(3).broadcast_to(spread),
                                                 ALU.mult))
                else:
                    done(nc.vector.tensor_tensor(out, pair_t[:, 0], pair_t[:, 1], ALU.add))

            def step(i, p):
                ahead, next_, last = group(i, p, 2), group(i, p, 1), group(i, p, -1)
                for t in range(TILES):
                    if ahead:
                        _, gp, n = ahead
                        dve.wait_ge(s["scores"].sem, s["scores"].at(TILES * n + t + 1))
                        if t == 0:
                            dve.wait_ge(s["maxT"].sem, s["maxT"].at(n - 1))
                        nc.vector.tensor_reduce(neg_max[:, gp % 2, t:t + 1], sc_ps[:, t % 4], X, ALU.max,
                                                negate=True).then_inc(s["max"].sem, 1)
                    if t == SPLIT and next_:
                        _, gp, n = next_
                        dve.wait_ge(s["maxT"].sem, s["maxT"].at(n + 1))
                        dve.wait_ge(s[f"rows{gp % 2}"].sem, s[f"rows{gp % 2}"].at(next_[0] * 64 + 32 * (gp // 2)))
                        nc.vector.tensor_copy(max_parts[:, gp % 2, 0].bitcast(F32R), mt_ps
                                              ).then_inc(s["max_hi"].sem, 1)
                    if t == SPLIT + 1 and next_:
                        _, gp, n = next_
                        dve.wait_ge(s["max_hi"].sem, s["max_hi"].at(n + 1))
                        nc.vector.tensor_tensor(max_parts[:, gp % 2, 1], mt_ps, max_parts[:, gp % 2, 0],
                                                ALU.subtract).then_inc(s["max_split"].sem, 1)
                    if t >= TILES - 4 and last and t - (TILES - 4) < DIVIDE:
                        divide(last, t - (TILES - 4))
                if last and DIVIDE > 4:
                    divide(last, 4)

            steps(dve, step)

        @block.tensor
        def _(pe):
            def values(cur, kt):
                _, gp, n = cur
                pe.wait_ge(s["exp"].sem, s["exp"].at(TILES * n + 4 * kt + 4))
                if kt == 0:
                    pe.wait_ge(s["raw"].sem, s["raw"].at(n))
                    pe.wait_ge(s["vg"].sem, s["vg"].at((n + 1) * PAIR))
                for j in range(4):
                    mm = nc.tensor.matmul(o_ps[32 * j:32 * j + 32], vg[:, gp, kt, 32 * j:32 * j + 32],
                                          probs[:, kt, j], start=kt == 0, stop=kt == KT - 1)
                mm.then_inc(s["pv"].sem, 1)

            def step(i, p):
                ahead, cur = group(i, p, 2), group(i, p)
                if ahead:
                    gi, gp, n = ahead
                    pe.wait_ge(s[f"load{gp}"].sem, s[f"load{gp}"].at(gi * 32 + 32))
                if cur:
                    gi, gp, n = cur
                    pe.wait_ge(s[f"rows{gp % 2}"].sem, s[f"rows{gp % 2}"].at(gi * 64 + 32 * (gp // 2) + 32))
                for t in range(TILES):
                    if ahead:
                        gi, gp, n = ahead
                        j, qt = t // KT, t % KT
                        pe.wait_ge(s["max"].sem, s["max"].at(TILES * n + t - 3))
                        r = slice(0, MAX_ROW)
                        nc.tensor.matmul(sc_ps[:, t % 4], qs[r, gp, j, qt * P:(qt + 1) * P], ks[r, gp, j],
                                         start=True, stop=True).then_inc(s["scores"].sem, 1)
                    if cur:
                        gi, gp, n = cur
                        kt, j = t // 4, t % 4
                        pe.wait_ge(s["exp"].sem, s["exp"].at(TILES * n + t - 1))
                        nc.tensor.matmul(st_ps[:, t % 2], ks[:, gp, j, kt * P:(kt + 1) * P], qs[:, gp, j],
                                         start=True, stop=True).then_inc(s["st"].sem, 1)
                    if t == SPLIT - 1 and (at := group(i, p, 1)):
                        _, gp, n = at
                        pe.wait_ge(s["max"].sem, s["max"].at(TILES * (n + 1)))
                        pe.wait_ge(s["divide"].sem, s["divide"].at(DIVIDE * (n - 2)))
                        nc.tensor.transpose(mt_ps, neg_max[:, gp % 2], g.identity
                                            ).then_inc(s["maxT"].sem, 1)
                    if t == TILES - 4 and (at := group(i, p, -1)):
                        _, gp, n = at
                        pe.wait_ge(s["raw"].sem, s["raw"].at(n + 1))
                        pe.wait_ge(s["divide"].sem, s["divide"].at(DIVIDE * n))
                        if at_next := group(i, p, 1):
                            pe.wait_ge(s["max_split"].sem, s["max_split"].at(at_next[2] + 1))
                        for qt in range(KT):
                            mm = nc.tensor.transpose(rt_ps[:, qt].rearrange("p j r -> p (j r)"),
                                                     raw[:, gp % 2, qt * P:(qt + 1) * P], g.identity)
                        mm.then_inc(s["rawT"].sem, 1)
                    if t == 2 and (at := group(i, p, -1)):
                        values(at, KT - 1)
                    if cur and t % 4 == 2 and t > 4:
                        values(cur, t // 4 - 1)

            steps(pe, step)

    for name in ("st", "scores", "max", "exp"):
        s[name].end(TILES * NG)
    for name in ("max_split", "max_hi", "maxT", "raw", "rawT"):
        s[name].end(NG)
    s["divide"].end(DIVIDE * NG)
    s["pv"].end(KT * NG)
    s["vg"].end(NG * PAIR)
    for p in range(BODY):
        s[f"load{p}"].end(32 * NG // BODY)
    for q in range(2):
        s[f"rows{q}"].end(32 * NG // 2)


def attention_output(nc, g, layer, weights, biased):
    s = g.s
    att = g.att_tok[:].rearrange("p (n d) -> p n d", d=P)
    with g.sb("attn", [P, B, T], F32) as attn, \
         g.sb("update", [P, B, T], F32) as upd, \
         g.pb("turn_ps", [P, B, T], F32) as turn_ps, \
         g.pb("out_ps", [P, B, T], F32) as ps, \
         nc.Block() as block:

        @block.tensor
        def _(pe):
            for b in range(B):
                for t in range(T // P):
                    mm = nc.tensor.transpose(turn_ps[:, b, t * P:(t + 1) * P], att[:, b * (T // P) + t],
                                             g.identity)
                mm.then_inc(s["rawT"].sem, 1)
            for b in range(B):
                pe.wait_ge(s["evac"].sem, s["evac"].at(b + 1))
                nc.tensor.matmul(ps[:, b], weights, attn[:, b], start=True, stop=True
                                 ).then_inc(s["mm"].sem, 1)

        @block.scalar
        def _(act):
            for b in range(B):
                act.wait_ge(s["rawT"].sem, s["rawT"].at(b + 1))
                nc.scalar.activation(attn[:, b], turn_ps[:, b], ACT.Copy).then_inc(s["evac"].sem, 1)
            for b in range(B):
                act.wait_ge(s["mm"].sem, s["mm"].at(b + 1))
                bias = g.gate_bias[:, layer, b:b + 1] if biased else 0.0
                nc.scalar.activation(upd[:, b], ps[:, b], ACT.Identity, bias=bias,
                                     scale=g.mod[:, layer, GATE_A, b:b + 1]).then_inc(s["act"].sem, 1)

        @block.vector
        def _(dve):
            for b in range(B):
                dve.wait_ge(s["act"].sem, s["act"].at(b + 1))
                nc.vector.tensor_tensor(g.xT[:, cols(b)], g.xT[:, cols(b)], upd[:, b], ALU.add
                                        ).then_inc(s["vec"].sem, 1)

    for name in ("rawT", "evac", "mm", "act", "vec"):
        s[name].end(B)


class Router:

    NT, E = N // P, EXPERTS

    def __init__(self, nc, g, kind, gate, r, rc, totals_sb, rows, banks, rows_banks):
        self.nc, self.s, self.g, self.kind = nc, g.s, g, kind
        self.r, self.rc, self.totals_sb, self.rows, self.rows_banks = r, rc, totals_sb, rows, rows_banks
        self.gate_w = g.gate_w[:, gate]
        self.gate_b = g.gate_b[:, gate] if gate < 2 else None
        W = self.NT * self.E
        self.nk = 2 if kind == "each" else 1
        self.logits, self.totals = banks[:, 0, 0:W], banks[:, 0, W:(1 + self.nk) * W]
        self.counts = banks[:, 1, 0:self.nk * W]

    P_, SEL, EQ, OH1, OH2, V, M, M_2, COMB, T1 = range(10)
    M1, M2, I1, SUM, R1, W1, W2 = range(7)

    def tensor_logits(self, pe):
        s, nc, E = self.s, self.nc, self.E
        for t in range(self.NT):
            mm = nc.tensor.matmul(self.logits[:, t * E:(t + 1) * E], self.g.hT[:, t * P:(t + 1) * P],
                                  self.gate_w, start=True, stop=True)
        mm.then_inc(s["logits"].sem, 1)

    def tensor(self, pe):
        s, nc, g, E, W = self.s, self.nc, self.g, self.E, self.NT * self.E
        if self.kind != "open":
            pe.wait_ge(s["chosen"].sem, s["chosen"].at(1))
            for k in range(self.nk):
                one = slice(k * W, (k + 1) * W)
                chosen = self.r[:, self.M + k].rearrange("p t e -> p (t e)")
                mm = nc.tensor.matmul(self.totals[:, one], chosen, g.all_ones, start=True, stop=True)
            mm.then_inc(s["totals"].sem, 1)
            pe.wait_ge(s["evac"].sem, s["evac"].at(1))
            for k in range(self.nk):
                one = slice(k * W, (k + 1) * W)
                chosen = self.r[:, self.M + k].rearrange("p t e -> p (t e)")
                nc.tensor.matmul(self.counts[:, one], g.tri, chosen, start=True, stop=False)
                mm = nc.tensor.matmul(self.counts[:, one], self.totals_sb[:, k], g.before, start=False, stop=True)
            mm.then_inc(s["counts"].sem, 1)
        pe.wait_ge(s["chosen"].sem, s["chosen"].at(2))
        for t in range(self.NT):
            mm = nc.tensor.transpose(self.rows_banks[t // 4][0:E, (t % 4) * P:(t % 4 + 1) * P],
                                     self.r[:, self.COMB, t], g.identity)
        mm.then_inc(s["maxT"].sem, 1)

    def scalar(self, act):
        s, nc = self.s, self.nc
        act.wait_ge(s["centre"].sem, s["centre"].at(1))
        nc.scalar.activation(self.r[:, self.T1], self.r[:, self.P_], ACT.Exp).then_inc(s["act"].sem, 1)
        if self.kind != "open":
            act.wait_ge(s["totals"].sem, s["totals"].at(1))
            nc.scalar.activation(self.totals_sb[:, 0:self.nk].rearrange("p k w -> p (k w)"), self.totals,
                                 ACT.Copy).then_inc(s["evac"].sem, 1)
        act.wait_ge(s["maxT"].sem, s["maxT"].at(1))
        for c in range(B):
            nc.scalar.activation(self.rows[:, cols(c)], self.rows_banks[c][0:self.E], ACT.Copy
                                 ).then_inc(s["evac"].sem, 1)

    def rows_ready(self):
        return self.s["evac"].at(B + (self.kind != "open"))

    def store(self, sp):
        s, g = self.s, self.g
        sp.dma_start(g.scratch["comb"][self.E].rearrange("(a b) -> a b", b=P), g.all_ones[0:self.NT, :]
                     ).then_inc(s["store"].sem, 16)
        sp.wait_ge(s["evac"].sem, self.rows_ready())
        sp.dma_start(g.scratch["comb"][0:self.E, :], self.rows[:]).then_inc(s["store"].sem, 16)
        sp.wait_ge(s["store"].sem, s["store"].at(32))

    def vector(self, dve):
        s, g, v, r, rc, kind, nk = self.s, self.g, self.nc.vector, self.r, self.rc, self.kind, self.nk
        NT, E = self.NT, self.E
        P_, SEL, EQ, OH1, OH2, V, M, COMB, T1 = (self.P_, self.SEL, self.EQ, self.OH1, self.OH2, self.V,
                                                 self.M, self.COMB, self.T1)
        M1, M2, I1, SUM, R1, W1, W2 = self.M1, self.M2, self.I1, self.SUM, self.R1, self.W1, self.W2
        big = 1e30 if kind == "open" else 4.0
        n = 0

        def spread(col):
            return col.unsqueeze(2).broadcast_to([P, NT, E])

        def over_tiles(t):
            return t.unsqueeze(1).broadcast_to([P, NT, E])

        def after(ins):
            nonlocal n
            n += 1
            ins.then_inc(s["route"].sem, 1)
            dve.wait_ge(s["route"].sem, s["route"].at(n))

        dve.wait_ge(s["logits"].sem, s["logits"].at(1))
        source = self.logits.rearrange("p (t e) -> p t e", e=E)
        if kind == "norm":
            after(v.tensor_tensor(r[:, P_], source, over_tiles(self.gate_b), ALU.add))
            source = r[:, P_]
        after(v.tensor_reduce(rc[:, M1], source, X, ALU.max))
        v.tensor_tensor(r[:, P_], source, spread(rc[:, M1]), ALU.subtract).then_inc(s["centre"].sem, 1)
        dve.wait_ge(s["act"].sem, s["act"].at(1))
        after(v.tensor_reduce(rc[:, SUM], r[:, T1], X, ALU.add))
        after(v.reciprocal(rc[:, R1], rc[:, SUM]))
        after(v.tensor_tensor(r[:, P_], r[:, T1], spread(rc[:, R1]), ALU.mult))
        sel = P_
        if kind == "open":
            sel = SEL
            after(v.tensor_tensor(r[:, SEL], r[:, P_], over_tiles(self.gate_b), ALU.add))
        for m, oh in ((M1, OH1), (M2, OH2)):
            after(v.tensor_reduce(rc[:, m], r[:, sel], X, ALU.max))
            after(v.tensor_tensor(r[:, EQ], r[:, sel], spread(rc[:, m]), ALU.is_equal))
            after(v.tensor_tensor(r[:, V], r[:, EQ], over_tiles(g.iota), ALU.mult))
            after(v.tensor_reduce(rc[:, I1], r[:, V], X, ALU.min))
            one_hot = oh if kind != "each" else M if m == M1 else self.M_2
            choice = v.tensor_tensor(r[:, one_hot], over_tiles(g.iota), spread(rc[:, I1]), ALU.is_equal)
            if m == M1:
                after(choice)
                after(v.tensor_scalar(r[:, T1], r[:, one_hot], -big, None, ALU.mult))
                after(v.tensor_tensor(r[:, SEL], r[:, T1], r[:, sel], ALU.add))
                sel = SEL
            elif kind == "each":
                choice.then_inc(s["chosen"].sem, 1)
            else:
                after(choice)
        if kind == "open":
            after(v.tensor_tensor(r[:, EQ], r[:, OH1], r[:, OH2], ALU.add))
            v.tensor_tensor(r[:, COMB], r[:, EQ], r[:, P_], ALU.mult).then_inc(s["chosen"].sem, 2)
        else:
            if kind == "norm":
                v.tensor_tensor(r[:, M], r[:, OH1], r[:, OH2], ALU.add).then_inc(s["chosen"].sem, 1)
            dve.wait_ge(s["chosen"].sem, s["chosen"].at(1))
            after(v.tensor_tensor(rc[:, SUM], rc[:, M1], rc[:, M2], ALU.add))
            if kind == "each":
                after(v.tensor_scalar(rc[:, SUM], rc[:, SUM], 1e-9, None, ALU.add))
            after(v.reciprocal(rc[:, R1], rc[:, SUM]))
            after(v.tensor_tensor(rc[:, W1:W2 + 1], rc[:, M1:M2 + 1],
                                  rc[:, R1].unsqueeze(1).broadcast_to([P, 2, NT]), ALU.mult))
            for m, oh, k in ((W1, OH1, M), (W2, OH2, self.M_2)):
                after(v.tensor_tensor(r[:, oh], r[:, k if kind == "each" else oh], spread(rc[:, m]), ALU.mult))
            if kind == "norm":
                after(v.tensor_tensor(r[:, OH1], r[:, OH1], r[:, OH2], ALU.add))
            dve.wait_ge(s["counts"].sem, s["counts"].at(1))
            counts = self.counts.rearrange("p (k t e) -> p k t e", k=nk, e=E)
            if kind == "norm":
                v.scalar_tensor_tensor(r[:, COMB], counts[:, 0], float(CAPACITY), r[:, OH1], ALU.is_le, ALU.mult
                                       ).then_inc(s["chosen"].sem, 1)
            else:
                after(v.scalar_tensor_tensor(r[:, OH1:OH2 + 1], counts, float(CAPACITY), r[:, OH1:OH2 + 1],
                                             ALU.is_le, ALU.mult))
                v.tensor_tensor(r[:, COMB], r[:, OH1], r[:, OH2], ALU.add).then_inc(s["chosen"].sem, 1)
        self.steps = n

    def end(self):
        s, ranked = self.s, self.kind != "open"
        s["route"].end(self.steps)
        s["chosen"].end(2)
        s["evac"].end(B + ranked)
        s["store"].end(32)
        for name in ("maxT", "centre", "act", "logits") + (("totals", "counts") if ranked else ()):
            s[name].end(1)


def experts_phase(nc, g, layer, kind, gate, up_names, down_name, n_experts, ff, gated, b1_name=None,
                  b2_name=None):
    s = g.s
    FT = ff // P
    NU = len(up_names)
    turns = (n_experts - 1) // 2
    PASSES = ((0, 0), (0, 1), (1, 0))
    with g.sb("w_up", [P, 2, NU, ff], F32) as wu, \
         g.sb("w_down", [P, 2, FT, P], F32) as wd, \
         g.sb("w_up_parts", [P, 2, 2, NU, ff], F32R) as wup, \
         g.sb("w_down_parts", [P, 2, 2, FT, P], F32R) as wdp, \
         g.sb("h_parts", [P, 2, N], F32R) as hp, \
         g.sb("b_up", [P, 2, FT], F32) as bu, \
         g.sb("weights_of", [P, 2, N], F32) as cb, \
         g.sb("hidden", [P, 4, T], F32) as full, \
         g.sb("hidden_parts", [P, 2, 2, FT, T], F32R) as hid, \
         g.sb("silu", [P, 2, T], F32) as silu, \
         g.sb("weighted", [P, 2, T], F32) as wtd, \
         g.sb("acc", [P, B, T], F32) as acc, \
         g.sb("b_down", [EXPERTS, P], F32) as bd, \
         g.sb("comb_rows", [EXPERTS, N], F32) as rows, \
         g.sb("router", [P, 10, N // P, EXPERTS], F32) as r, \
         g.sb("router_col", [P, 7, N // P], F32) as rc, \
         g.sb("totals", [P, 2, P], F32) as totals_sb, \
         g.pb("up_ps", [P, 4, T], F32) as up_ps, \
         g.pb("down_ps", [P, 2, T], F32) as dn_ps, \
         g.pb("router_ps", [P, 2, T], F32) as r_ps, \
         nc.Block() as block:
        f32 = lambda ap: ap.bitcast(F32)
        spare = [dn_ps[:, 0], dn_ps[:, 1], r_ps[:, 0], r_ps[:, 1]]
        router = Router(nc, g, kind, gate, r, rc, totals_sb, rows, r_ps, spare)
        w_load = 16 * (NU + 1)

        def experts(eng, step):
            with eng.Fori(0, turns) as i:
                for q in range(2):
                    step(i * 2 + q, q, i)
            for e in range(2 * turns, n_experts):
                step(e, e % 2, e // 2)

        def following(e, q, i, c):
            if c + 1 < B:
                return e, q, i, c + 1
            if isinstance(e, int) and e + 1 == n_experts:
                return None
            return e + 1, 1 - q, i + q, 0

        @block.sync
        def _(sp):
            if b2_name:
                sp.dma_start(bd[:], g.dram[b2_name]).then_inc(s["dma"].sem, 16)

            def load_weights(e, q):
                one = bass.ds(e, 1)
                for k, name in enumerate(up_names):
                    sp.dma_start(wu[:, q, k], g.dram[name][one].rearrange("o d f -> (o d) f")
                                 ).then_inc(s[f"load{q}"].sem, 16)
                sp.dma_start(wd[:, q], g.dram[down_name][one].rearrange("o (t p) d -> p (o t) d", p=P)
                             ).then_inc(s[f"load{q}"].sem, 16)

            def load_bias(e, q):
                if b1_name:
                    sp.dma_start(bu[:, q], g.dram[b1_name][bass.ds(e, 1)].rearrange("o p t -> (o p) t")
                                 ).then_inc(s[f"bias{q}"].sem, 16)

            def step(e, q):
                sp.wait_ge(s["added"].sem, s["added"].at(B * (e - 1)))
                sp.dma_start(cb[:, q], g.scratch["comb"][bass.ds(e, 1)].rearrange("o n -> (o n)")
                             .partition_broadcast(P)).then_inc(s[f"comb{q}"].sem, 16)
                if not isinstance(e, int) or e + 2 < n_experts:
                    sp.wait_ge(s["w_split"].sem, s["w_split"].at(e + 1))
                    load_weights(e + 2, q)
                    if b1_name:
                        sp.wait_ge(s["full"].sem, s["full"].at(B * FT * (e + 1)))
                        load_bias(e + 2, q)

            for e in range(2):
                load_weights(e, e)
                load_bias(e, e)
            router.store(sp)
            with sp.Fori(0, (n_experts - 2) // 2) as i:
                for q in range(2):
                    step(i * 2 + q, q)
            for e in range((n_experts - 2) // 2 * 2, n_experts):
                step(e, e % 2)

        @block.tensor
        def _(pe):
            def up(at):
                e, q, i, c = at
                if c == 0:
                    pe.wait_ge(s["w_split"].sem, s["w_split"].at(e + 1))
                for t in range(FT):
                    for k in range(NU):
                        h = (e * B + c) * FT + t
                        n = (c * FT + t) * NU + k
                        pe.wait_ge(s["full"].sem, s["full"].at(h - 1 if gated else h - 3))
                        for w_part, h_part in PASSES:
                            mm = nc.tensor.matmul(up_ps[:, n % 4], wup[:, q, w_part, k, t * P:(t + 1) * P],
                                                  hp[:, h_part, cols(c)], start=w_part + h_part == 0,
                                                  stop=w_part == 1)
                        mm.then_inc(s["up"].sem, 1)

            def step(e, q, i):
                for c in range(B):
                    if after := following(e, q, i, c):
                        up(after)
                    m = e * B + c
                    pe.wait_ge(s["lo"].sem, s["lo"].at((m + 1) * FT))
                    pe.wait_ge(s["weighted"].sem, s["weighted"].at(m - 1))
                    for t in range(FT):
                        for w_part, h_part in PASSES:
                            mm = nc.tensor.matmul(dn_ps[:, c % 2], wdp[:, q, w_part, t], hid[:, c % 2, h_part, t],
                                                  start=t + w_part + h_part == 0,
                                                  stop=t == FT - 1 and w_part == 1)
                    mm.then_inc(s["down"].sem, 1)

            router.tensor_logits(pe)
            pe.wait_ge(s["split"].sem, s["split"].at(B))
            up((0, 0, 0, 0))
            router.tensor(pe)
            pe.wait_ge(s["evac"].sem, router.rows_ready())
            if b2_name:
                pe.wait_ge(s["dma"].sem, s["dma"].at(16))
                for c in range(B):
                    nc.tensor.matmul(spare[c], bd[:], rows[:, cols(c)], start=True, stop=True
                                     ).then_inc(s["mm"].sem, 1)
                pe.wait_ge(s["first"].sem, s["first"].at(B))
            experts(pe, step)

        @block.scalar
        def _(act):
            for c in range(B):
                nc.scalar.activation(hp[:, 0, cols(c)], g.hT[:, cols(c)], ACT.Copy).then_inc(s["max_hi"].sem, 1)
            router.scalar(act)

            def step(e, q, i):
                if b1_name:
                    act.wait_ge(s[f"bias{q}"].sem, s[f"bias{q}"].at(16 * (i + 1)))

                def hi(c, t):
                    h = (e * B + c) * FT + t
                    act.wait_ge(s["full"].sem, s["full"].at(h + 1))
                    nc.scalar.activation(hid[:, c % 2, 0, t], full[:, (c * FT + t) % 4], ACT.Copy
                                         ).then_inc(s["hi"].sem, 1)

                for c in range(B):
                    m = e * B + c
                    act.wait_ge(s["down"].sem, s["down"].at(m - 1))
                    for t in range(FT):
                        h, n = m * FT + t, (c * FT + t) * NU
                        act.wait_ge(s["up"].sem, s["up"].at(h * NU + 1))
                        if gated:
                            act.wait_ge(s["full"].sem, s["full"].at(h - 1))
                            nc.scalar.activation(silu[:, (c * FT + t) % 2], up_ps[:, n % 4], ACT.Silu
                                                 ).then_inc(s["silu"].sem, 1)
                        else:
                            act.wait_ge(s["lo"].sem, s["lo"].at(h - 3))
                            nc.scalar.activation(full[:, n % 4], up_ps[:, n % 4], ACT.Relu,
                                                 bias=bu[:, q, t:t + 1]).then_inc(s["full"].sem, 1)
                        if t:
                            hi(c, t - 1)
                    hi(c, FT - 1)

            experts(act, step)

        @block.vector
        def _(dve):
            for c in range(B):
                dve.wait_ge(s["max_hi"].sem, s["max_hi"].at(c + 1))
                nc.vector.tensor_tensor(hp[:, 1, cols(c)], g.hT[:, cols(c)], f32(hp[:, 0, cols(c)]),
                                        ALU.subtract).then_inc(s["split"].sem, 1)
            def split_weights(e, q, i):
                dve.wait_ge(s[f"load{q}"].sem, s[f"load{q}"].at(w_load * (i + 1)))
                dve.wait_ge(s["down"].sem, s["down"].at(B * (e - 1)))
                nc.vector.tensor_copy(wup[:, q, 0], wu[:, q]).then_inc(s["w_hi"].sem, 1)
                nc.vector.tensor_copy(wdp[:, q, 0], wd[:, q]).then_inc(s["w_hi"].sem, 1)

            def hidden(at):
                e, q, i, c = at
                for t in range(FT):
                    h = (e * B + c) * FT + t
                    tile = (c * FT + t) % 4
                    if gated:
                        dve.wait_ge(s["up"].sem, s["up"].at((h + 1) * NU))
                        dve.wait_ge(s["silu"].sem, s["silu"].at(h + 1))
                        dve.wait_ge(s["lo"].sem, s["lo"].at(h - 3))
                        dve.wait_ge(s["hi"].sem, s["hi"].at(h - 3))
                        nc.vector.tensor_tensor(full[:, tile], silu[:, (c * FT + t) % 2],
                                                up_ps[:, ((c * FT + t) * NU + 1) % 4], ALU.mult
                                                ).then_inc(s["full"].sem, 1)
                for t in range(FT):
                    h = (e * B + c) * FT + t
                    tile = (c * FT + t) % 4
                    dve.wait_ge(s["hi"].sem, s["hi"].at(h + 1))
                    nc.vector.tensor_tensor(hid[:, c % 2, 1, t], full[:, tile], f32(hid[:, c % 2, 0, t]),
                                            ALU.subtract).then_inc(s["lo"].sem, 1)

            split_weights(0, 0, 0)
            router.vector(dve)

            def step(e, q, i):
                for c in range(B):
                    if after := following(e, q, i, c):
                        hidden(after)
                    if c == 1 and (after := following(e, q, i, B - 1)):
                        split_weights(*after[:3])
                    m = e * B + c
                    if c == 0:
                        dve.wait_ge(s[f"comb{q}"].sem, s[f"comb{q}"].at(16 * (i + 1)))
                    dve.wait_ge(s["down"].sem, s["down"].at(m + 1))
                    dve.wait_ge(s["added"].sem, s["added"].at(m - 1))
                    nc.vector.tensor_tensor(wtd[:, c % 2], cb[:, q, cols(c)], dn_ps[:, c % 2], ALU.mult
                                            ).then_inc(s["weighted"].sem, 1)

            for c in range(B):
                if b2_name:
                    dve.wait_ge(s["mm"].sem, s["mm"].at(c + 1))
                    nc.vector.tensor_copy(acc[:, c], spare[c]).then_inc(s["first"].sem, 1)
                else:
                    nc.vector.memset(acc[:, c], 0.0).then_inc(s["first"].sem, 1)
            hidden((0, 0, 0, 0))
            experts(dve, step)
            dve.wait_ge(s["added"].sem, s["added"].at(B * n_experts))
            for c in range(B):
                nc.vector.scalar_tensor_tensor(g.xT[:, cols(c)], acc[:, c], g.mod[:, layer, GATE_B, c:c + 1],
                                               g.xT[:, cols(c)], ALU.mult, ALU.add).then_inc(s["vec"].sem, 1)

        @block.gpsimd
        def _(pool):
            def split_weights(e, q, i):
                pool.wait_ge(s["w_hi"].sem, s["w_hi"].at(2 * (e + 1)))
                nc.gpsimd.tensor_tensor(wup[:, q, 1], wu[:, q], f32(wup[:, q, 0]), ALU.subtract
                                        ).then_inc(s["w_lo"].sem, 1)
                nc.gpsimd.tensor_tensor(wdp[:, q, 1], wd[:, q], f32(wdp[:, q, 0]), ALU.subtract
                                        ).then_inc(s["w_split"].sem, 1)

            split_weights(0, 0, 0)
            pool.wait_ge(s["first"].sem, s["first"].at(B))

            def step(e, q, i):
                for c in range(B):
                    if c == 2 and (after := following(e, q, i, B - 1)):
                        split_weights(*after[:3])
                    m = e * B + c
                    pool.wait_ge(s["weighted"].sem, s["weighted"].at(m + 1))
                    pool.wait_ge(s["added"].sem, s["added"].at(m - 3))
                    nc.gpsimd.tensor_tensor(acc[:, c], acc[:, c], wtd[:, c % 2], ALU.add
                                            ).then_inc(s["added"].sem, 1)

            experts(pool, step)

    if b2_name:
        s["dma"].end(16)
        s["mm"].end(B)
    router.end()
    for name in ("first", "vec", "max_hi", "split"):
        s[name].end(B)
    s["up"].end(B * FT * NU * n_experts)
    for name in ("full", "hi", "lo") + (("silu",) if gated else ()):
        s[name].end(B * FT * n_experts)
    for name in ("down", "weighted", "added"):
        s[name].end(B * n_experts)
    s["w_hi"].end(2 * n_experts)
    s["w_lo"].end(n_experts)
    s["w_split"].end(n_experts)
    for q in range(2):
        s[f"load{q}"].end(w_load * ((n_experts + 1 - q) // 2))
        s[f"comb{q}"].end(16 * ((n_experts + 1 - q) // 2))
        if b1_name:
            s[f"bias{q}"].end(16 * ((n_experts + 1 - q) // 2))


def linear_chain_phase(nc, g):
    s = g.s
    with g.sb("chain", [P, 3, B, T], F32) as mid, \
         g.pb("chain_ps", [P, 2, B, T], F32) as ps, \
         nc.Block() as block:

        @block.tensor
        def _(pe):
            for k, w in enumerate(("L2_f0", "L2_f1", "L2_f2")):
                for c in range(B):
                    if k:
                        pe.wait_ge(s["evac"].sem, s["evac"].at(B * (k - 1) + c + 1))
                    nc.tensor.matmul(ps[:, k % 2, c], g.square(w), g.hT[:, cols(c)] if k == 0 else mid[:, k - 1, c],
                                     start=True, stop=True).then_inc(s["mm"].sem, 1)

        @block.scalar
        def _(act):
            for k in range(3):
                for c in range(B):
                    act.wait_ge(s["mm"].sem, s["mm"].at(B * k + c + 1))
                    if k < 2:
                        nc.scalar.activation(mid[:, k, c], ps[:, k % 2, c], ACT.Copy).then_inc(s["evac"].sem, 1)
                    else:
                        nc.scalar.activation(mid[:, k, c], ps[:, k % 2, c], ACT.Tanh, bias=g.col("L2_bias")
                                             ).then_inc(s["act"].sem, 1)

        @block.vector
        def _(dve):
            for c in range(B):
                dve.wait_ge(s["act"].sem, s["act"].at(c + 1))
                nc.vector.scalar_tensor_tensor(g.xT[:, cols(c)], mid[:, 2, c], g.mod[:, 2, GATE_B, c:c + 1],
                                               g.xT[:, cols(c)], ALU.mult, ALU.add).then_inc(s["vec"].sem, 1)

    s["mm"].end(3 * B)
    s["evac"].end(2 * B)
    s["act"].end(B)
    s["vec"].end(B)


def head_rms_phase(nc, g):
    s = g.s
    heads, d = 16, 8
    src = by_part(g.att_tok, 2)
    with g.sb("sq", [P, N], F32) as sq, \
         g.sb("ms", [P, N // d], F32) as ms, \
         g.sb("ordered", [P, N], F32) as ordered, \
         nc.Block() as block:

        @block.scalar
        def _(act):
            nc.scalar.activation(sq[:], g.att_tok[:], ACT.Square).then_inc(s["act"].sem, 1)
            act.wait_ge(s["vec"].sem, s["vec"].at(1))
            nc.scalar.activation(ms[:], ms[:], ACT.Sqrt, bias=g.eps[:, 0:1], scale=1.0 / d).then_inc(s["act"].sem, 1)

        @block.vector
        def _(dve):
            dve.wait_ge(s["act"].sem, s["act"].at(1))
            nc.vector.tensor_reduce(ms[:], sq[:].rearrange("p (h d) -> p h d", d=d), X, ALU.add
                                    ).then_inc(s["vec"].sem, 1)
            nc.vector.tensor_scalar(g.wo2[:], g.square("L2_Wo"), g.rms_w[:], None, ALU.mult
                                    ).then_inc(s["vec"].sem, 1)
            dve.wait_ge(s["act"].sem, s["act"].at(2))
            nc.vector.reciprocal(ms[:], ms[:]).then_inc(s["vec"].sem, 1)
            dve.wait_ge(s["vec"].sem, s["vec"].at(3))
            nc.vector.tensor_tensor(ordered[:].rearrange("p (h d) -> p h d", d=d),
                                    g.att_tok[:].rearrange("p (h d) -> p h d", d=d),
                                    ms[:].unsqueeze(2).broadcast_to([P, N // d, d]), ALU.mult
                                    ).then_inc(s["vec"].sem, 1)
            dve.wait_ge(s["vec"].sem, s["vec"].at(4))
            w = P // 2
            back = g.att_tok[:].rearrange("p (b t i w) -> p b i t w", b=B, i=2, w=w)
            o = ordered[:].rearrange("p (b i t w) -> p b i t w", b=B, i=2, w=w)
            for b in range(B):
                nc.vector.tensor_copy(back[:, b], o[:, b]).then_inc(s["vec"].sem, 1)

    s["act"].end(2)
    s["vec"].end(4 + B)


def alibi_attention(nc, g):
    s = g.s
    HEADS, HD = 16, 64
    NU = HEADS * B
    BODY = 8
    KT = T // P
    ALIBI_ROW = 64
    OUT = HD + 1
    with g.sb("w_head", [P, 2, 5, HD], F32) as wh, \
         g.sb("qa", [P, 4, T], F32R) as qa, \
         g.sb("qb", [P, 4, T], F32R) as qb, \
         g.sb("ka", [P, 4, T], F32R) as ka, \
         g.sb("kb", [P, 4, T], F32R) as kb, \
         g.sb("v_one", [P, 4, KT, OUT], F32) as vo, \
         g.sb("probs", [P, 2, KT, T], F32) as probs, \
         g.sb("neg_max", [P, 2, KT], F32) as neg_max, \
         g.sb("max_parts", [KT, 2, 2, P], F32) as max_parts, \
         g.sb("recip", [P, KT], F32) as recip, \
         g.sb("mask", [P, 3, P], BF16) as mask, \
         g.pb("proj", [P, 2, T], F32) as pj, \
         g.pb("scores", [P, 2, T], F32) as sc_ps, \
         g.pb("scoresT", [P, 2, T], F32) as st_ps, \
         g.pb("values", [P, T], F32) as o_ps, \
         g.pb("maxT", [P, T], F32) as mt_ps, \
         nc.Block() as block:
        f32 = lambda ap: ap.bitcast(F32)
        identity, above, below = mask[:, 0], mask[:, 1], mask[:, 2]

        def unit(i, p, d=0):
            i, p = i + (p + d) // BODY, (p + d) % BODY
            if isinstance(i, int) and not 0 <= BODY * i + p < NU:
                return None
            return i, p, i * BODY + p

        def steps(eng, step):
            for i in (-1, 0):
                for p in range(BODY):
                    step(i, p)
            with eng.Fori(1, NU // BODY - 1) as i:
                for p in range(BODY):
                    step(i, p)
            for i in (NU // BODY - 1, NU // BODY):
                for p in range(BODY):
                    step(i, p)

        @block.sync
        def _(sp):
            sp.dma_start(mask[:], g.dram["mask"]).then_inc(s["dma"].sem, 16)

            def step(i, p):
                if (at := unit(i, p, 4)) and at[1] % 4 == 0:
                    gi, gp, n = at
                    q = gp // 4
                    sp.wait_ge(s["mm"].sem, s["mm"].at(3 * (n - 4)))
                    sp.dma_start(wh[:, q], g.dram["L1_wqkv"][bass.ds(gi * 2 + q, 1)]
                                 .rearrange("o p c d -> (o p) c d")).then_inc(s[f"load{q}"].sem, 16)
                if at := unit(i, p, 3):
                    gi, gp, n = at
                    sp.wait_ge(s["zeros"].sem, s["zeros"].at(5))
                    sp.wait_ge(s["st"].sem, s["st"].at(KT * (n - 3)))
                    sp.dma_start(f32(kb[ALIBI_ROW:ALIBI_ROW + 2, gp % 4]),
                                 g.scratch["alibi"][bass.ds(gi * 2 + gp // 4, 1)].rearrange("o r t -> (o r) t")
                                 ).then_inc(s[f"alibi{gp % 4}"].sem, 16)
                if at := unit(i, p, 1):
                    gi, gp, n = at
                    sp.wait_ge(s["max_split"].sem, s["max_split"].at(n + 1))
                    for r in range(2):
                        row = slice(MAX_ROW + r, MAX_ROW + r + 1)
                        sp.dma_start(f32(qb[row, gp % 4]).rearrange("o (t q) -> o t q", t=KT),
                                     max_parts[:, gp % 2, r]).then_inc(s[f"rows{gp % 2}"].sem, 16)

            steps(sp, step)

        @block.gpsimd
        def _(pool):
            nc.gpsimd.memset(vo[:], 1.0).then_inc(s["ones"].sem, 1)

            def step(i, p):
                if at := unit(i, p, 3):
                    _, gp, n = at
                    pool.wait_ge(s["hi"].sem, s["hi"].at(2 * n + 2))
                    pool.wait_ge(s["st"].sem, s["st"].at(KT * (n - 3)))
                    pool.wait_ge(s["zeros"].sem, s["zeros"].at(5))
                    nc.gpsimd.tensor_tensor(kb[0:HD, gp % 4], f32(ka[0:HD, gp % 4]),
                                            g.all_ones[0:HD, 0:1].broadcast_to([HD, T]), ALU.mult).then_inc(s["kb"].sem, 1)

            steps(pool, step)

        @block.scalar
        def _(act):
            def step(i, p):
                cur, new = unit(i, p), unit(i, p, 3)
                for kt in range(KT):
                    if cur:
                        _, gp, n = cur
                        if kt == 0:
                            act.wait_ge(s["pv"].sem, s["pv"].at(n - 1))
                        act.wait_ge(s["st"].sem, s["st"].at(KT * n + kt + 1))
                        nc.scalar.activation(probs[:, gp % 2, kt, kt * P:T], st_ps[:, kt % 2, kt * P:T],
                                             ACT.Exp, scale=HD ** -0.5).then_inc(s["exp"].sem, 1)
                    if new:
                        _, gp, n = new
                        b = gp % 4
                        if kt == 0:
                            act.wait_ge(s["st"].sem, s["st"].at(KT * (n - 3)))
                            act.wait_ge(s["mm"].sem, s["mm"].at(3 * n + 1))
                            nc.scalar.activation(qa[:, b], pj[:, (3 * gp) % 2], ACT.Copy).then_inc(s["hi"].sem, 1)
                        elif kt == 1:
                            act.wait_ge(s["mm"].sem, s["mm"].at(3 * n + 2))
                            nc.scalar.activation(ka[:, b], pj[:, (3 * gp + 1) % 2], ACT.Copy
                                                 ).then_inc(s["hi"].sem, 1)
                        elif kt == 3:
                            act.wait_ge(s["mm"].sem, s["mm"].at(3 * n + 3))
                            act.wait_ge(s["ones"].sem, s["ones"].at(1))
                            act.wait_ge(s["pv"].sem, s["pv"].at(n - 3))
                            nc.scalar.activation(vo[:, b, :, 0:HD], pj[:, (3 * gp + 2) % 2, 0:KT * HD]
                                                 .rearrange("p (t d) -> p t d", d=HD), ACT.Copy
                                                 ).then_inc(s["vg"].sem, 1)

            steps(act, step)

        @block.vector
        def _(dve):
            nc.vector.memset(f32(qb[HD:P]), 0.0).then_inc(s["zeros"].sem, 1)
            nc.vector.memset(f32(kb[HD:P]), 0.0).then_inc(s["zeros"].sem, 1)
            dve.wait_ge(s["zeros"].sem, s["zeros"].at(2))
            nc.vector.memset(f32(qb[ALIBI_ROW:ALIBI_ROW + 2]), 1.0).then_inc(s["zeros"].sem, 1)
            nc.vector.memset(f32(kb[MAX_ROW:MAX_ROW + 2]), 1.0).then_inc(s["zeros"].sem, 1)
            nc.vector.memset(f32(neg_max[:]), 0.0).then_inc(s["zeros"].sem, 1)

            def step(i, p):
                ahead, next_, new, last = unit(i, p, 2), unit(i, p, 1), unit(i, p, 3), unit(i, p, -2)
                if last:
                    gi, gp, n = last
                    o = o_ps[:, 0:KT * OUT].rearrange("p (t d) -> p t d", d=OUT)
                    dve.wait_ge(s["pv"].sem, s["pv"].at(n + 1))
                    nc.vector.reciprocal(recip[:], o[:, :, HD]).then_inc(s["recip"].sem, 1)
                    dve.wait_ge(s["recip"].sem, s["recip"].at(n + 1))
                    out = g.att1[:, (gp % 4) * KT:(gp % 4) * KT + KT, bass.ds((gi * 2 + gp // 4) * HD, HD)]
                    nc.vector.tensor_tensor(out, o[:, :, 0:HD], recip[:].unsqueeze(2).broadcast_to([P, KT, HD]),
                                            ALU.mult).then_inc(s["divide"].sem, 1)
                for qt in range(KT):
                    if ahead:
                        _, gp, n = ahead
                        if qt == 0:
                            dve.wait_ge(s["maxT"].sem, s["maxT"].at(n - 1))
                        dve.wait_ge(s["scores"].sem, s["scores"].at(KT * n + qt + 1))
                        nc.vector.tensor_reduce(neg_max[:, gp % 2, qt:qt + 1], sc_ps[:, qt % 2, 0:(qt + 1) * P],
                                                X, ALU.max, negate=True).then_inc(s["max"].sem, 1)
                    if qt == 0 and next_:
                        gi, gp, n = next_
                        dve.wait_ge(s["maxT"].sem, s["maxT"].at(n + 1))
                        dve.wait_ge(s[f"rows{gp % 2}"].sem, s[f"rows{gp % 2}"].at(gi * 128 + 32 * (gp // 2)))
                        nc.vector.tensor_copy(max_parts[:, gp % 2, 0].bitcast(F32R), mt_ps[0:KT, 0:P]
                                              ).then_inc(s["max_hi"].sem, 1)
                        dve.wait_ge(s["max_hi"].sem, s["max_hi"].at(n + 1))
                        nc.vector.tensor_tensor(max_parts[:, gp % 2, 1], mt_ps[0:KT, 0:P],
                                                max_parts[:, gp % 2, 0], ALU.subtract
                                                ).then_inc(s["max_split"].sem, 1)
                    if new and qt in (0, 1):
                        _, gp, n = new
                        b = gp % 4
                        dve.wait_ge(s["hi"].sem, s["hi"].at(2 * n + qt + 1))
                        if qt == 0:
                            nc.vector.tensor_tensor(qb[0:HD, b], pj[0:HD, (3 * gp) % 2], f32(qa[0:HD, b]),
                                                    ALU.subtract).then_inc(s["lo"].sem, 1)
                        else:
                            nc.vector.tensor_tensor(ka[HD:P, b], pj[HD:P, (3 * gp + 1) % 2], f32(ka[HD:P, b]),
                                                    ALU.subtract).then_inc(s["lo"].sem, 1)

            steps(dve, step)

        @block.tensor
        def _(pe):
            def project(at, c):
                gi, gp, n = at
                b, q = gp % 4, gp // 4
                if c == 0:
                    pe.wait_ge(s[f"load{q}"].sem, s[f"load{q}"].at(gi * 16 + 16))
                    pe.wait_ge(s["lo"].sem, s["lo"].at(2 * n))
                if c == 1:
                    pe.wait_ge(s["vg"].sem, s["vg"].at(n))
                if c == 2:
                    pe.wait_ge(s["lo"].sem, s["lo"].at(2 * n + 1))
                if c < 2:
                    nc.tensor.matmul(pj[:, (3 * gp + c) % 2],
                                     wh[:, q, 2 * c:2 * c + 2].rearrange("p c d -> p (c d)"), g.hT[:, cols(b)],
                                     start=True, stop=True).then_inc(s["mm"].sem, 1)
                else:
                    for t in range(KT):
                        at_ = b * T + t * P
                        mm = nc.tensor.matmul(pj[:, (3 * gp + 2) % 2, t * HD:(t + 1) * HD], g.hT[:, at_:at_ + P],
                                              wh[:, q, 4], start=True, stop=True)
                    mm.then_inc(s["mm"].sem, 1)

            def scores(at, qt):
                gi, gp, n = at
                b, w = gp % 4, (qt + 1) * P
                tile, row = slice(qt * P, w), slice(0, MAX_ROW)
                pe.wait_ge(s["max"].sem, s["max"].at(KT * n + qt - 1))
                nc.tensor.matmul(sc_ps[:, qt % 2, 0:w], qa[:, b, tile], ka[:, b, 0:w], start=True, stop=False)
                nc.tensor.matmul(sc_ps[:, qt % 2, 0:w], qb[row, b, tile], kb[row, b, 0:w], start=False, stop=False)
                nc.tensor.matmul(sc_ps[:, qt % 2, tile], identity, above, start=False, stop=True
                                 ).then_inc(s["scores"].sem, 1)

            def scores_t(at, kt):
                gi, gp, n = at
                b, tile, right = gp % 4, slice(kt * P, (kt + 1) * P), slice(kt * P, T)
                pe.wait_ge(s["exp"].sem, s["exp"].at(KT * n + kt - 1))
                nc.tensor.matmul(st_ps[:, kt % 2, right], ka[:, b, tile], qa[:, b, right], start=True, stop=False)
                nc.tensor.matmul(st_ps[:, kt % 2, right], kb[:, b, tile], qb[:, b, right], start=False, stop=False)
                nc.tensor.matmul(st_ps[:, kt % 2, tile], identity, below, start=False, stop=True
                                 ).then_inc(s["st"].sem, 1)

            def values(at, qt):
                gi, gp, n = at
                if qt == 0:
                    pe.wait_ge(s["divide"].sem, s["divide"].at(n))
                    pe.wait_ge(s["exp"].sem, s["exp"].at(KT * (n + 1)))
                for kt in range(qt + 1):
                    mm = nc.tensor.matmul(o_ps[:, qt * OUT:(qt + 1) * OUT],
                                          probs[:, gp % 2, kt, qt * P:(qt + 1) * P], vo[:, gp % 4, kt],
                                          start=kt == 0, stop=kt == qt)
                if qt == KT - 1:
                    mm.then_inc(s["pv"].sem, 1)

            pe.wait_ge(s["dma"].sem, s["dma"].at(16))

            def step(i, p):
                cur, ahead, next_ = unit(i, p), unit(i, p, 2), unit(i, p, 1)
                new, before = unit(i, p, 3), unit(i, p, -1)
                if cur:
                    gi, gp, n = cur
                    pe.wait_ge(s[f"rows{gp % 2}"].sem, s[f"rows{gp % 2}"].at(gi * 128 + 32 * (gp // 2) + 32))
                if ahead:
                    gi, gp, n = ahead
                    pe.wait_ge(s["kb"].sem, s["kb"].at(n + 1))
                    pe.wait_ge(s["lo"].sem, s["lo"].at(2 * n + 2))
                    pe.wait_ge(s[f"alibi{gp % 4}"].sem, s[f"alibi{gp % 4}"].at(gi * 32 + 16 * (gp // 4) + 16))
                for k in range(KT):
                    if cur:
                        scores_t(cur, k)
                    if ahead:
                        scores(ahead, k)
                    if k > 0 and before:
                        if k == 1:
                            values(before, 0)
                        values(before, k)
                    if k == 0 and next_:
                        gi, gp, n = next_
                        pe.wait_ge(s["max"].sem, s["max"].at(KT * (n + 1)))
                        pe.wait_ge(s["max_split"].sem, s["max_split"].at(n))
                        nc.tensor.transpose(mt_ps[0:KT, 0:P], neg_max[:, gp % 2], g.identity
                                            ).then_inc(s["maxT"].sem, 1)
                    if new and k != 2:
                        project(new, min(k, 2))

            steps(pe, step)

    s["dma"].end(16)
    s["mm"].end(3 * NU)
    for q in range(2):
        s[f"load{q}"].end(16 * HEADS // 2)
        s[f"rows{q}"].end(32 * NU // 2)
    for b in range(B):
        s[f"alibi{b}"].end(16 * HEADS)
    s["zeros"].end(5)
    s["ones"].end(1)
    s["hi"].end(2 * NU)
    s["lo"].end(2 * NU)
    for name in ("kb", "vg", "pv", "maxT", "max_hi", "max_split", "recip", "divide"):
        s[name].end(NU)
    for name in ("scores", "st", "max", "exp"):
        s[name].end(KT * NU)


def alibi_output(nc, g):
    s = g.s
    KD = 8
    with g.sb("w_out", [P, KD, P], F32) as wo, \
         g.sb("attn", [P, 4, T], F32) as attn, \
         g.sb("update", [P, B, T], F32) as upd, \
         g.pb("turn_ps", [P, 4, T], F32) as turn_ps, \
         g.pb("out_ps", [P, B, T], F32) as ps, \
         nc.Block() as block:
        tiles = [(b, k) for b in range(B) for k in range(KD)]

        @block.sync
        def _(sp):
            sp.dma_start(wo[:], g.dram["L1_wout"]).then_inc(s["dma"].sem, 16)

        @block.tensor
        def _(pe):
            def turn(n):
                b, k = tiles[n]
                if n >= 4:
                    pe.wait_ge(s["evac"].sem, s["evac"].at(n - 3))
                for t in range(T // P):
                    mm = nc.tensor.transpose(turn_ps[:, n % 4, t * P:(t + 1) * P],
                                             g.att1[:, b * (T // P) + t, k * P:(k + 1) * P], g.identity)
                mm.then_inc(s["rawT"].sem, 1)

            pe.wait_ge(s["dma"].sem, s["dma"].at(16))
            turn(0)
            turn(1)
            for n, (b, k) in enumerate(tiles):
                if n + 2 < len(tiles):
                    turn(n + 2)
                pe.wait_ge(s["evac"].sem, s["evac"].at(n + 1))
                nc.tensor.matmul(ps[:, b], wo[:, k], attn[:, n % 4], start=k == 0, stop=k == KD - 1
                                 ).then_inc(s["mm"].sem, 1)

        @block.scalar
        def _(act):
            for n in range(len(tiles)):
                act.wait_ge(s["rawT"].sem, s["rawT"].at(n + 1))
                act.wait_ge(s["mm"].sem, s["mm"].at(n - 3))
                nc.scalar.activation(attn[:, n % 4], turn_ps[:, n % 4], ACT.Copy).then_inc(s["evac"].sem, 1)
            for b in range(B):
                act.wait_ge(s["mm"].sem, s["mm"].at(KD * (b + 1)))
                nc.scalar.activation(upd[:, b], ps[:, b], ACT.Identity, bias=g.gate_bias[:, 1, b:b + 1],
                                     scale=g.mod[:, 1, GATE_A, b:b + 1]).then_inc(s["act"].sem, 1)

        @block.vector
        def _(dve):
            for b in range(B):
                dve.wait_ge(s["act"].sem, s["act"].at(b + 1))
                nc.vector.tensor_tensor(g.xT[:, cols(b)], g.xT[:, cols(b)], upd[:, b], ALU.add
                                        ).then_inc(s["vec"].sem, 1)

    s["dma"].end(16)
    for name in ("rawT", "evac", "mm"):
        s[name].end(B * KD)
    s["act"].end(B)
    s["vec"].end(B)


def linear_attention(nc, g):
    s = g.s
    HG, KT = 4, T // P
    OUT = 9
    with g.sb("head_proj", [P, 4 * P], F32) as pm, \
         g.sb("q_k", [P, 2, 2, T], F32) as qk, \
         g.sb("v_one", [P, 2, KT, 16, OUT], F32) as vo, \
         g.sb("expd", [P, 4, T], F32) as ex, \
         g.sb("features", [P, 16, T], F32) as feat, \
         g.sb("kv", [P, 2, HG, 4, OUT], F32) as kv, \
         g.sb("kv_mask", [P, 4, OUT], F32) as kv_mask, \
         g.sb("recip", [P, 2, KT, 16], F32) as recip, \
         g.pb("proj", [P, T], F32) as pj, \
         g.pb("feat_ps", [P, 4, T], F32) as f_ps, \
         g.pb("kv_ps", [P, HG, P], F32) as kv_ps, \
         g.pb("out_ps", [P, KT, 2 * P], F32) as o_ps, \
         nc.Block() as block:
        F = 2 * 4

        @block.sync
        def _(sp):
            sp.dma_start(pm[:], g.dram["L3_proj"]).then_inc(s["dma"].sem, 16)
            sp.dma_start(kv_mask[:], g.dram["kv_mask"]).then_inc(s["dma"].sem, 16)

        @block.tensor
        def _(pe):
            pe.wait_ge(s["dma"].sem, s["dma"].at(32))

            def project(b, c):
                pe.wait_ge(s["evac"].sem, s["evac"].at(3 * b + c))
                if c < 2:
                    nc.tensor.matmul(pj[:], g.square(("L3_Wq", "L3_Wk")[c]), g.hT[:, cols(b)],
                                     start=True, stop=True).then_inc(s["mm"].sem, 1)
                else:
                    for t in range(KT):
                        at = b * T + t * P
                        mm = nc.tensor.matmul(pj[:, t * P:(t + 1) * P], g.hT[:, at:at + P], g.square("L3_Wv"),
                                              start=True, stop=True)
                    mm.then_inc(s["mm"].sem, 1)

            for c in range(3):
                project(0, c)
            for b in range(B + 1):
                for f in range(F):
                    if b < B:
                        n = F * b + f
                        if f == 0:
                            pe.wait_ge(s["evac"].sem, s["evac"].at(3 * (b + 1)))
                        pe.wait_ge(s["feat"].sem, s["feat"].at(n - 3))
                        if f < 4:
                            nc.tensor.matmul(f_ps[:, n % 4], pm[:, f * P:(f + 1) * P], qk[:, b % 2, 0],
                                             start=True, stop=True).then_inc(s["up"].sem, 1)
                        else:
                            nc.tensor.matmul(f_ps[:, n % 4], qk[:, b % 2, 1, (f - 4) * P:(f - 3) * P], pm[:],
                                             start=True, stop=True).then_inc(s["up"].sem, 1)
                    if b > 0 and f < HG:
                        hg = f
                        pe.wait_ge(s["feat"].sem, s["feat"].at(F * b))
                        pe.wait_ge(s["kb"].sem, s["kb"].at(b - 1))
                        for t in range(KT):
                            mm = nc.tensor.matmul(
                                kv_ps[:, hg, 0:4 * OUT], feat[:, 8 * ((b - 1) % 2) + 4 + t, hg * P:(hg + 1) * P],
                                vo[:, (b - 1) % 2, t, 4 * hg:4 * hg + 4].rearrange("p j d -> p (j d)"),
                                start=t == 0, stop=t == KT - 1)
                        if hg == HG - 1:
                            mm.then_inc(s["pv"].sem, 1)
                    elif b > 0:
                        t = f - HG
                        pe.wait_ge(s["kb"].sem, s["kb"].at(b))
                        pe.wait_ge(s["divide"].sem, s["divide"].at(b - 1))
                        for hg in range(HG):
                            mm = nc.tensor.matmul(
                                o_ps[:, t, hg * 4 * OUT:(hg + 1) * 4 * OUT],
                                feat[:, 8 * ((b - 1) % 2) + hg, t * P:(t + 1) * P],
                                kv[:, (b - 1) % 2, hg].rearrange("p j d -> p (j d)"), start=True, stop=True)
                        if t == KT - 1:
                            mm.then_inc(s["down"].sem, 1)
                    if b + 1 < B and f in (2, 4, 6):
                        project(b + 1, f // 2 - 1)

        @block.scalar
        def _(act):
            def evacuate(b, c):
                act.wait_ge(s["mm"].sem, s["mm"].at(3 * b + c + 1))
                if c < 2:
                    act.wait_ge(s["up"].sem, s["up"].at(F * (b - 1)))
                    nc.scalar.activation(qk[:, b % 2, c], pj[:], ACT.Copy).then_inc(s["evac"].sem, 1)
                else:
                    act.wait_ge(s["ones"].sem, s["ones"].at(1))
                    act.wait_ge(s["pv"].sem, s["pv"].at(b - 1))
                    nc.scalar.activation(vo[:, b % 2, :, :, 0:8],
                                         pj[:].rearrange("p (t h d) -> p t h d", h=16, d=8), ACT.Copy
                                         ).then_inc(s["evac"].sem, 1)

            for c in range(3):
                evacuate(0, c)
            for b in range(B):
                for f in range(F):
                    n = F * b + f
                    act.wait_ge(s["clip"].sem, s["clip"].at(n + 1))
                    nc.scalar.activation(ex[:, n % 4], ex[:, n % 4], ACT.Exp).then_inc(s["exp"].sem, 1)
                    if b + 1 < B and f in (2, 4, 6):
                        evacuate(b + 1, f // 2 - 1)

        @block.gpsimd
        def _(pool):
            nc.gpsimd.memset(vo[:], 1.0).then_inc(s["ones"].sem, 1)

        @block.vector
        def _(dve):
            dve.wait_ge(s["dma"].sem, s["dma"].at(32))
            def mask(b):
                dve.wait_ge(s["pv"].sem, s["pv"].at(b + 1))
                nc.vector.tensor_tensor(kv[:, b % 2], kv_mask[:].unsqueeze(1).broadcast_to([P, HG, 4, OUT]),
                                        kv_ps[:, :, 0:4 * OUT].rearrange("p g (j d) -> p g j d", d=OUT),
                                        ALU.mult).then_inc(s["kb"].sem, 1)

            def divide(b):
                o = o_ps[:, :, 0:16 * OUT].rearrange("p t (h d) -> p t h d", d=OUT)
                dve.wait_ge(s["down"].sem, s["down"].at(b + 1))
                nc.vector.tensor_scalar(recip[:, 0], o[:, :, :, 8], 1e-8, None, ALU.add
                                        ).then_inc(s["recip"].sem, 1)
                dve.wait_ge(s["recip"].sem, s["recip"].at(2 * b + 1))
                nc.vector.reciprocal(recip[:, 1], recip[:, 0]).then_inc(s["recip"].sem, 1)
                dve.wait_ge(s["recip"].sem, s["recip"].at(2 * b + 2))
                for t in range(KT):
                    done = s["divide"] if t == KT - 1 else s["vec"]
                    nc.vector.tensor_tensor(
                        g.att_tok[:].rearrange("p (n h d) -> p n h d", h=16, d=8)[:, b * KT + t],
                        o[:, t, :, 0:8], recip[:, 1, t].unsqueeze(2).broadcast_to([P, 16, 8]), ALU.mult
                    ).then_inc(done.sem, 1)

            for b in range(B + 1):
                for f in range(F + 1):
                    n = F * b + f
                    if f < F and b < B:
                        dve.wait_ge(s["up"].sem, s["up"].at(n + 1))
                        dve.wait_ge(s["feat"].sem, s["feat"].at(n - 3))
                        nc.vector.tensor_scalar(ex[:, n % 4], f_ps[:, n % 4], 0.0, None, ALU.min
                                                ).then_inc(s["clip"].sem, 1)
                    if f and b < B:
                        dve.wait_ge(s["exp"].sem, s["exp"].at(n))
                        dve.wait_ge(s["down"].sem, s["down"].at(b - 1))
                        nc.vector.scalar_tensor_tensor(feat[:, 8 * (b % 2) + f - 1], f_ps[:, (n - 1) % 4], 0.0,
                                                       ex[:, (n - 1) % 4], ALU.max, ALU.add
                                                       ).then_inc(s["feat"].sem, 1)
                    if b > 0 and f == HG:
                        mask(b - 1)
                if b > 0:
                    divide(b - 1)

    s["dma"].end(32)
    s["mm"].end(3 * B)
    s["evac"].end(3 * B)
    for name in ("up", "exp", "clip", "feat"):
        s[name].end(F * B)
    for name in ("kb", "pv", "down", "divide"):
        s[name].end(B)
    s["recip"].end(2 * B)
    s["vec"].end(3 * B)
    s["ones"].end(1)


def residual_output(nc, g):
    s = g.s
    att = g.att_tok[:].rearrange("p (n d) -> p n d", d=P)
    with g.sb("attn", [P, B, T], F32) as attn, \
         g.pb("turn_ps", [P, B, T], F32) as turn_ps, \
         g.pb("out_ps", [P, B, T], F32) as ps, \
         nc.Block() as block:

        @block.tensor
        def _(pe):
            for b in range(B):
                for t in range(T // P):
                    mm = nc.tensor.transpose(turn_ps[:, b, t * P:(t + 1) * P], att[:, b * (T // P) + t],
                                             g.identity)
                mm.then_inc(s["rawT"].sem, 1)
            for b in range(B):
                pe.wait_ge(s["evac"].sem, s["evac"].at(b + 1))
                nc.tensor.matmul(ps[:, b], g.square("L3_Wo"), attn[:, b], start=True, stop=True
                                 ).then_inc(s["mm"].sem, 1)

        @block.scalar
        def _(act):
            for b in range(B):
                act.wait_ge(s["rawT"].sem, s["rawT"].at(b + 1))
                nc.scalar.activation(attn[:, b], turn_ps[:, b], ACT.Copy).then_inc(s["evac"].sem, 1)

        @block.vector
        def _(dve):
            for b in range(B):
                dve.wait_ge(s["mm"].sem, s["mm"].at(b + 1))
                nc.vector.scalar_tensor_tensor(g.hT[:, cols(b)], ps[:, b], g.col("L3_bo"), g.hT[:, cols(b)],
                                               ALU.add, ALU.add).then_inc(s["vec"].sem, 1)

    for name in ("rawT", "evac", "mm", "vec"):
        s[name].end(B)


def gelu_ffn(nc, g):
    s = g.s
    FT = 4
    with g.sb("w1", [P, 4 * P], F32) as w1, \
         g.sb("w2", [P, FT, P], F32) as w2, \
         g.sb("hidden", [P, 2, FT, T], F32) as hid, \
         g.pb("up_ps", [P, 4, T], F32) as up_ps, \
         g.pb("down_ps", [P, 2, T], F32) as dn_ps, \
         nc.Block() as block:

        @block.sync
        def _(sp):
            sp.dma_start(w1[:], g.dram["L3_w1"]).then_inc(s["dma"].sem, 16)
            sp.dma_start(w2[:], g.dram["L3_w2"]).then_inc(s["dma"].sem, 16)

        @block.tensor
        def _(pe):
            pe.wait_ge(s["dma"].sem, s["dma"].at(32))

            def up(c):
                for t in range(FT):
                    pe.wait_ge(s["hidden"].sem, s["hidden"].at(FT * (c - 1) + t + 1))
                    nc.tensor.matmul(up_ps[:, t], w1[:, t * P:(t + 1) * P], g.hT[:, cols(c)],
                                     start=True, stop=True).then_inc(s["up"].sem, 1)

            up(0)
            for c in range(B):
                if c + 1 < B:
                    up(c + 1)
                pe.wait_ge(s["hidden"].sem, s["hidden"].at(FT * (c + 1)))
                pe.wait_ge(s["vec"].sem, s["vec"].at(c - 1))
                for t in range(FT):
                    mm = nc.tensor.matmul(dn_ps[:, c % 2], w2[:, t], hid[:, c % 2, t], start=t == 0,
                                          stop=t == FT - 1)
                mm.then_inc(s["down"].sem, 1)

        @block.scalar
        def _(act):
            for c in range(B):
                act.wait_ge(s["down"].sem, s["down"].at(c - 1))
                for t in range(FT):
                    act.wait_ge(s["up"].sem, s["up"].at(FT * c + t + 1))
                    nc.scalar.activation(hid[:, c % 2, t], up_ps[:, t], ACT.Gelu, bias=g.col(f"L3_b1_{t}")
                                         ).then_inc(s["hidden"].sem, 1)

        @block.vector
        def _(dve):
            for c in range(B):
                dve.wait_ge(s["down"].sem, s["down"].at(c + 1))
                nc.vector.scalar_tensor_tensor(g.hT[:, cols(c)], dn_ps[:, c % 2], g.col("L3_b2"), g.hT[:, cols(c)],
                                               ALU.add, ALU.add).then_inc(s["vec"].sem, 1)

    s["dma"].end(32)
    s["up"].end(B * FT)
    s["hidden"].end(B * FT)
    s["down"].end(B)
    s["vec"].end(B)


def gated_add(nc, g, layer, gate):
    s = g.s
    with nc.Block() as block:
        @block.vector
        def _(dve):
            for c in range(B):
                nc.vector.scalar_tensor_tensor(g.xT[:, cols(c)], g.hT[:, cols(c)], g.mod[:, layer, gate, c:c + 1],
                                               g.xT[:, cols(c)], ALU.mult, ALU.add).then_inc(s["vec"].sem, 1)
    s["vec"].end(B)


class Program:

    def __init__(self, nc):
        self.nc, self.count = nc, 0

    def sb(self, name, shape, dtype):
        self.count += 1
        return self.nc.sbuf_tensor(f"{name}_{self.count}", shape, dtype)

    def pb(self, name, shape, dtype):
        self.count += 1
        return self.nc.psum_tensor(f"{name}_{self.count}", shape, dtype)


def build(nc, dram, debug=None):
    g = Program(nc)
    g.dram = dram
    names = ["dma", "vec", "act", "pe", "pool", "mean", "square", "var", "centre", "std", "norm", "mm",
             "evac", "split", "store", "scores", "st", "max", "exp", "max_split", "max_hi", "maxT", "raw",
             "rawT", "divide", "pv", "vg", "ones", "zeros"]
    names += [f"load{p}" for p in range(4)] + [f"rows{q}" for q in range(2)]
    names += MORE_SIGNALS
    g.s = {n: Signal(nc, n) for n in names}
    g.scratch = {n: nc.dram_tensor(f"scratch_{n}", shape, F32, kind="Internal").ap() for n, shape in
                 (("q", (B * 16 * 24, T)), ("k", (B * 16 * 24, T)), ("comb", (9, N)),
                  ("alibi", (16, 2, T)))}
    g.xT = nc.alloc_sbuf_tensor("x_keep", [P, N], F32)
    g.hT = nc.alloc_sbuf_tensor("h_keep", [P, N], F32)
    g.squares = nc.alloc_sbuf_tensor("squares_keep", [P, len(SQUARES), P], F32)
    g.columns = nc.alloc_sbuf_tensor("columns_keep", [P, len(COLUMNS)], F32)
    g.consts = nc.alloc_sbuf_tensor("consts_keep", [P, 7 * P + 16], F32)
    g.iota = g.consts[:, 7 * P + 8:7 * P + 16]
    g.gate_w = nc.alloc_sbuf_tensor("gate_w_keep", [P, 3, EXPERTS], F32)
    g.gate_b = nc.alloc_sbuf_tensor("gate_b_keep", [P, 2, EXPERTS], F32)
    g.wo2 = nc.alloc_sbuf_tensor("wo2", [P, P], F32)
    g.v_tok = nc.alloc_sbuf_tensor("v_tok", [P, N], F32)
    g.att_tok = nc.alloc_sbuf_tensor("att_tok", [P, N], F32)
    g.cs = nc.alloc_sbuf_tensor("silu_c", [P, 16], F32)
    g.mod = nc.alloc_sbuf_tensor("mod", [P, 4, 6, B], F32)
    g.gate_bias = nc.alloc_sbuf_tensor("gate_bias", [P, 2, B], F32)
    g.rms_w = nc.alloc_sbuf_tensor("rms_w", [P, 1], F32)
    g.neg_lam = nc.alloc_sbuf_tensor("neg_lam", [P, 1], F32)
    g.eps = nc.alloc_sbuf_tensor("eps", [P, 2], F32)
    const = lambda n: g.consts[:, n * P:(n + 1) * P]
    g.identity, g.mean_w, g.den_sel, g.head_mean, g.tri, g.all_ones, g.before = (
        const(n) for n in range(7))
    g.den_eps = lambda hd: g.consts[:, 7 * P:7 * P + 1] if hd == 8 else g.eps[:, 1:2]
    g.square = lambda name: g.squares[:, SQUARES.index(name)]
    g.col = lambda name: g.columns[:, COLUMNS.index(name):COLUMNS.index(name) + 1]
    g.modcol = lambda layer, j: (lambda c: g.mod[:, layer, j, c:c + 1])

    with nc.Block() as block:
        @block.sync
        def _(sp):
            for signal in g.s.values():
                sp.sem_inc(signal.sem, START)

    def dump(name):
        if debug and name in debug:
            with nc.Block() as block:
                @block.sync
                def _(sp):
                    src = g.hT if name.startswith("h") else g.xT
                    sp.dma_start(debug[name], src[:]).then_inc(g.s["dma"].sem, 16)
                    sp.wait_ge(g.s["dma"].sem, g.s["dma"].at(16))
            g.s["dma"].end(16)

    setup_phase(nc, g)
    norm_phase(nc, g, g.xT, g.modcol(0, SCALE_A), g.modcol(0, SHIFT_A))
    dump("h0")
    q_stack, k_stack, v_group = small_head_stacks(g)
    with q_stack as qs, k_stack as ks, v_group as vg:
        small_head_projections(nc, g, (qs, ks, vg), 8, "L0_Wq", "L0_Wk", "L0_Wv")
        small_head_attention(nc, g, (qs, ks, vg), 8, float(8 ** -0.5))
    attention_output(nc, g, 0, g.square("L0_Wo"), True)
    dump("x0")
    norm_phase(nc, g, g.xT, g.modcol(0, SCALE_B), g.modcol(0, SHIFT_B))
    dump("h1")
    experts_phase(nc, g, 0, "norm", 0, ["L0_w1"], "L0_w2", EXPERTS, 512, False, "L0_b1", "L0_b2")
    dump("x1")

    norm_phase(nc, g, g.xT, g.modcol(1, SCALE_A), g.modcol(1, SHIFT_A))
    dump("h2")
    with g.sb("att1", [P, N // P, 16 * 64], F32) as g.att1:
        alibi_attention(nc, g)
        alibi_output(nc, g)
    dump("x2")
    norm_phase(nc, g, g.xT, g.modcol(1, SCALE_B), g.modcol(1, SHIFT_B))
    experts_phase(nc, g, 1, "open", 1, ["L1_w1", "L1_w3"], "L1_w2", EXPERTS + 1, 256, True)
    dump("x3")

    norm_phase(nc, g, g.xT, g.modcol(2, SCALE_A), g.modcol(2, SHIFT_A))
    dump("h4")
    q_stack, k_stack, v_group = small_head_stacks(g)
    with q_stack as qs, k_stack as ks, v_group as vg:
        small_head_projections(nc, g, (qs, ks, vg), 4, "L2_Wq", "L2_Wk", "L2_Wv", "L2_Wqs", "L2_Wks")
        small_head_attention(nc, g, (qs, ks, vg), 4, 0.5, differential=True)
    head_rms_phase(nc, g)
    attention_output(nc, g, 2, g.wo2[:], False)
    dump("x4")
    norm_phase(nc, g, g.xT, g.modcol(2, SCALE_B), g.modcol(2, SHIFT_B))
    linear_chain_phase(nc, g)
    dump("x5")

    norm_phase(nc, g, g.xT, g.modcol(3, SCALE_A), g.modcol(3, SHIFT_A))
    dump("h6")
    linear_attention(nc, g)
    residual_output(nc, g)
    gamma, beta = (lambda c: g.col("L3_gamma")), (lambda c: g.col("L3_beta"))
    norm_phase(nc, g, g.hT, gamma, beta)
    gelu_ffn(nc, g)
    norm_phase(nc, g, g.hT, gamma, beta)
    gated_add(nc, g, 3, GATE_A)
    dump("x6")
    norm_phase(nc, g, g.xT, g.modcol(3, SCALE_B), g.modcol(3, SHIFT_B))
    dump("h7")
    experts_phase(nc, g, 3, "each", 2, ["L3_gate", "L3_up"], "L3_down", EXPERTS, 256, True)

    with nc.Block() as block:
        @block.sync
        def _(sp):
            sp.dma_start(dram["outT"], g.xT[:]).then_inc(g.s["dma"].sem, 16)
            sp.wait_ge(g.s["dma"].sem, g.s["dma"].at(16))


MORE_SIGNALS = ["logits", "totals", "counts", "route", "bias0", "bias1",
                "log", "full", "w_hi", "w_lo", "w_split", "comb0", "comb1", "chosen", "first", "up", "hidden", "silu", "down", "weighted", "added", "hi", "lo", "kb",
                "recip", "feat", "clip", "alibi0", "alibi1", "alibi2", "alibi3"]


def host_arrays(inp):
    a = {k: np.asarray(v) for k, v in inp.items()}
    t = np.transpose
    out = {"xT": np.ascontiguousarray(a["L0_attn_x"].reshape(N, P).T)}
    out["cT"] = np.ascontiguousarray(np.concatenate([a[f"L{i}_c"] for i in range(4)]).T)
    for i in range(4):
        out[f"L{i}_wmod"] = np.ascontiguousarray(a[f"L{i}_wmod"])
    out["lambdas"] = np.stack([a[f"L2_attn_lambda_{n}"] for n in ("q1", "k1", "q2", "k2")])
    swap = np.arange(P) ^ 1
    qkv3 = np.split(a["L3_attn_w_qkv"], 3)
    squares = [a["L0_attn_Wq"].T, a["L0_attn_Wk"].T, a["L0_attn_Wv"].T, a["L0_attn_Wo"].T,
               a["L2_attn_Wq"].T, a["L2_attn_Wq"][swap].T, a["L2_attn_Wk"].T, a["L2_attn_Wk"][swap].T,
               a["L2_attn_Wv"].T, a["L2_attn_Wo"].T,
               a["L2_ffn_weight"], a["L2_ffn_aux_weight1"], a["L2_ffn_aux_weight2"],
               qkv3[0].T, qkv3[1].T, qkv3[2].T, a["L3_attn_w_out"].T]
    out["squares"] = np.ascontiguousarray(np.stack(squares, axis=1))
    out["columns"] = np.ascontiguousarray(np.stack(
        [a["L0_attn_bo"], a["L1_attn_b_out"], np.tile(a["L2_attn_rms_weight"], 16), a["L2_ffn_bias"],
         a["L3_attn_b_out"], a["L3_attn_gamma"], a["L3_attn_beta"], a["L3_attn_b2"],
         *a["L3_attn_b1"].reshape(4, P)], axis=1))
    i = np.arange(P)
    den_sel = (i[:, None] == 32 * (i[None, :] // 32) + 8)
    head_mean = (i[:, None] // 8 == i[None, :] // 8) / 8
    tri = i[:, None] <= i[None, :]
    before = (i[:, None] // EXPERTS < i[None, :] // EXPERTS) & (i[:, None] % EXPERTS == i[None, :] % EXPERTS)
    den_eps = np.zeros((P, 16))
    den_eps[8::32, 0] = 1e-8
    den_eps[:, 8:16] = np.arange(EXPERTS) - EXPERTS
    out["consts"] = np.concatenate([np.eye(P), np.full((P, P), 1 / P), den_sel, head_mean, tri,
                                    np.ones((P, P)), before, den_eps], axis=1).astype(np.float32)
    angle = (1.0 / 10000.0 ** np.linspace(0.0, 1.0, 2)).astype(np.float32)
    f = np.arange(T, dtype=np.float32)[None, :] * angle[(i % 4) // 2][:, None]
    out["rope"] = np.stack([np.cos(f), np.sin(f) * np.where(i % 2, 1, -1)[:, None]], axis=1).astype(np.float32)
    bf = mybir.dt.np(BF16)
    above = np.where(i[None, :] > i[:, None], -1e30, 0.0)
    out["mask"] = np.stack([np.eye(P), above, above.T], axis=1).astype(bf)
    slope = np.array([(2 ** -0.5) ** (h + 1) for h in range(16)])
    al = (8 * slope[:, None] * np.arange(T)[None, :]).astype(np.float32)
    hi = (al.view(np.uint32) & np.uint32(0xFFFFF000)).view(np.float32)
    out["alibi"] = np.stack([hi, al - hi], axis=1)
    j = np.arange(4)
    out["kv_mask"] = np.broadcast_to((i[:, None] // 32 == j[None, :])[:, :, None], (P, 4, 9)).astype(np.float32)

    c = np.ascontiguousarray
    out["gate_w"] = c(np.stack([a["L0_ffn_gate_w"], a["L1_ffn_gate_w"].T, a["L3_ffn_gate_w"].T], axis=1))
    out["gate_b"] = c(np.stack([a["L0_ffn_gate_b"], a["L1_ffn_gate_bias"]]))
    out["L0_w1"], out["L0_w2"], out["L0_b2"] = a["L0_ffn_w1"], a["L0_ffn_w2"], a["L0_ffn_b2"]
    out["L0_b1"] = c(a["L0_ffn_b1"].reshape(EXPERTS, 4, P).transpose(0, 2, 1))
    wq = a["L1_attn_w_qkv"].reshape(P, 3, 16, 64)
    out["L1_wqkv"] = c(wq.transpose(2, 0, 1, 3)[:, :, [0, 0, 1, 1, 2]])
    out["L1_wout"] = c(a["L1_attn_w_out"].reshape(8, P, P).transpose(1, 0, 2))
    for n in ("w1", "w2", "w3"):
        both = np.concatenate([a[f"L1_ffn_{n}"], a[f"L1_ffn_s{n}"][None]])
        out[f"L1_{n}"] = c(both.transpose(0, 2, 1))
    pm = np.zeros((P, 16, 32), np.float32)
    for h in range(16):
        pm[8 * h:8 * h + 8, h] = a["L3_attn_proj"][h]
    out["L3_proj"] = pm.reshape(P, 512)
    out["L3_w1"] = c(a["L3_attn_w1"].T)
    out["L3_w2"] = c(a["L3_attn_w2"].T.reshape(4, P, P).transpose(1, 0, 2))
    for n, m in (("gate", "gate_proj_w"), ("up", "up_proj_w"), ("down", "down_proj_w")):
        out[f"L3_{n}"] = c(a[f"L3_ffn_{m}"].transpose(0, 2, 1))
    return out


def kernel(**inputs):
    import concourse.bacc as bacc
    from concourse.bass_utils import run_bass_kernel_spmd as run

    arrays = host_arrays(inputs)
    nc = bacc.Bacc("TRN2", target_bir_lowering=False, num_devices=1)
    dram = {k: nc.dram_tensor(f"in_{k}", v.shape, mybir.dt.from_np(v.dtype), kind="ExternalInput").ap()
            for k, v in arrays.items()}
    dram["outT"] = nc.dram_tensor("outT", (P, N), F32, kind="ExternalOutput").ap()
    build(nc, dram)
    r = run(nc, [{f"in_{k}": v for k, v in arrays.items()}], core_ids=[0])
    return np.ascontiguousarray(r.results[0]["outT"].T).reshape(B, T, P)
```

```python
import concourse.bass as bass
from concourse import mybir
import numpy as np

F32 = mybir.dt.float32
F32R = mybir.dt.float32r
BF16 = mybir.dt.bfloat16
ACT = mybir.ActivationFunctionType
ALU = mybir.AluOpType
X = mybir.AxisListType.X

P = 128
B, T = 4, 512
N = B * T
LN_EPS = 1e-5
EXPERTS = 8
CAPACITY = int(1.25 * N / EXPERTS)
LAMBDA_INIT = 0.8 - 0.6 * float(np.exp(-0.3 * 12))
PASSES = ((0, 0), (0, 1), (1, 0))
LATE = 16 * 3
MAX_ROW = 96
START = 64

SQUARES = ["L0_Wq", "L0_Wk", "L0_Wv", "L0_Wo",
           "L2_Wq", "L2_Wqs", "L2_Wk", "L2_Wks", "L2_Wv", "L2_Wo", "L2_f0", "L2_f1", "L2_f2",
           "L3_Wq", "L3_Wk", "L3_Wv", "L3_Wo"]
COLUMNS = ["L0_bo", "L1_bo", "L2_rms", "L2_bias", "L3_bo", "L3_gamma", "L3_beta", "L3_b2",
           "L3_b1_0", "L3_b1_1", "L3_b1_2", "L3_b1_3"]
SHIFT_A, SCALE_A, GATE_A, SHIFT_B, SCALE_B, GATE_B = range(6)


class Signal:

    def __init__(self, nc, name):
        self.sem = nc.alloc_semaphore(name)
        self.base = START

    def at(self, n):
        return n + self.base

    def end(self, n):
        self.base += n


def cols(c):
    return slice(c * T, (c + 1) * T)


class Norm:

    ON_SCALAR = 2

    def __init__(self, nc, g, src, scales, shifts):
        self.nc, self.s, self.g, self.src, self.scales, self.shifts = nc, g.s, g, src, scales, shifts

    def buffers(self):
        g = self.g
        return (g.sb("squared", [P, B, T], F32), g.sb("primer", [P, 1], F32),
                g.pb("centred_ps", [P, B, T], F32), g.pb("var_ps", [P, B, T], F32))

    def use(self, work, primer, centred, var):
        self.work, self.primer, self.centred, self.var = work, primer, centred, var

    def tensor_centre(self, pe):
        for c in range(B):
            self.nc.tensor.matmul(self.centred[:, c], self.g.centre_w, self.src[:, cols(c)],
                                  start=True, stop=True).then_inc(self.s["centre"].sem, 1)

    def tensor_variance(self, pe):
        s = self.s
        for c in range(B):
            pe.wait_ge(s["square"].sem, s["square"].at(c + 1))
            self.nc.tensor.matmul(self.var[:, c], self.g.mean_w, self.work[:, c],
                                  start=True, stop=True).then_inc(s["var"].sem, 1)

    def scalar(self, act):
        s, nc, work = self.s, self.nc, self.work
        nc.scalar.activation(self.primer[:], self.g.eps[:, 0:1], ACT.Ln).then_inc(s["primed"].sem, 1)
        for c in range(B):
            act.wait_ge(s["centre"].sem, s["centre"].at(c + 1))
            nc.scalar.activation(work[:, c], self.centred[:, c], ACT.Square).then_inc(s["square"].sem, 1)
        for c in range(B):
            act.wait_ge(s["var"].sem, s["var"].at(c + 1))
            nc.scalar.activation(work[:, c], self.var[:, c], ACT.Ln, bias=self.g.eps[:, 0:1]
                                 ).then_inc(s["log"].sem, 1)
        for c in range(B):
            act.wait_ge(s["log"].sem, s["log"].at(c + 1))
            nc.scalar.activation(work[:, c], work[:, c], ACT.Exp, scale=-0.5).then_inc(s["std"].sem, 1)

    def scalar_modulate(self, act):
        s = self.s
        for c in range(self.ON_SCALAR):
            act.wait_ge(s["norm"].sem, s["norm"].at(c + 1))
            self.nc.scalar.activation(self.g.hT[:, cols(c)], self.work[:, c], ACT.Identity,
                                      scale=self.scales(c), bias=self.shifts(c)).then_inc(s["mod_act"].sem, 1)

    def vector(self, dve):
        s, work = self.s, self.work
        for c in range(B):
            dve.wait_ge(s["std"].sem, s["std"].at(c + 1))
            self.nc.vector.tensor_tensor(work[:, c], work[:, c], self.centred[:, c], ALU.mult
                                         ).then_inc(s["norm"].sem, 1)

    def vector_modulate(self, dve):
        s = self.s
        for c in range(self.ON_SCALAR, B):
            dve.wait_ge(s["norm"].sem, s["norm"].at(c + 1))
            self.nc.vector.tensor_scalar(self.g.hT[:, cols(c)], self.work[:, c], self.scales(c),
                                         self.shifts(c), ALU.mult, ALU.add).then_inc(s["mod_dve"].sem, 1)

    def end(self):
        s = self.s
        for name in ("square", "var", "centre", "std", "log", "norm"):
            s[name].end(B)
        s["primed"].end(1)
        s["mod_act"].end(self.ON_SCALAR)
        s["mod_dve"].end(B - self.ON_SCALAR)


def norm_phase(nc, g, src, scales, shifts):
    norm = Norm(nc, g, src, scales, shifts)
    work, primer, centred, var = norm.buffers()
    with work as work, primer as primer, centred as centred, var as var, nc.Block() as block:
        norm.use(work, primer, centred, var)

        @block.tensor
        def _(pe):
            norm.tensor_centre(pe)
            norm.tensor_variance(pe)

        @block.scalar
        def _(act):
            norm.scalar(act)
            norm.scalar_modulate(act)

        @block.vector
        def _(dve):
            norm.vector(dve)
            norm.vector_modulate(dve)

    norm.end()


def setup_phase(nc, g):
    D, s = g.dram, g.s
    norm = Norm(nc, g, g.xT, g.modcol(0, SCALE_A), g.modcol(0, SHIFT_A))
    work, primer, centred, var = norm.buffers()
    with g.sb("wmod", [P, 4, 6 * P], F32) as wmod, \
         g.sb("cond", [P, 16], F32) as cond, \
         g.sb("cond_t", [P, 3, 16], F32) as ct, \
         g.sb("lam_in", [P, 4, 4], F32) as lam_in, \
         g.sb("lam_t", [P, 2, 4], F32) as lam_t, \
         g.sb("lam_s", [P, 4], F32) as lam_s, \
         g.sb("gate_t", [P, 4, 2, 2, B], F32) as gt, \
         work as work, primer as primer, centred as centred, var as var, \
         nc.Block() as block:
        norm.use(work, primer, centred, var)
        mod_ps = var[:, 0]
        EPS, SILU, LAMBDAS = 2, 5, 8

        @block.sync
        def _(sp):
            for dst, src, name in (
                    [(g.consts[:], D["consts"], "dma_x"), (g.xT[:], D["xT"], "dma_x"), (cond[:], D["cT"], "dma_c"),
                     (lam_in[:], D["lambdas"].partition_broadcast(P), "dma_c")]
                    + [(wmod[:, i], D[f"L{i}_wmod"], "dma") for i in range(4)]
                    + [(g.columns[:], D["columns"], "dma"), (g.gate_w[:], D["gate_w"], "dma"),
                       (g.gate_b[:], D["gate_b"].partition_broadcast(P), "dma"),
                       (g.squares[:], D["squares"], "late"), (g.l3_w[:], D["L3_w"], "late")]):
                sp.dma_start(dst, src).then_inc(s[name].sem, 16)
            sp.dma_start(g.scratch["alibi"], D["alibi"]).then_inc(s["late"].sem, 16)

        @block.scalar
        def _(act):
            act.wait_ge(s["dma_c"].sem, s["dma_c"].at(32))
            nc.scalar.activation(ct[:, 0], cond[:], ACT.Exp, scale=-1.0).then_inc(s["act"].sem, 1)
            act.wait_ge(s["vec"].sem, s["vec"].at(LAMBDAS))
            nc.scalar.activation(lam_s[:, 2:4], lam_s[:, 0:2], ACT.Exp).then_inc(s["act"].sem, 1)
            norm.scalar(act)
            act.wait_ge(s["modulated"].sem, s["modulated"].at(1))
            norm.scalar_modulate(act)

        @block.vector
        def _(dve):
            n = 0

            def after(ins):
                nonlocal n
                n += 1
                ins.then_inc(s["vec"].sem, 1)
                dve.wait_ge(s["vec"].sem, s["vec"].at(n))

            after(nc.vector.memset(g.eps[:, 0:1], LN_EPS))
            after(nc.vector.memset(g.eps[:, 1:2], 0.0))
            dve.wait_ge(s["dma_c"].sem, s["dma_c"].at(32))
            dve.wait_ge(s["act"].sem, s["act"].at(1))
            after(nc.vector.tensor_scalar(ct[:, 1], ct[:, 0], 1.0, None, ALU.add))
            after(nc.vector.reciprocal(ct[:, 2], ct[:, 1]))
            after(nc.vector.tensor_tensor(g.cs[:], cond[:], ct[:, 2], ALU.mult))
            after(nc.vector.tensor_tensor(lam_t[:, 0], lam_in[:, 0], lam_in[:, 1], ALU.mult))
            after(nc.vector.tensor_tensor(lam_t[:, 1], lam_in[:, 2], lam_in[:, 3], ALU.mult))
            after(nc.vector.tensor_reduce(lam_s[:, 0:2], lam_t[:], X, ALU.add))
            dve.wait_ge(s["act"].sem, s["act"].at(2))
            after(nc.vector.tensor_scalar(lam_s[:, 0:1], lam_s[:, 3:4], -LAMBDA_INIT, None, ALU.add))
            after(nc.vector.tensor_tensor(g.neg_lam[:], lam_s[:, 0:1], lam_s[:, 2:3], ALU.subtract))
            norm.vector(dve)
            dve.wait_ge(s["pe"].sem, s["pe"].at(1))
            after(nc.vector.tensor_copy(g.mod[:], mod_ps[:, 0:96].rearrange(
                "p (l j b) -> p l j b", l=4, j=6)))
            after(nc.vector.tensor_scalar(g.mod[:, :, SCALE_B], g.mod[:, :, SCALE_B], 1.0, None, ALU.add))
            nc.vector.tensor_scalar(g.mod[:, :, SCALE_A], g.mod[:, :, SCALE_A], 1.0, None, ALU.add
                                    ).then_inc(s["modulated"].sem, 1)
            dve.wait_ge(s["modulated"].sem, s["modulated"].at(1))
            norm.vector_modulate(dve)
            for i, j in enumerate((GATE_A, GATE_B)):
                gate = g.mod[:, :, j]
                sign, size = gt[:, :, i, 0], gt[:, :, i, 1]
                after(nc.vector.tensor_scalar(sign, gate, 0.0, 2.0, ALU.is_ge, ALU.mult))
                after(nc.vector.tensor_scalar(size, gate, -1.0, 0.25, ALU.mult, ALU.max))
                after(nc.vector.tensor_tensor(size, size, gate, ALU.max))
                after(nc.vector.tensor_scalar(sign, sign, -1.0, None, ALU.add))
                after(nc.vector.tensor_tensor(gate, size, sign, ALU.mult))
            for layer, name in ((0, "L0_bo"), (1, "L1_bo")):
                after(nc.vector.tensor_scalar(g.gate_bias[:, layer], g.mod[:, layer, GATE_A],
                                              g.col(name), None, ALU.mult))
            after(nc.vector.tensor_scalar(g.rms_w[:], g.col("L2_rms"), 1.0 - LAMBDA_INIT, None, ALU.mult))
            g.n_vec = n

        @block.tensor
        def _(pe):
            pe.wait_ge(s["dma_x"].sem, s["dma_x"].at(32))
            norm.tensor_centre(pe)
            norm.tensor_variance(pe)
            pe.wait_ge(s["dma"].sem, s["dma"].at(16 * 7))
            pe.wait_ge(s["vec"].sem, s["vec"].at(SILU))
            pe.wait_ge(s["log"].sem, s["log"].at(1))
            for layer in range(4):
                for j in range(6):
                    at = (layer * 6 + j) * B
                    mm = nc.tensor.matmul(mod_ps[:, at:at + B], wmod[:, layer, j * P:(j + 1) * P],
                                          g.cs[:, layer * B:(layer + 1) * B], start=True, stop=True)
            mm.then_inc(s["pe"].sem, 1)

    norm.end()
    s["dma_x"].end(32)
    s["dma_c"].end(32)
    s["dma"].end(16 * 7)
    s["act"].end(2)
    s["vec"].end(g.n_vec)
    s["modulated"].end(1)
    s["pe"].end(1)


def by_part(tensor, parts):
    return tensor[:].rearrange("p (i t w) -> p i t w", i=B * parts, t=T // P)


def small_head_stacks(g):
    return (g.sb("q_stack", [P, 4, 4, T], F32R), g.sb("k_stack", [P, 4, 4, T], F32R),
            g.sb("v_group", [P, 4, T // P, P], F32))


def small_head_projections(nc, g, stacks, hd, wq, wk, wv, wq_swapped=None, wk_swapped=None):
    s = g.s
    heads = P // hd
    rope = wq_swapped is not None
    per_b = [("q", wq), ("qs", wq_swapped), ("k", wk), ("ks", wk_swapped)] if rope else [("q", wq), ("k", wk)]
    tasks = [(b, kind, w) for b in range(B) for kind, w in per_b + [("v", wv)]]
    n_task = len(tasks) // B
    parts = heads // 16
    q_scr = g.scratch["q"].rearrange("(b e r) t -> b e r t", b=B, e=heads)
    k_scr = g.scratch["k"].rearrange("(b e r) t -> b e r t", b=B, e=heads)
    with g.sb("full", [P, 4 if rope else 2, N], F32) as full, \
         g.sb("hi", [P, 2, N], F32) as hi, \
         g.sb("lo", [P, 2, N], F32) as lo, \
         g.sb("rope", [P, 2, T], F32) as rope_t, \
         g.pb("proj", [P, 8, T], F32) as ps, \
         nc.Block() as block:
        slot = {"q": 0, "k": 1, "qs": 2, "ks": 3}
        hi_r = hi[:].bitcast(F32R)

        @block.gpsimd
        def _(pool):
            qs, ks, vg = stacks
            nc.gpsimd.memset(ks[:].bitcast(F32), 0.0).then_inc(s["zeros"].sem, 1)
            nc.gpsimd.memset(vg[:], 1.0).then_inc(s["zeros"].sem, 1)
            nc.gpsimd.memset(qs[:, 2:4].bitcast(F32), 0.0).then_inc(s["zeros"].sem, 1)
            pool.wait_ge(s["zeros"].sem, s["zeros"].at(3))
            nc.gpsimd.memset(ks[MAX_ROW:MAX_ROW + 2].bitcast(F32), 1.0).then_inc(s["zeros"].sem, 1)

        @block.tensor
        def _(pe):
            pe.wait_ge(s["late"].sem, s["late"].at(LATE))
            for n, (b, kind, w) in enumerate(tasks):
                if n >= 8:
                    pe.wait_ge(s["evac"].sem, s["evac"].at(n - 7))
                if kind != "v":
                    mm = nc.tensor.matmul(ps[:, n % 8], g.square(w), g.hT[:, cols(b)], start=True, stop=True)
                else:
                    for t in range(T // P):
                        at = b * T + t * P
                        mm = nc.tensor.matmul(ps[:, n % 8, t * P:(t + 1) * P], g.hT[:, at:at + P],
                                              g.square(w), start=True, stop=True)
                mm.then_inc(s["mm"].sem, 1)

        @block.scalar
        def _(act):
            for n, (b, kind, _) in enumerate(tasks):
                act.wait_ge(s["mm"].sem, s["mm"].at(n + 1))
                if kind != "v":
                    nc.scalar.activation(full[:, slot[kind], cols(b)], ps[:, n % 8], ACT.Copy
                                         ).then_inc(s["evac"].sem, 1)
                else:
                    nc.scalar.activation(
                        by_part(g.v_tok, parts)[:, b * parts:(b + 1) * parts],
                        ps[:, n % 8].rearrange("p (t i w) -> p i t w", t=T // P, i=parts), ACT.Copy
                    ).then_inc(s["evac"].sem, 1)

        @block.vector
        def _(dve):
            step = s["vec"]
            n = 0

            def after(ins):
                nonlocal n
                n += 1
                ins.then_inc(step.sem, 1)
                dve.wait_ge(step.sem, step.at(n))

            after(nc.vector.memset(stacks[0][:, 0:2].bitcast(F32), 0.0))
            if rope:
                dve.wait_ge(s["dma"].sem, s["dma"].at(16))
            for b in range(B):
                for i in range(2):
                    dve.wait_ge(s["evac"].sem, s["evac"].at(n_task * b + (i + 1) * len(per_b) // 2))
                    f = full[:, i, cols(b)]
                    if rope:
                        f2 = full[:, 2 + i, cols(b)]
                        after(nc.vector.tensor_tensor(f, f, rope_t[:, 0], ALU.mult))
                        after(nc.vector.tensor_tensor(f2, f2, rope_t[:, 1], ALU.mult))
                        after(nc.vector.tensor_tensor(f, f, f2, ALU.add))
                    after(nc.vector.tensor_copy(hi_r[:, i, cols(b)], f))
                    nc.vector.tensor_tensor(lo[:, i, cols(b)], f, hi[:, i, cols(b)], ALU.subtract
                                            ).then_inc(s["split"].sem, 1)
            g.n_vec = n

        @block.sync
        def _(sp):
            if rope:
                sp.dma_start(rope_t[:], g.dram["rope"]).then_inc(s["dma"].sem, 16)
            for b in range(B):
                for i, (scr, parts) in enumerate(((q_scr, (hi, hi, lo)), (k_scr, (hi, lo, hi)))):
                    sp.wait_ge(s["split"].sem, s["split"].at(2 * b + i + 1))
                    for r, part in enumerate(parts):
                        sp.dma_start(scr[b, :, r * hd:(r + 1) * hd, :], part[:, i, cols(b)]
                                     ).then_inc(s["store"].sem, 16)
            sp.wait_ge(s["store"].sem, s["store"].at(16 * 6 * B))

    s["zeros"].end(4)
    s["mm"].end(len(tasks))
    s["evac"].end(len(tasks))
    s["vec"].end(g.n_vec)
    s["split"].end(2 * B)
    s["store"].end(16 * 6 * B)
    if rope:
        s["dma"].end(16)


def small_head_attention(nc, g, stacks, hd, scale, differential=False):
    s = g.s
    heads = P // hd
    NG = B * heads // 4
    K1 = 3 * hd
    KT = T // P
    TILES = 4 * KT
    DIVIDE = 5 if differential else 2
    BODY = 4
    q_scr = g.scratch["q"].rearrange("(e r) t -> e r t", r=K1)
    k_scr = g.scratch["k"].rearrange("(e r) t -> e r t", r=K1)
    HD_V = 8
    PAIR = 2 if differential else 1
    v_part, out_part = by_part(g.v_tok, heads // 16), by_part(g.att_tok, heads // 16)
    WIDTH = 4 // PAIR * HD_V
    qs, ks, vg = stacks
    with g.sb("probs", [P, KT, 4, T], F32) as probs, \
         g.sb("neg_max", [P, 2, TILES], F32) as neg_max, \
         g.sb("max_parts", [TILES, 2, 2, P], F32) as max_parts, \
         g.sb("raw", [P, 2, T], F32) as raw, \
         g.sb("recip", [P, KT, 4], F32) as recip, \
         g.sb("second", [P, 2, KT, 2, HD_V], F32) as pair_t, \
         g.pb("scores", [P, 4, T], F32) as sc_ps, \
         g.pb("scoresT", [P, 2, T], F32) as st_ps, \
         g.pb("values", [P, T], F32) as o_ps, \
         g.pb("rawT", [P, KT, 4, 32], F32) as rt_ps, \
         nc.Block() as block:
        mt_ps = rt_ps[:].rearrange("p t j r -> p (t j r)")[0:TILES, 0:P]
        SPLIT = 5

        def group(i, p, d=0):
            i, p = i + (p + d) // BODY, (p + d) % BODY
            if isinstance(i, int) and not 0 <= BODY * i + p < NG:
                return None
            return i, p, i * BODY + p

        def steps(eng, step):
            for i in (-1, 0):
                for p in range(BODY):
                    step(i, p)
            with eng.Fori(1, NG // BODY - 1) as i:
                for p in range(BODY):
                    step(i, p)
            for i in (NG // BODY - 1, NG // BODY):
                for p in range(BODY):
                    step(i, p)

        @block.sync
        def _(sp):
            def step(i, p):
                if at := group(i, p, 3):
                    gi, gp, n = at
                    sp.wait_ge(s["st"].sem, s["st"].at(TILES * (n - 3)))
                    for dst, src in ((qs, q_scr), (ks, k_scr)):
                        sp.dma_start(dst[0:K1, gp].bitcast(F32), src[bass.ds(n * 4, 4)].rearrange("e r t -> r e t")
                                     ).then_inc(s[f"load{gp}"].sem, 16)
                if at := group(i, p, 1):
                    gi, gp, n = at
                    sp.wait_ge(s["max_split"].sem, s["max_split"].at(n + 1))
                    for r in range(2):
                        sp.dma_start(qs[MAX_ROW + r:MAX_ROW + r + 1, gp].bitcast(F32)
                                     .rearrange("o j (t q) -> o (j t) q", t=KT), max_parts[:, gp % 2, r]).then_inc(s[f"rows{gp % 2}"].sem, 16)

            steps(sp, step)

        @block.gpsimd
        def _(pool):
            by_one = g.all_ones[:, 0:KT * WIDTH].rearrange("p (t j d) -> p t j d", t=KT, d=HD_V)

            def step(i, p):
                if at := group(i, p, 1):
                    gi, gp, n = at
                    pool.wait_ge(s["pv"].sem, s["pv"].at(KT * (n - 3)))
                    dst = vg[:, gp].rearrange("p t (j c r) -> p c t j r", c=PAIR, r=32)
                    for c in range(PAIR):
                        src = v_part[:, bass.ds(gi, 1), :, gp * WIDTH:(gp + 1) * WIDTH].rearrange(
                            "p i t (j d) -> p (i t) j d", d=HD_V)
                        nc.gpsimd.tensor_tensor(dst[:, c, :, :, 0:HD_V], src, by_one, ALU.mult
                                                ).then_inc(s["vg"].sem, 1)

            steps(pool, step)

        @block.scalar
        def _(act):
            def step(i, p):
                cur = group(i, p)
                for t in range(TILES):
                    if cur:
                        _, _, n = cur
                        kt, j = t // 4, t % 4
                        act.wait_ge(s["st"].sem, s["st"].at(TILES * n + t + 1))
                        if j == 0:
                            act.wait_ge(s["pv"].sem, s["pv"].at(KT * (n - 1) + kt + 1))
                        nc.scalar.activation(probs[:, kt, j], st_ps[:, t % 2], ACT.Exp, scale=scale
                                             ).then_inc(s["exp"].sem, 1)
                    if t == 4 and (at := group(i, p, -1)):
                        gi, gp, n = at
                        act.wait_ge(s["pv"].sem, s["pv"].at(KT * (n + 1)))
                        act.wait_ge(s["rawT"].sem, s["rawT"].at(n - 1))
                        nc.scalar.activation(raw[:, gp % 2], o_ps[:], ACT.Identity,
                                             bias=g.den_eps(hd)).then_inc(s["raw"].sem, 1)

            steps(act, step)

        @block.vector
        def _(dve):
            def divide(at, first):
                gi, gp, n = at
                done = lambda ins: ins.then_inc(s["divide"].sem, 1)
                dve.wait_ge(s["divide"].sem, s["divide"].at(DIVIDE * n + first))
                out = out_part[:, bass.ds(gi, 1), :, gp * WIDTH:(gp + 1) * WIDTH].rearrange(
                    "p i t (j d) -> p (i t) j d", d=HD_V)
                spread = [P, KT, 4 // PAIR, HD_V]
                if first == 0:
                    dve.wait_ge(s["rawT"].sem, s["rawT"].at(n + 1))
                    done(nc.vector.reciprocal(recip[:], rt_ps[:, :, :, HD_V]))
                elif not differential:
                    done(nc.vector.tensor_tensor(out, rt_ps[:, :, :, 0:HD_V],
                                                 recip[:].unsqueeze(3).broadcast_to(spread), ALU.mult))
                elif first == 1:
                    done(nc.vector.tensor_scalar(recip[:, :, 1::2], recip[:, :, 1::2], g.neg_lam[:], None,
                                                 ALU.mult))
                elif first < 4:
                    c = first - 2
                    done(nc.vector.tensor_tensor(pair_t[:, c], rt_ps[:, :, c::2, 0:HD_V],
                                                 recip[:, :, c::2].unsqueeze(3).broadcast_to(spread),
                                                 ALU.mult))
                else:
                    done(nc.vector.tensor_tensor(out, pair_t[:, 0], pair_t[:, 1], ALU.add))

            def step(i, p):
                ahead, next_, last = group(i, p, 2), group(i, p, 1), group(i, p, -1)
                for t in range(TILES):
                    if ahead:
                        _, gp, n = ahead
                        dve.wait_ge(s["scores"].sem, s["scores"].at(TILES * n + t + 1))
                        if t == 0:
                            dve.wait_ge(s["maxT"].sem, s["maxT"].at(n - 1))
                        nc.vector.tensor_reduce(neg_max[:, gp % 2, t:t + 1], sc_ps[:, t % 4], X, ALU.max,
                                                negate=True).then_inc(s["max"].sem, 1)
                    if t == SPLIT and next_:
                        _, gp, n = next_
                        dve.wait_ge(s["maxT"].sem, s["maxT"].at(n + 1))
                        dve.wait_ge(s[f"rows{gp % 2}"].sem, s[f"rows{gp % 2}"].at(next_[0] * 64 + 32 * (gp // 2)))
                        nc.vector.tensor_copy(max_parts[:, gp % 2, 0].bitcast(F32R), mt_ps
                                              ).then_inc(s["max_hi"].sem, 1)
                    if t == SPLIT + 1 and next_:
                        _, gp, n = next_
                        dve.wait_ge(s["max_hi"].sem, s["max_hi"].at(n + 1))
                        nc.vector.tensor_tensor(max_parts[:, gp % 2, 1], mt_ps, max_parts[:, gp % 2, 0],
                                                ALU.subtract).then_inc(s["max_split"].sem, 1)
                    if t >= TILES - 4 and last and t - (TILES - 4) < DIVIDE:
                        divide(last, t - (TILES - 4))
                if last and DIVIDE > 4:
                    divide(last, 4)

            steps(dve, step)

        @block.tensor
        def _(pe):
            def values(cur, kt):
                _, gp, n = cur
                pe.wait_ge(s["exp"].sem, s["exp"].at(TILES * n + 4 * kt + 4))
                if kt == 0:
                    pe.wait_ge(s["raw"].sem, s["raw"].at(n))
                    pe.wait_ge(s["vg"].sem, s["vg"].at((n + 1) * PAIR))
                for j in range(4):
                    mm = nc.tensor.matmul(o_ps[32 * j:32 * j + 32], vg[:, gp, kt, 32 * j:32 * j + 32],
                                          probs[:, kt, j], start=kt == 0, stop=kt == KT - 1)
                mm.then_inc(s["pv"].sem, 1)

            def step(i, p):
                ahead, cur = group(i, p, 2), group(i, p)
                if ahead:
                    gi, gp, n = ahead
                    pe.wait_ge(s[f"load{gp}"].sem, s[f"load{gp}"].at(gi * 32 + 32))
                if cur:
                    gi, gp, n = cur
                    pe.wait_ge(s[f"rows{gp % 2}"].sem, s[f"rows{gp % 2}"].at(gi * 64 + 32 * (gp // 2) + 32))
                for t in range(TILES):
                    if ahead:
                        gi, gp, n = ahead
                        j, qt = t // KT, t % KT
                        pe.wait_ge(s["max"].sem, s["max"].at(TILES * n + t - 3))
                        r = slice(0, MAX_ROW)
                        nc.tensor.matmul(sc_ps[:, t % 4], qs[r, gp, j, qt * P:(qt + 1) * P], ks[r, gp, j],
                                         start=True, stop=True).then_inc(s["scores"].sem, 1)
                    if cur:
                        gi, gp, n = cur
                        kt, j = t // 4, t % 4
                        pe.wait_ge(s["exp"].sem, s["exp"].at(TILES * n + t - 1))
                        nc.tensor.matmul(st_ps[:, t % 2], ks[:, gp, j, kt * P:(kt + 1) * P], qs[:, gp, j],
                                         start=True, stop=True).then_inc(s["st"].sem, 1)
                    if t == SPLIT - 1 and (at := group(i, p, 1)):
                        _, gp, n = at
                        pe.wait_ge(s["max"].sem, s["max"].at(TILES * (n + 1)))
                        pe.wait_ge(s["divide"].sem, s["divide"].at(DIVIDE * (n - 2)))
                        nc.tensor.transpose(mt_ps, neg_max[:, gp % 2], g.identity
                                            ).then_inc(s["maxT"].sem, 1)
                    if t == TILES - 4 and (at := group(i, p, -1)):
                        _, gp, n = at
                        pe.wait_ge(s["raw"].sem, s["raw"].at(n + 1))
                        pe.wait_ge(s["divide"].sem, s["divide"].at(DIVIDE * n))
                        if at_next := group(i, p, 1):
                            pe.wait_ge(s["max_split"].sem, s["max_split"].at(at_next[2] + 1))
                        for qt in range(KT):
                            mm = nc.tensor.transpose(rt_ps[:, qt].rearrange("p j r -> p (j r)"),
                                                     raw[:, gp % 2, qt * P:(qt + 1) * P], g.identity)
                        mm.then_inc(s["rawT"].sem, 1)
                    if t == 2 and (at := group(i, p, -1)):
                        values(at, KT - 1)
                    if cur and t % 4 == 2 and t > 4:
                        values(cur, t // 4 - 1)

            steps(pe, step)

    for name in ("st", "scores", "max", "exp"):
        s[name].end(TILES * NG)
    for name in ("max_split", "max_hi", "maxT", "raw", "rawT"):
        s[name].end(NG)
    s["divide"].end(DIVIDE * NG)
    s["pv"].end(KT * NG)
    s["vg"].end(NG * PAIR)
    for p in range(BODY):
        s[f"load{p}"].end(32 * NG // BODY)
    for q in range(2):
        s[f"rows{q}"].end(32 * NG // 2)


def attention_output(nc, g, layer, weights, biased):
    s = g.s
    att = g.att_tok[:].rearrange("p (n d) -> p n d", d=P)
    with g.sb("attn", [P, B, T], F32) as attn, \
         g.sb("update", [P, B, T], F32) as upd, \
         g.pb("turn_ps", [P, B, T], F32) as turn_ps, \
         g.pb("out_ps", [P, B, T], F32) as ps, \
         nc.Block() as block:

        @block.tensor
        def _(pe):
            for b in range(B):
                for t in range(T // P):
                    mm = nc.tensor.transpose(turn_ps[:, b, t * P:(t + 1) * P], att[:, b * (T // P) + t],
                                             g.identity)
                mm.then_inc(s["rawT"].sem, 1)
            for b in range(B):
                pe.wait_ge(s["evac"].sem, s["evac"].at(b + 1))
                nc.tensor.matmul(ps[:, b], weights, attn[:, b], start=True, stop=True
                                 ).then_inc(s["mm"].sem, 1)

        @block.scalar
        def _(act):
            for b in range(B):
                act.wait_ge(s["rawT"].sem, s["rawT"].at(b + 1))
                nc.scalar.activation(attn[:, b], turn_ps[:, b], ACT.Copy).then_inc(s["evac"].sem, 1)
            for b in range(B):
                act.wait_ge(s["mm"].sem, s["mm"].at(b + 1))
                bias = g.gate_bias[:, layer, b:b + 1] if biased else 0.0
                nc.scalar.activation(upd[:, b], ps[:, b], ACT.Identity, bias=bias,
                                     scale=g.mod[:, layer, GATE_A, b:b + 1]).then_inc(s["act"].sem, 1)

        @block.vector
        def _(dve):
            for b in range(B):
                dve.wait_ge(s["act"].sem, s["act"].at(b + 1))
                nc.vector.tensor_tensor(g.xT[:, cols(b)], g.xT[:, cols(b)], upd[:, b], ALU.add
                                        ).then_inc(s["vec"].sem, 1)

    for name in ("rawT", "evac", "mm", "act", "vec"):
        s[name].end(B)


class Router:

    NT, E = N // P, EXPERTS

    def __init__(self, nc, g, kind, gate, r, rc, totals_sb, rows, banks):
        self.nc, self.s, self.g, self.kind = nc, g.s, g, kind
        self.r, self.rc, self.totals_sb, self.rows, self.banks = r, rc, totals_sb, rows, banks
        self.gate_w = g.gate_w[:, gate]
        self.gate_b = g.gate_b[:, gate] if gate < 2 else None
        W = self.NT * self.E
        self.nk = 2 if kind == "each" else 1
        self.logits, self.totals = banks[:, 0, 0:W], banks[:, 0, W:(1 + self.nk) * W]
        self.counts = banks[:, 1, 0:self.nk * W]

    P_, SEL, EQ, OH1, OH2, V, M, M_2, COMB, T1 = range(10)
    M1, M2, I1, SUM, R1, W1, W2 = range(7)

    def tensor_logits(self, pe):
        s, nc, E = self.s, self.nc, self.E
        for t in range(self.NT):
            mm = nc.tensor.matmul(self.logits[:, t * E:(t + 1) * E], self.g.hT[:, t * P:(t + 1) * P],
                                  self.gate_w, start=True, stop=True)
        mm.then_inc(s["logits"].sem, 1)

    def tensor_ranks(self, pe):
        s, nc, g, E, W = self.s, self.nc, self.g, self.E, self.NT * self.E
        if self.kind != "open":
            pe.wait_ge(s["chosen"].sem, s["chosen"].at(1))
            for k in range(self.nk):
                one = slice(k * W, (k + 1) * W)
                chosen = self.r[:, self.M + k].rearrange("p t e -> p (t e)")
                mm = nc.tensor.matmul(self.totals[:, one], chosen, g.all_ones, start=True, stop=True)
            mm.then_inc(s["totals"].sem, 1)
            pe.wait_ge(s["evac"].sem, s["evac"].at(1))
            for k in range(self.nk):
                one = slice(k * W, (k + 1) * W)
                chosen = self.r[:, self.M + k].rearrange("p t e -> p (t e)")
                nc.tensor.matmul(self.counts[:, one], g.tri, chosen, start=True, stop=False)
                mm = nc.tensor.matmul(self.counts[:, one], self.totals_sb[:, k], g.before, start=False, stop=True)
            mm.then_inc(s["counts"].sem, 1)

    def tensor_rows(self, pe, half):
        s, nc, g, E = self.s, self.nc, self.g, self.E
        if half == 0:
            pe.wait_ge(s["chosen"].sem, s["chosen"].at(2))
        else:
            pe.wait_ge(s["evac"].sem, self.rows_ready(1))
        for t in range(half * self.NT // 2, (half + 1) * self.NT // 2):
            mm = nc.tensor.transpose(self.banks[0:E, t // 4 % 2, (t % 4) * P:(t % 4 + 1) * P],
                                     self.r[:, self.COMB, t], g.identity)
        mm.then_inc(s["maxT"].sem, 1)

    def scalar_exp(self, act):
        s, nc = self.s, self.nc
        act.wait_ge(s["centre"].sem, s["centre"].at(1))
        nc.scalar.activation(self.r[:, self.T1], self.r[:, self.P_], ACT.Exp).then_inc(s["act"].sem, 1)

    def scalar_totals(self, act):
        s, nc = self.s, self.nc
        if self.kind != "open":
            act.wait_ge(s["totals"].sem, s["totals"].at(1))
            nc.scalar.activation(self.totals_sb[:, 0:self.nk].rearrange("p k w -> p (k w)"), self.totals,
                                 ACT.Copy).then_inc(s["evac"].sem, 1)

    def scalar_rows(self, act, half):
        s, nc = self.s, self.nc
        act.wait_ge(s["maxT"].sem, s["maxT"].at(half + 1))
        for c in (2 * half, 2 * half + 1):
            nc.scalar.activation(self.rows[:, cols(c)], self.banks[0:self.E, c % 2], ACT.Copy
                                 ).then_inc(s["evac"].sem, 1)

    def rows_ready(self, halves):
        return self.s["evac"].at(2 * halves + (self.kind != "open"))

    def store(self, sp):
        s, g = self.s, self.g
        sp.dma_start(g.scratch["comb"][self.E].rearrange("(a b) -> a b", b=P), g.all_ones[0:self.NT, :]
                     ).then_inc(s["store"].sem, 16)
        sp.wait_ge(s["evac"].sem, self.rows_ready(2))
        sp.dma_start(g.scratch["comb"][0:self.E, :], self.rows[:]).then_inc(s["store"].sem, 16)
        sp.wait_ge(s["store"].sem, s["store"].at(32))

    def vector(self, dve, between, before_ranks):
        s, g, v, r, rc, kind, nk = self.s, self.g, self.nc.vector, self.r, self.rc, self.kind, self.nk
        NT, E = self.NT, self.E
        P_, SEL, EQ, OH1, OH2, V, M, COMB, T1 = (self.P_, self.SEL, self.EQ, self.OH1, self.OH2, self.V,
                                                 self.M, self.COMB, self.T1)
        M1, M2, I1, SUM, R1, W1, W2 = self.M1, self.M2, self.I1, self.SUM, self.R1, self.W1, self.W2
        big = 1e30 if kind == "open" else 4.0
        n = 0

        def spread(col):
            return col.unsqueeze(2).broadcast_to([P, NT, E])

        def over_tiles(t):
            return t.unsqueeze(1).broadcast_to([P, NT, E])

        def after(ins):
            nonlocal n
            n += 1
            ins.then_inc(s["route"].sem, 1)
            if n % 4 == 0:
                between()
            dve.wait_ge(s["route"].sem, s["route"].at(n))

        dve.wait_ge(s["logits"].sem, s["logits"].at(1))
        source = self.logits.rearrange("p (t e) -> p t e", e=E)
        if kind == "norm":
            after(v.tensor_tensor(r[:, P_], source, over_tiles(self.gate_b), ALU.add))
            source = r[:, P_]
        after(v.tensor_reduce(rc[:, M1], source, X, ALU.max))
        v.tensor_tensor(r[:, P_], source, spread(rc[:, M1]), ALU.subtract).then_inc(s["centre"].sem, 1)
        dve.wait_ge(s["act"].sem, s["act"].at(1))
        after(v.tensor_reduce(rc[:, SUM], r[:, T1], X, ALU.add))
        after(v.reciprocal(rc[:, R1], rc[:, SUM]))
        after(v.tensor_tensor(r[:, P_], r[:, T1], spread(rc[:, R1]), ALU.mult))
        sel = P_
        if kind == "open":
            sel = SEL
            after(v.tensor_tensor(r[:, SEL], r[:, P_], over_tiles(self.gate_b), ALU.add))
        for m, oh in ((M1, OH1), (M2, OH2)):
            after(v.tensor_reduce(rc[:, m], r[:, sel], X, ALU.max))
            after(v.tensor_tensor(r[:, EQ], r[:, sel], spread(rc[:, m]), ALU.is_equal))
            after(v.tensor_tensor(r[:, V], r[:, EQ], over_tiles(g.iota), ALU.mult))
            after(v.tensor_reduce(rc[:, I1], r[:, V], X, ALU.min))
            one_hot = oh if kind != "each" else M if m == M1 else self.M_2
            choice = v.tensor_tensor(r[:, one_hot], over_tiles(g.iota), spread(rc[:, I1]), ALU.is_equal)
            if m == M1:
                after(choice)
                after(v.tensor_scalar(r[:, T1], r[:, one_hot], -big, None, ALU.mult))
                after(v.tensor_tensor(r[:, SEL], r[:, T1], r[:, sel], ALU.add))
                sel = SEL
            elif kind == "each":
                choice.then_inc(s["chosen"].sem, 1)
            else:
                after(choice)
        if kind == "open":
            after(v.tensor_tensor(r[:, EQ], r[:, OH1], r[:, OH2], ALU.add))
            v.tensor_tensor(r[:, COMB], r[:, EQ], r[:, P_], ALU.mult).then_inc(s["chosen"].sem, 2)
        else:
            if kind == "norm":
                v.tensor_tensor(r[:, M], r[:, OH1], r[:, OH2], ALU.add).then_inc(s["chosen"].sem, 1)
            dve.wait_ge(s["chosen"].sem, s["chosen"].at(1))
            after(v.tensor_tensor(rc[:, SUM], rc[:, M1], rc[:, M2], ALU.add))
            if kind == "each":
                after(v.tensor_scalar(rc[:, SUM], rc[:, SUM], 1e-9, None, ALU.add))
            after(v.reciprocal(rc[:, R1], rc[:, SUM]))
            after(v.tensor_tensor(rc[:, W1:W2 + 1], rc[:, M1:M2 + 1],
                                  rc[:, R1].unsqueeze(1).broadcast_to([P, 2, NT]), ALU.mult))
            for m, oh, k in ((W1, OH1, M), (W2, OH2, self.M_2)):
                after(v.tensor_tensor(r[:, oh], r[:, k if kind == "each" else oh], spread(rc[:, m]), ALU.mult))
            if kind == "norm":
                after(v.tensor_tensor(r[:, OH1], r[:, OH1], r[:, OH2], ALU.add))
            before_ranks()
            dve.wait_ge(s["counts"].sem, s["counts"].at(1))
            counts = self.counts.rearrange("p (k t e) -> p k t e", k=nk, e=E)
            if kind == "norm":
                v.scalar_tensor_tensor(r[:, COMB], counts[:, 0], float(CAPACITY), r[:, OH1], ALU.is_le, ALU.mult
                                       ).then_inc(s["chosen"].sem, 1)
            else:
                after(v.scalar_tensor_tensor(r[:, OH1:OH2 + 1], counts, float(CAPACITY), r[:, OH1:OH2 + 1],
                                             ALU.is_le, ALU.mult))
                v.tensor_tensor(r[:, COMB], r[:, OH1], r[:, OH2], ALU.add).then_inc(s["chosen"].sem, 1)
        self.steps = n

    def end(self):
        s, ranked = self.s, self.kind != "open"
        s["route"].end(self.steps)
        s["chosen"].end(2)
        s["evac"].end(B + ranked)
        s["store"].end(32)
        s["maxT"].end(2)
        for name in ("centre", "act", "logits") + (("totals", "counts") if ranked else ()):
            s[name].end(1)


def experts_phase(nc, g, layer, kind, gate, up_names, down_name, n_experts, ff, gated, b1_name=None,
                  b2_name=None):
    s = g.s
    FT = ff // P
    NU = len(up_names)
    turns = (n_experts - 2) // 2
    with g.sb("w_up", [P, 2, NU, ff], F32) as wu, \
         g.sb("w_down", [P, 2, FT, P], F32) as wd, \
         g.sb("w_up_parts", [P, 2, 2, NU, ff], F32R) as wup, \
         g.sb("w_down_parts", [P, 2, 2, FT, P], F32R) as wdp, \
         g.sb("h_parts", [P, 2, N], F32R) as hp, \
         g.sb("b_up", [P, 2, FT], F32) as bu, \
         g.sb("weights_of", [P, 2, N], F32) as cb, \
         g.sb("hidden", [P, 4, T], F32) as full, \
         g.sb("hidden_parts", [P, 2, 2, FT, T], F32R) as hid, \
         g.sb("silu_weighted", [P, 4, T], F32) as silu_weighted, \
         g.sb("acc", [P, B, T], F32) as acc, \
         g.sb("bias_sum", [P, B if b2_name else 1, T], F32) as bias_sum, \
         g.sb("b_down", [EXPERTS, P], F32) as bd, \
         g.sb("comb_rows", [EXPERTS, N], F32) as rows, \
         g.sb("router", [P, 12, N // P, EXPERTS], F32) as r, \
         g.sb("router_col", [P, 7, N // P], F32) as rc, \
         g.pb("up_ps", [P, 4, T], F32) as up_ps, \
         g.pb("down_ps", [P, 2, T], F32) as dn_ps, \
         g.pb("router_ps", [P, 2, T], F32) as r_ps, \
         nc.Block() as block:
        f32 = lambda ap: ap.bitcast(F32)
        silu, wtd = silu_weighted[:, 0:2], silu_weighted[:, 2:4]
        totals_sb = r[:, 10:12].rearrange("p k t e -> p k (t e)")
        router = Router(nc, g, kind, gate, r, rc, totals_sb, rows, r_ps)
        w_load = 16 * (NU + 1)

        def experts(eng, step):
            with eng.Fori(0, turns) as i:
                step(i * 2 + 1, 1, i)
                step(i * 2 + 2, 0, i + 1)
            for e in range(2 * turns + 1, n_experts):
                step(e, e % 2, e // 2)

        def following(e, q, i, c):
            if c + 1 < B:
                return e, q, i, c + 1
            if isinstance(e, int) and e + 1 == n_experts:
                return None
            return e + 1, 1 - q, i + q, 0

        @block.sync
        def _(sp):
            if b2_name:
                sp.dma_start(bd[:], g.dram[b2_name]).then_inc(s["dma"].sem, 16)

            def load_weights(e, q):
                one = bass.ds(e, 1)
                for k, name in enumerate(up_names):
                    sp.dma_start(wu[:, q, k], g.dram[name][one].rearrange("o d f -> (o d) f")
                                 ).then_inc(s[f"load{q}"].sem, 16)
                sp.dma_start(wd[:, q], g.dram[down_name][one].rearrange("o (t p) d -> p (o t) d", p=P)
                             ).then_inc(s[f"load{q}"].sem, 16)

            def load_bias(e, q):
                if b1_name:
                    sp.dma_start(bu[:, q], g.dram[b1_name][bass.ds(e, 1)].rearrange("o p t -> (o p) t")
                                 ).then_inc(s[f"bias{q}"].sem, 16)

            def load_comb(e, q):
                sp.dma_start(cb[:, q], g.scratch["comb"][bass.ds(e, 1)].rearrange("o n -> (o n)")
                             .partition_broadcast(P)).then_inc(s[f"comb{q}"].sem, 16)

            def step(e, q):
                more = not isinstance(e, int) or e + 2 < n_experts
                if more:
                    sp.wait_ge(s["w_split"].sem, s["w_split"].at(e + 1))
                    load_weights(e + 2, q)
                sp.wait_ge(s["added"].sem, s["added"].at(B * (e - 1)))
                load_comb(e + 1, 1 - q)
                if more and b1_name:
                    sp.wait_ge(s["full"].sem, s["full"].at(B * FT * (e + 1)))
                    load_bias(e + 2, q)

            for e in range(2):
                load_weights(e, e)
                load_bias(e, e)
            sp.wait_ge(s["w_split"].sem, s["w_split"].at(1))
            load_weights(2, 0)
            router.store(sp)
            load_comb(0, 0)
            load_comb(1, 1)
            if b1_name:
                sp.wait_ge(s["full"].sem, s["full"].at(B * FT))
                load_bias(2, 0)
            sp.wait_ge(s["first"].sem, s["first"].at(B))
            loads = (n_experts - 3) // 2
            with sp.Fori(0, loads) as i:
                step(i * 2 + 1, 1)
                step(i * 2 + 2, 0)
            for e in range(2 * loads + 1, n_experts - 1):
                step(e, e % 2)

        @block.tensor
        def _(pe):
            def up(at):
                e, q, i, c = at
                if c == 0:
                    pe.wait_ge(s["w_split"].sem, s["w_split"].at(e + 1))
                for t in range(FT):
                    for k in range(NU):
                        h = (e * B + c) * FT + t
                        n = (c * FT + t) * NU + k
                        pe.wait_ge(s["full"].sem, s["full"].at(h - 1 if gated else h - 3))
                        for w_part, h_part in PASSES:
                            mm = nc.tensor.matmul(up_ps[:, n % 4], wup[:, q, w_part, k, t * P:(t + 1) * P],
                                                  hp[:, h_part, cols(c)], start=w_part + h_part == 0,
                                                  stop=w_part == 1)
                        mm.then_inc(s["up"].sem, 1)

            def down(q, c):
                for t in range(FT):
                    for w_part, h_part in PASSES:
                        mm = nc.tensor.matmul(dn_ps[:, c % 2], wdp[:, q, w_part, t], hid[:, c % 2, h_part, t],
                                              start=t + w_part + h_part == 0,
                                              stop=t == FT - 1 and w_part == 1)
                mm.then_inc(s["down"].sem, 1)

            def step(e, q, i):
                for c in range(B):
                    if after := following(e, q, i, c):
                        up(after)
                    m = (e - 1) * B + c
                    pe.wait_ge(s["lo"].sem, s["lo"].at((m + 1) * FT))
                    pe.wait_ge(s["weighted"].sem, s["weighted"].at(m - 1))
                    down(q, c)

            router.tensor_logits(pe)
            pe.wait_ge(s["split"].sem, s["split"].at(B))
            up((0, 0, 0, 0))
            for c in range(B):
                up(following(0, 0, 0, c))
                if c == 0:
                    router.tensor_ranks(pe)
                pe.wait_ge(s["lo0"].sem, s["lo0"].at((c + 1) * FT))
                pe.wait_ge(s["raw0"].sem, s["raw0"].at(c - 1))
                down(0, c)
                if c in (1, 2):
                    router.tensor_rows(pe, c - 1)
            if b2_name:
                pe.wait_ge(s["dma"].sem, s["dma"].at(16))
                pe.wait_ge(s["evac"].sem, router.rows_ready(2))
                for c in range(B):
                    pe.wait_ge(s["bias_out"].sem, s["bias_out"].at(c - 1))
                    nc.tensor.matmul(r_ps[:, c % 2], bd[:], rows[:, cols(c)], start=True, stop=True
                                     ).then_inc(s["mm"].sem, 1)
            pe.wait_ge(s["raw0"].sem, s["raw0"].at(B))
            experts(pe, step)

        @block.scalar
        def _(act):
            for c in range(B):
                nc.scalar.activation(hp[:, 0, cols(c)], g.hT[:, cols(c)], ACT.Copy).then_inc(s["max_hi"].sem, 1)
            router.scalar_exp(act)

            def chunk(e, q, c, lo, base):
                m = e * B + c

                def hi(t):
                    act.wait_ge(s["full"].sem, s["full"].at(m * FT + t + 1))
                    nc.scalar.activation(hid[:, c % 2, 0, t], full[:, (c * FT + t) % 4], ACT.Copy
                                         ).then_inc(s["hi"].sem, 1)

                act.wait_ge(s["down"].sem, s["down"].at(m - 1))
                for t in range(FT):
                    h, n = m * FT + t, (c * FT + t) * NU
                    act.wait_ge(s["up"].sem, s["up"].at(h * NU + 1))
                    if gated:
                        act.wait_ge(s["full"].sem, s["full"].at(h - 1))
                        nc.scalar.activation(silu[:, (c * FT + t) % 2], up_ps[:, n % 4], ACT.Silu
                                             ).then_inc(s["silu"].sem, 1)
                    else:
                        act.wait_ge(lo.sem, lo.at(h - 3 - base))
                        nc.scalar.activation(full[:, n % 4], up_ps[:, n % 4], ACT.Relu,
                                             bias=bu[:, q, t:t + 1]).then_inc(s["full"].sem, 1)
                    if t:
                        hi(t - 1)
                hi(FT - 1)

            def keep(c):
                act.wait_ge(s["down"].sem, s["down"].at(c + 1))
                nc.scalar.activation(acc[:, c], dn_ps[:, c % 2], ACT.Copy).then_inc(s["raw0"].sem, 1)

            if b1_name:
                act.wait_ge(s["bias0"].sem, s["bias0"].at(16))
            for c in range(B):
                chunk(0, 0, c, s["lo0"], 0)
                if c == 1:
                    router.scalar_totals(act)
                if c:
                    keep(c - 1)
                if c >= 2:
                    router.scalar_rows(act, c - 2)
            keep(B - 1)
            if b2_name:
                for c in range(B):
                    act.wait_ge(s["mm"].sem, s["mm"].at(c + 1))
                    nc.scalar.activation(bias_sum[:, c], r_ps[:, c % 2], ACT.Copy).then_inc(s["bias_out"].sem, 1)
            act.wait_ge(s["lo0"].sem, s["lo0"].at(B * FT))

            def step(e, q, i):
                if b1_name:
                    act.wait_ge(s[f"bias{q}"].sem, s[f"bias{q}"].at(16 * (i + 1)))
                for c in range(B):
                    chunk(e, q, c, s["lo"], B * FT)

            experts(act, step)

        @block.vector
        def _(dve):
            for c in range(B):
                dve.wait_ge(s["max_hi"].sem, s["max_hi"].at(c + 1))
                nc.vector.tensor_tensor(hp[:, 1, cols(c)], g.hT[:, cols(c)], f32(hp[:, 0, cols(c)]),
                                        ALU.subtract).then_inc(s["split"].sem, 1)

            def split_weights(e, q, i):
                dve.wait_ge(s[f"load{q}"].sem, s[f"load{q}"].at(w_load * (i + 1)))
                dve.wait_ge(s["down"].sem, s["down"].at(B * (e - 1)))
                nc.vector.tensor_copy(wup[:, q, 0], wu[:, q]).then_inc(s["w_hi"].sem, 1)
                nc.vector.tensor_copy(wdp[:, q, 0], wd[:, q]).then_inc(s["w_hi"].sem, 1)

            def gate_product(h, tile, lo, base):
                dve.wait_ge(s["up"].sem, s["up"].at((h + 1) * NU))
                dve.wait_ge(s["silu"].sem, s["silu"].at(h + 1))
                dve.wait_ge(lo.sem, lo.at(h - 3 - base))
                dve.wait_ge(s["hi"].sem, s["hi"].at(h - 3))
                nc.vector.tensor_tensor(full[:, tile % 4], silu[:, tile % 2], up_ps[:, (tile * NU + 1) % 4],
                                        ALU.mult).then_inc(s["full"].sem, 1)

            def hidden(at):
                e, q, i, c = at
                if gated:
                    for t in range(FT):
                        gate_product((e * B + c) * FT + t, c * FT + t, s["lo"], B * FT)
                for t in range(FT):
                    dve.wait_ge(s["hi"].sem, s["hi"].at((e * B + c) * FT + t + 1))
                    nc.vector.tensor_tensor(hid[:, c % 2, 1, t], full[:, (c * FT + t) % 4],
                                            f32(hid[:, c % 2, 0, t]), ALU.subtract).then_inc(s["lo"].sem, 1)

            split_weights(0, 0, 0)
            split_weights(1, 1, 0)
            products = 0

            def between():
                nonlocal products
                if gated and products < B * FT:
                    gate_product(products, products, s["lo0"], 0)
                    products += 1

            def before_ranks():
                while gated and products < 2 * FT:
                    between()

            router.vector(dve, between, before_ranks)
            while gated and products < B * FT:
                between()

            def step(e, q, i):
                for c in range(B):
                    if after := following(e, q, i, c):
                        hidden(after)
                    if c == 1 and (after := following(e, q, i, B - 1)):
                        split_weights(*after[:3])
                    m = (e - 1) * B + c
                    if c == 0:
                        dve.wait_ge(s[f"comb{q}"].sem, s[f"comb{q}"].at(16 * (i + 1)))
                    dve.wait_ge(s["down"].sem, s["down"].at(B + m + 1))
                    dve.wait_ge(s["added"].sem, s["added"].at(m - 1))
                    nc.vector.tensor_tensor(wtd[:, c % 2], cb[:, q, cols(c)], dn_ps[:, c % 2], ALU.mult
                                            ).then_inc(s["weighted"].sem, 1)

            dve.wait_ge(s["lo0"].sem, s["lo0"].at(B * FT))
            hidden((1, 1, 0, 0))
            dve.wait_ge(s["comb0"].sem, s["comb0"].at(16))
            for c in range(B):
                dve.wait_ge(s["raw0"].sem, s["raw0"].at(c + 1))
                ins = nc.vector.tensor_tensor(acc[:, c], acc[:, c], cb[:, 0, cols(c)], ALU.mult)
                if b2_name:
                    ins.then_inc(s["weighted0"].sem, 1)
                    dve.wait_ge(s["weighted0"].sem, s["weighted0"].at(c + 1))
                    dve.wait_ge(s["bias_out"].sem, s["bias_out"].at(c + 1))
                    ins = nc.vector.tensor_tensor(acc[:, c], acc[:, c], bias_sum[:, c], ALU.add)
                ins.then_inc(s["first"].sem, 1)
            experts(dve, step)
            dve.wait_ge(s["added"].sem, s["added"].at(B * (n_experts - 1)))
            for c in range(B):
                nc.vector.scalar_tensor_tensor(g.xT[:, cols(c)], acc[:, c], g.mod[:, layer, GATE_B, c:c + 1],
                                               g.xT[:, cols(c)], ALU.mult, ALU.add).then_inc(s["vec"].sem, 1)

        @block.gpsimd
        def _(pool):
            def split_weights(e, q, i):
                pool.wait_ge(s["w_hi"].sem, s["w_hi"].at(2 * (e + 1)))
                nc.gpsimd.tensor_tensor(wup[:, q, 1], wu[:, q], f32(wup[:, q, 0]), ALU.subtract
                                        ).then_inc(s["w_lo"].sem, 1)
                nc.gpsimd.tensor_tensor(wdp[:, q, 1], wd[:, q], f32(wdp[:, q, 0]), ALU.subtract
                                        ).then_inc(s["w_split"].sem, 1)

            split_weights(0, 0, 0)
            for c in range(B):
                if c == 2:
                    split_weights(1, 1, 0)
                for t in range(FT):
                    pool.wait_ge(s["hi"].sem, s["hi"].at(c * FT + t + 1))
                    nc.gpsimd.tensor_tensor(hid[:, c % 2, 1, t], full[:, (c * FT + t) % 4],
                                            f32(hid[:, c % 2, 0, t]), ALU.subtract).then_inc(s["lo0"].sem, 1)
            pool.wait_ge(s["first"].sem, s["first"].at(B))

            def step(e, q, i):
                for c in range(B):
                    if c == 2 and (after := following(e, q, i, B - 1)):
                        split_weights(*after[:3])
                    m = (e - 1) * B + c
                    pool.wait_ge(s["weighted"].sem, s["weighted"].at(m + 1))
                    pool.wait_ge(s["added"].sem, s["added"].at(m - 3))
                    nc.gpsimd.tensor_tensor(acc[:, c], acc[:, c], wtd[:, c % 2], ALU.add
                                            ).then_inc(s["added"].sem, 1)

            experts(pool, step)

    if b2_name:
        s["dma"].end(16)
        for name in ("mm", "bias_out", "weighted0"):
            s[name].end(B)
    router.end()
    for name in ("first", "vec", "max_hi", "split"):
        s[name].end(B)
    s["up"].end(B * FT * NU * n_experts)
    for name in ("full", "hi") + (("silu",) if gated else ()):
        s[name].end(B * FT * n_experts)
    s["lo"].end(B * FT * (n_experts - 1))
    s["lo0"].end(B * FT)
    s["raw0"].end(B)
    s["down"].end(B * n_experts)
    for name in ("weighted", "added"):
        s[name].end(B * (n_experts - 1))
    s["w_hi"].end(2 * n_experts)
    s["w_lo"].end(n_experts)
    s["w_split"].end(n_experts)
    for q in range(2):
        s[f"load{q}"].end(w_load * ((n_experts + 1 - q) // 2))
        s[f"comb{q}"].end(16 * ((n_experts + 1 - q) // 2))
        if b1_name:
            s[f"bias{q}"].end(16 * ((n_experts + 1 - q) // 2))


def linear_chain_phase(nc, g):
    s = g.s
    with g.sb("chain", [P, 3, B, T], F32) as mid, \
         g.pb("chain_ps", [P, 2, B, T], F32) as ps, \
         nc.Block() as block:

        @block.tensor
        def _(pe):
            for k, w in enumerate(("L2_f0", "L2_f1", "L2_f2")):
                for c in range(B):
                    if k:
                        pe.wait_ge(s["evac"].sem, s["evac"].at(B * (k - 1) + c + 1))
                    nc.tensor.matmul(ps[:, k % 2, c], g.square(w), g.hT[:, cols(c)] if k == 0 else mid[:, k - 1, c],
                                     start=True, stop=True).then_inc(s["mm"].sem, 1)

        @block.scalar
        def _(act):
            for k in range(3):
                for c in range(B):
                    act.wait_ge(s["mm"].sem, s["mm"].at(B * k + c + 1))
                    if k < 2:
                        nc.scalar.activation(mid[:, k, c], ps[:, k % 2, c], ACT.Copy).then_inc(s["evac"].sem, 1)
                    else:
                        nc.scalar.activation(mid[:, k, c], ps[:, k % 2, c], ACT.Tanh, bias=g.col("L2_bias")
                                             ).then_inc(s["act"].sem, 1)

        @block.vector
        def _(dve):
            for c in range(B):
                dve.wait_ge(s["act"].sem, s["act"].at(c + 1))
                nc.vector.scalar_tensor_tensor(g.xT[:, cols(c)], mid[:, 2, c], g.mod[:, 2, GATE_B, c:c + 1],
                                               g.xT[:, cols(c)], ALU.mult, ALU.add).then_inc(s["vec"].sem, 1)

    s["mm"].end(3 * B)
    s["evac"].end(2 * B)
    s["act"].end(B)
    s["vec"].end(B)


def head_rms_phase(nc, g):
    s = g.s
    heads, d = 16, 8
    src = by_part(g.att_tok, 2)
    with g.sb("sq", [P, N], F32) as sq, \
         g.sb("ms", [P, N // d], F32) as ms, \
         g.sb("ordered", [P, N], F32) as ordered, \
         nc.Block() as block:

        @block.scalar
        def _(act):
            nc.scalar.activation(sq[:], g.att_tok[:], ACT.Square).then_inc(s["act"].sem, 1)
            act.wait_ge(s["vec"].sem, s["vec"].at(1))
            nc.scalar.activation(ms[:], ms[:], ACT.Sqrt, bias=g.eps[:, 0:1], scale=1.0 / d).then_inc(s["act"].sem, 1)

        @block.vector
        def _(dve):
            dve.wait_ge(s["act"].sem, s["act"].at(1))
            nc.vector.tensor_reduce(ms[:], sq[:].rearrange("p (h d) -> p h d", d=d), X, ALU.add
                                    ).then_inc(s["vec"].sem, 1)
            nc.vector.tensor_scalar(g.wo2[:], g.square("L2_Wo"), g.rms_w[:], None, ALU.mult
                                    ).then_inc(s["vec"].sem, 1)
            dve.wait_ge(s["act"].sem, s["act"].at(2))
            nc.vector.reciprocal(ms[:], ms[:]).then_inc(s["vec"].sem, 1)
            dve.wait_ge(s["vec"].sem, s["vec"].at(3))
            nc.vector.tensor_tensor(ordered[:].rearrange("p (h d) -> p h d", d=d),
                                    g.att_tok[:].rearrange("p (h d) -> p h d", d=d),
                                    ms[:].unsqueeze(2).broadcast_to([P, N // d, d]), ALU.mult
                                    ).then_inc(s["vec"].sem, 1)
            dve.wait_ge(s["vec"].sem, s["vec"].at(4))
            w = P // 2
            back = g.att_tok[:].rearrange("p (b t i w) -> p b i t w", b=B, i=2, w=w)
            o = ordered[:].rearrange("p (b i t w) -> p b i t w", b=B, i=2, w=w)
            for b in range(B):
                nc.vector.tensor_copy(back[:, b], o[:, b]).then_inc(s["vec"].sem, 1)

    s["act"].end(2)
    s["vec"].end(4 + B)


def alibi_attention(nc, g):
    s = g.s
    HEADS, HD = 16, 64
    NU = HEADS * B
    BODY = 8
    KT = T // P
    ALIBI_ROW = 64
    OUT = HD + 1
    with g.sb("w_head", [P, 2, 4, HD], F32) as w_raw, \
         g.sb("w_head_parts", [P, 2, 2, 4, HD], F32R) as wh, \
         g.sb("w_values", [P, 2 * HD], F32) as wv, \
         g.sb("h_parts", [P, 2, N], F32R) as hp, \
         g.sb("qa", [P, 4, T], F32R) as qa, \
         g.sb("qb", [P, 4, T], F32R) as qb, \
         g.sb("ka", [P, 4, T], F32R) as ka, \
         g.sb("kb", [P, 4, T], F32R) as kb, \
         g.sb("v_one", [P, 2, B, KT, OUT], F32) as vo, \
         g.sb("probs", [P, 2, KT, T], F32) as probs, \
         g.sb("neg_max", [P, 2, KT], F32) as neg_max, \
         g.sb("max_parts", [KT, 2, 2, P], F32) as max_parts, \
         g.sb("recip", [P, KT], F32) as recip, \
         g.sb("mask", [P, 3, P], BF16) as mask, \
         g.pb("proj", [P, 2, T], F32) as pj, \
         g.pb("scores", [P, 2, T], F32) as sc_ps, \
         g.pb("scoresT", [P, 2, T], F32) as st_ps, \
         g.pb("values", [P, T], F32) as o_ps, \
         g.pb("maxT", [P, T], F32) as mt_ps, \
         nc.Block() as block:
        f32 = lambda ap: ap.bitcast(F32)
        identity, above, below = mask[:, 0], mask[:, 1], mask[:, 2]

        def bank(gp, c):
            return (2 * gp + min(gp, B) + c) % 2

        def unit(i, p, d=0):
            i, p = i + (p + d) // BODY, (p + d) % BODY
            if isinstance(i, int) and not 0 <= BODY * i + p < NU:
                return None
            return i, p, i * BODY + p

        def steps(eng, step):
            for i in (-1, 0):
                for p in range(BODY):
                    step(i, p)
            with eng.Fori(1, NU // BODY - 1) as i:
                for p in range(BODY):
                    step(i, p)
            for i in (NU // BODY - 1, NU // BODY):
                for p in range(BODY):
                    step(i, p)

        @block.sync
        def _(sp):
            sp.dma_start(mask[:], g.dram["mask"]).then_inc(s["dma"].sem, 16)

            def step(i, p):
                if (at := unit(i, p, 7)) and at[1] % 4 == 0:
                    gi, gp, n = at
                    q = gp // 4
                    sp.wait_ge(s["w_split"].sem, s["w_split"].at(gi * 2 + q - 1))
                    sp.dma_start(w_raw[:, q], g.dram["L1_wqk"][bass.ds(gi * 2 + q, 1)]
                                 .rearrange("o p c d -> (o p) c d")).then_inc(s[f"load{q}"].sem, 16)
                if (at := unit(i, p, 4)) and at[1] == 0:
                    gi, gp, n = at
                    sp.wait_ge(s["v_mm"].sem, s["v_mm"].at(B * gi))
                    sp.dma_start(wv[:], g.dram["L1_wv"][bass.ds(gi, 1)].rearrange("o p d -> (o p) d")
                                 ).then_inc(s["load_v"].sem, 16)
                if at := unit(i, p, 3):
                    gi, gp, n = at
                    sp.wait_ge(s["zeros"].sem, s["zeros"].at(3))
                    sp.wait_ge(s["ones"].sem, s["ones"].at(3))
                    sp.wait_ge(s["st"].sem, s["st"].at(KT * (n - 3)))
                    sp.dma_start(f32(kb[ALIBI_ROW:ALIBI_ROW + 2, gp % 4]),
                                 g.scratch["alibi"][bass.ds(gi * 2 + gp // 4, 1)].rearrange("o r t -> (o r) t")
                                 ).then_inc(s[f"alibi{gp % 4}"].sem, 16)
                if at := unit(i, p, 1):
                    gi, gp, n = at
                    sp.wait_ge(s["max_split"].sem, s["max_split"].at(n + 1))
                    for r in range(2):
                        row = slice(MAX_ROW + r, MAX_ROW + r + 1)
                        sp.dma_start(f32(qb[row, gp % 4]).rearrange("o (t q) -> o t q", t=KT),
                                     max_parts[:, gp % 2, r]).then_inc(s[f"rows{gp % 2}"].sem, 16)

            steps(sp, step)

        @block.gpsimd
        def _(pool):
            nc.gpsimd.memset(vo[:], 1.0).then_inc(s["ones"].sem, 1)
            pool.wait_ge(s["ones"].sem, s["ones"].at(1))
            nc.gpsimd.memset(f32(kb[HD:P]), 0.0).then_inc(s["ones"].sem, 1)
            pool.wait_ge(s["ones"].sem, s["ones"].at(2))
            nc.gpsimd.memset(f32(kb[MAX_ROW:MAX_ROW + 2]), 1.0).then_inc(s["ones"].sem, 1)
            pool.wait_ge(s["ones"].sem, s["ones"].at(3))

            def step(i, p):
                if (at := unit(i, p, 5)) and at[1] % 4 == 0:
                    gi, gp, n = at
                    q = gp // 4
                    pool.wait_ge(s["w_hi"].sem, s["w_hi"].at(gi * 2 + q + 1))
                    nc.gpsimd.tensor_tensor(wh[:, q, 1], w_raw[:, q], f32(wh[:, q, 0]), ALU.subtract
                                            ).then_inc(s["w_split"].sem, 1)
                if at := unit(i, p, 3):
                    _, gp, n = at
                    pool.wait_ge(s["hi"].sem, s["hi"].at(2 * n + 2))
                    pool.wait_ge(s["st"].sem, s["st"].at(KT * (n - 3)))
                    nc.gpsimd.tensor_tensor(kb[0:HD, gp % 4], f32(ka[0:HD, gp % 4]),
                                            g.all_ones[0:HD, 0:1].broadcast_to([HD, T]), ALU.mult).then_inc(s["kb"].sem, 1)

            steps(pool, step)

        @block.scalar
        def _(act):
            for c in range(B):
                nc.scalar.activation(hp[:, 0, cols(c)], g.hT[:, cols(c)], ACT.Copy).then_inc(s["h_hi"].sem, 1)

            def step(i, p):
                cur, new = unit(i, p), unit(i, p, 3)
                for kt in range(KT):
                    if cur:
                        _, gp, n = cur
                        if kt == 0:
                            act.wait_ge(s["pv"].sem, s["pv"].at(n - 1))
                        act.wait_ge(s["st"].sem, s["st"].at(KT * n + kt + 1))
                        nc.scalar.activation(probs[:, gp % 2, kt, kt * P:T], st_ps[:, kt % 2, kt * P:T],
                                             ACT.Exp, scale=HD ** -0.5).then_inc(s["exp"].sem, 1)
                    if new:
                        _, gp, n = new
                        b = gp % 4
                        if kt == 0:
                            act.wait_ge(s["st"].sem, s["st"].at(KT * (n - 3)))
                            act.wait_ge(s["mm"].sem, s["mm"].at(2 * n + 1))
                            nc.scalar.activation(qa[:, b], pj[:, bank(gp, 0)], ACT.Copy).then_inc(s["hi"].sem, 1)
                        elif kt == 1:
                            act.wait_ge(s["mm"].sem, s["mm"].at(2 * n + 2))
                            nc.scalar.activation(ka[:, b], pj[:, bank(gp, 1)], ACT.Copy
                                                 ).then_inc(s["hi"].sem, 1)
                        elif kt == 3 and gp < B:
                            act.wait_ge(s["v_mm"].sem, s["v_mm"].at(new[0] * B + gp + 1))
                            act.wait_ge(s["ones"].sem, s["ones"].at(3))
                            act.wait_ge(s["pv"].sem, s["pv"].at(n - 3))
                            nc.scalar.activation(
                                vo[:, :, gp, :, 0:HD],
                                pj[:, bank(gp, 2)].rearrange("p (t h d) -> p h t d", h=2, d=HD), ACT.Copy
                            ).then_inc(s["vg"].sem, 1)

            steps(act, step)

        @block.vector
        def _(dve):
            nc.vector.memset(f32(qb[HD:P]), 0.0).then_inc(s["zeros"].sem, 1)
            nc.vector.memset(f32(neg_max[:]), 0.0).then_inc(s["zeros"].sem, 1)
            dve.wait_ge(s["zeros"].sem, s["zeros"].at(2))
            nc.vector.memset(f32(qb[ALIBI_ROW:ALIBI_ROW + 2]), 1.0).then_inc(s["zeros"].sem, 1)
            for c in range(B):
                dve.wait_ge(s["h_hi"].sem, s["h_hi"].at(c + 1))
                nc.vector.tensor_tensor(hp[:, 1, cols(c)], g.hT[:, cols(c)], f32(hp[:, 0, cols(c)]),
                                        ALU.subtract).then_inc(s["split"].sem, 1)

            def step(i, p):
                ahead, next_, new, last = unit(i, p, 2), unit(i, p, 1), unit(i, p, 3), unit(i, p, -2)
                if last:
                    gi, gp, n = last
                    o = o_ps[:, 0:KT * OUT].rearrange("p (t d) -> p t d", d=OUT)
                    dve.wait_ge(s["pv"].sem, s["pv"].at(n + 1))
                    nc.vector.reciprocal(recip[:], o[:, :, HD]).then_inc(s["recip"].sem, 1)
                    dve.wait_ge(s["recip"].sem, s["recip"].at(n + 1))
                    out = g.att1[:, (gp % 4) * KT:(gp % 4) * KT + KT, bass.ds((gi * 2 + gp // 4) * HD, HD)]
                    nc.vector.tensor_tensor(out, o[:, :, 0:HD], recip[:].unsqueeze(2).broadcast_to([P, KT, HD]),
                                            ALU.mult).then_inc(s["divide"].sem, 1)
                if (at := unit(i, p, 5)) and at[1] % 4 == 0:
                    gi, gp, n = at
                    q = gp // 4
                    dve.wait_ge(s[f"load{q}"].sem, s[f"load{q}"].at(gi * 16 + 16))
                    dve.wait_ge(s["mm"].sem, s["mm"].at(2 * (n - 4)))
                    nc.vector.tensor_copy(wh[:, q, 0], w_raw[:, q]).then_inc(s["w_hi"].sem, 1)
                for qt in range(KT):
                    if ahead:
                        _, gp, n = ahead
                        if qt == 0:
                            dve.wait_ge(s["maxT"].sem, s["maxT"].at(n - 1))
                        dve.wait_ge(s["scores"].sem, s["scores"].at(KT * n + qt + 1))
                        nc.vector.tensor_reduce(neg_max[:, gp % 2, qt:qt + 1], sc_ps[:, qt % 2, 0:(qt + 1) * P],
                                                X, ALU.max, negate=True).then_inc(s["max"].sem, 1)
                    if qt == 0 and next_:
                        gi, gp, n = next_
                        dve.wait_ge(s["maxT"].sem, s["maxT"].at(n + 1))
                        dve.wait_ge(s[f"rows{gp % 2}"].sem, s[f"rows{gp % 2}"].at(gi * 128 + 32 * (gp // 2)))
                        nc.vector.tensor_copy(max_parts[:, gp % 2, 0].bitcast(F32R), mt_ps[0:KT, 0:P]
                                              ).then_inc(s["max_hi"].sem, 1)
                        dve.wait_ge(s["max_hi"].sem, s["max_hi"].at(n + 1))
                        nc.vector.tensor_tensor(max_parts[:, gp % 2, 1], mt_ps[0:KT, 0:P],
                                                max_parts[:, gp % 2, 0], ALU.subtract
                                                ).then_inc(s["max_split"].sem, 1)
                    if new and qt in (0, 1):
                        _, gp, n = new
                        b = gp % 4
                        dve.wait_ge(s["hi"].sem, s["hi"].at(2 * n + qt + 1))
                        if qt == 0:
                            nc.vector.tensor_tensor(qb[0:HD, b], pj[0:HD, bank(gp, 0)], f32(qa[0:HD, b]),
                                                    ALU.subtract).then_inc(s["lo"].sem, 1)
                        else:
                            nc.vector.tensor_tensor(ka[HD:P, b], pj[HD:P, bank(gp, 1)], f32(ka[HD:P, b]),
                                                    ALU.subtract).then_inc(s["lo"].sem, 1)

            steps(dve, step)

        @block.tensor
        def _(pe):
            def project(at, c):
                gi, gp, n = at
                b, q = gp % 4, gp // 4
                if c == 0:
                    pe.wait_ge(s["w_split"].sem, s["w_split"].at(gi * 2 + q + 1))
                    pe.wait_ge(s["lo"].sem, s["lo"].at(2 * n))
                if c == 1:
                    pe.wait_ge(s["vg"].sem, s["vg"].at(gi * B + min(gp, B)))
                if c == 2:
                    pe.wait_ge(s["load_v"].sem, s["load_v"].at(gi * 16 + 16))
                    pe.wait_ge(s["lo"].sem, s["lo"].at(2 * n + 1))
                if c < 2:
                    for w_part, h_part in PASSES:
                        mm = nc.tensor.matmul(pj[:, bank(gp, c)],
                                              wh[:, q, w_part, 2 * c:2 * c + 2].rearrange("p c d -> p (c d)"),
                                              hp[:, h_part, cols(b)], start=w_part + h_part == 0, stop=w_part == 1)
                    mm.then_inc(s["mm"].sem, 1)
                else:
                    for t in range(KT):
                        at_ = b * T + t * P
                        mm = nc.tensor.matmul(pj[:, bank(gp, 2), t * P:(t + 1) * P], g.hT[:, at_:at_ + P], wv[:],
                                              start=True, stop=True)
                    mm.then_inc(s["v_mm"].sem, 1)

            def scores(at, qt):
                gi, gp, n = at
                b, w = gp % 4, (qt + 1) * P
                tile, row = slice(qt * P, w), slice(0, MAX_ROW)
                pe.wait_ge(s["max"].sem, s["max"].at(KT * n + qt - 1))
                nc.tensor.matmul(sc_ps[:, qt % 2, 0:w], qa[:, b, tile], ka[:, b, 0:w], start=True, stop=False)
                nc.tensor.matmul(sc_ps[:, qt % 2, 0:w], qb[row, b, tile], kb[row, b, 0:w], start=False, stop=False)
                nc.tensor.matmul(sc_ps[:, qt % 2, tile], identity, above, start=False, stop=True
                                 ).then_inc(s["scores"].sem, 1)

            def scores_t(at, kt):
                gi, gp, n = at
                b, tile, right = gp % 4, slice(kt * P, (kt + 1) * P), slice(kt * P, T)
                pe.wait_ge(s["exp"].sem, s["exp"].at(KT * n + kt - 1))
                nc.tensor.matmul(st_ps[:, kt % 2, right], ka[:, b, tile], qa[:, b, right], start=True, stop=False)
                nc.tensor.matmul(st_ps[:, kt % 2, right], kb[:, b, tile], qb[:, b, right], start=False, stop=False)
                nc.tensor.matmul(st_ps[:, kt % 2, tile], identity, below, start=False, stop=True
                                 ).then_inc(s["st"].sem, 1)

            def values(at, qt):
                gi, gp, n = at
                if qt == 0:
                    pe.wait_ge(s["divide"].sem, s["divide"].at(n))
                    pe.wait_ge(s["exp"].sem, s["exp"].at(KT * (n + 1)))
                for kt in range(qt + 1):
                    mm = nc.tensor.matmul(o_ps[:, qt * OUT:(qt + 1) * OUT],
                                          probs[:, gp % 2, kt, qt * P:(qt + 1) * P], vo[:, gp // B, gp % B, kt],
                                          start=kt == 0, stop=kt == qt)
                if qt == KT - 1:
                    mm.then_inc(s["pv"].sem, 1)

            pe.wait_ge(s["dma"].sem, s["dma"].at(16))
            pe.wait_ge(s["split"].sem, s["split"].at(B))

            def step(i, p):
                cur, ahead, next_ = unit(i, p), unit(i, p, 2), unit(i, p, 1)
                new, before = unit(i, p, 3), unit(i, p, -1)
                if cur:
                    gi, gp, n = cur
                    pe.wait_ge(s[f"rows{gp % 2}"].sem, s[f"rows{gp % 2}"].at(gi * 128 + 32 * (gp // 2) + 32))
                if ahead:
                    gi, gp, n = ahead
                    pe.wait_ge(s["kb"].sem, s["kb"].at(n + 1))
                    pe.wait_ge(s["lo"].sem, s["lo"].at(2 * n + 2))
                    pe.wait_ge(s[f"alibi{gp % 4}"].sem, s[f"alibi{gp % 4}"].at(gi * 32 + 16 * (gp // 4) + 16))
                for k in range(KT):
                    if cur:
                        scores_t(cur, k)
                    if ahead:
                        scores(ahead, k)
                    if k > 0 and before:
                        if k == 1:
                            values(before, 0)
                        values(before, k)
                    if k == 0 and next_:
                        gi, gp, n = next_
                        pe.wait_ge(s["max"].sem, s["max"].at(KT * (n + 1)))
                        pe.wait_ge(s["max_split"].sem, s["max_split"].at(n))
                        nc.tensor.transpose(mt_ps[0:KT, 0:P], neg_max[:, gp % 2], g.identity
                                            ).then_inc(s["maxT"].sem, 1)
                    if new and k != 2 and (k < 2 or new[1] < B):
                        project(new, min(k, 2))

            steps(pe, step)

    s["dma"].end(16)
    s["mm"].end(2 * NU)
    s["v_mm"].end(NU // 2)
    s["load_v"].end(16 * HEADS // 2)
    s["vg"].end(NU // 2)
    for q in range(2):
        s[f"load{q}"].end(16 * HEADS // 2)
        s[f"rows{q}"].end(32 * NU // 2)
    for b in range(B):
        s[f"alibi{b}"].end(16 * HEADS)
    s["zeros"].end(3)
    s["h_hi"].end(B)
    s["split"].end(B)
    s["w_hi"].end(HEADS)
    s["w_split"].end(HEADS)
    s["ones"].end(3)
    s["hi"].end(2 * NU)
    s["lo"].end(2 * NU)
    for name in ("kb", "pv", "maxT", "max_hi", "max_split", "recip", "divide"):
        s[name].end(NU)
    for name in ("scores", "st", "max", "exp"):
        s[name].end(KT * NU)


def alibi_output(nc, g):
    s = g.s
    KD = 8
    with g.sb("w_out", [P, KD, P], F32) as wo, \
         g.sb("attn", [P, 4, T], F32) as attn, \
         g.sb("update", [P, B, T], F32) as upd, \
         g.pb("turn_ps", [P, 4, T], F32) as turn_ps, \
         g.pb("out_ps", [P, B, T], F32) as ps, \
         nc.Block() as block:
        tiles = [(b, k) for b in range(B) for k in range(KD)]

        @block.sync
        def _(sp):
            sp.dma_start(wo[:], g.dram["L1_wout"]).then_inc(s["dma"].sem, 16)

        @block.tensor
        def _(pe):
            def turn(n):
                b, k = tiles[n]
                if n >= 4:
                    pe.wait_ge(s["evac"].sem, s["evac"].at(n - 3))
                for t in range(T // P):
                    mm = nc.tensor.transpose(turn_ps[:, n % 4, t * P:(t + 1) * P],
                                             g.att1[:, b * (T // P) + t, k * P:(k + 1) * P], g.identity)
                mm.then_inc(s["rawT"].sem, 1)

            pe.wait_ge(s["dma"].sem, s["dma"].at(16))
            turn(0)
            turn(1)
            for n, (b, k) in enumerate(tiles):
                if n + 2 < len(tiles):
                    turn(n + 2)
                pe.wait_ge(s["evac"].sem, s["evac"].at(n + 1))
                nc.tensor.matmul(ps[:, b], wo[:, k], attn[:, n % 4], start=k == 0, stop=k == KD - 1
                                 ).then_inc(s["mm"].sem, 1)

        @block.scalar
        def _(act):
            for n in range(len(tiles)):
                act.wait_ge(s["rawT"].sem, s["rawT"].at(n + 1))
                act.wait_ge(s["mm"].sem, s["mm"].at(n - 3))
                nc.scalar.activation(attn[:, n % 4], turn_ps[:, n % 4], ACT.Copy).then_inc(s["evac"].sem, 1)
            for b in range(B):
                act.wait_ge(s["mm"].sem, s["mm"].at(KD * (b + 1)))
                nc.scalar.activation(upd[:, b], ps[:, b], ACT.Identity, bias=g.gate_bias[:, 1, b:b + 1],
                                     scale=g.mod[:, 1, GATE_A, b:b + 1]).then_inc(s["act"].sem, 1)

        @block.vector
        def _(dve):
            for b in range(B):
                dve.wait_ge(s["act"].sem, s["act"].at(b + 1))
                nc.vector.tensor_tensor(g.xT[:, cols(b)], g.xT[:, cols(b)], upd[:, b], ALU.add
                                        ).then_inc(s["vec"].sem, 1)

    s["dma"].end(16)
    for name in ("rawT", "evac", "mm"):
        s[name].end(B * KD)
    s["act"].end(B)
    s["vec"].end(B)


def linear_attention(nc, g):
    s = g.s
    HG, KT = 4, T // P
    OUT = 9
    pm = g.l3_w[:, 0]
    with g.sb("q_k", [P, 2, 2, T], F32) as qk, \
         g.sb("v_one", [P, 2, KT, 16, OUT], F32) as vo, \
         g.sb("expd", [P, 4, T], F32) as ex, \
         g.sb("features", [P, 16, T], F32) as feat, \
         g.sb("kv", [P, 2, HG, 4, OUT], F32) as kv, \
         g.sb("kv_mask", [P, 4, OUT], F32) as kv_mask, \
         g.sb("recip", [P, 2, KT, 16], F32) as recip, \
         g.pb("proj", [P, T], F32) as pj, \
         g.pb("feat_ps", [P, 4, T], F32) as f_ps, \
         g.pb("kv_ps", [P, HG, P], F32) as kv_ps, \
         g.pb("out_ps", [P, KT, 2 * P], F32) as o_ps, \
         nc.Block() as block:
        F = 2 * 4

        @block.sync
        def _(sp):
            sp.dma_start(kv_mask[:], g.dram["kv_mask"]).then_inc(s["dma"].sem, 16)

        @block.tensor
        def _(pe):
            def project(b, c):
                pe.wait_ge(s["evac"].sem, s["evac"].at(3 * b + c))
                if c < 2:
                    nc.tensor.matmul(pj[:], g.square(("L3_Wq", "L3_Wk")[c]), g.hT[:, cols(b)],
                                     start=True, stop=True).then_inc(s["mm"].sem, 1)
                else:
                    for t in range(KT):
                        at = b * T + t * P
                        mm = nc.tensor.matmul(pj[:, t * P:(t + 1) * P], g.hT[:, at:at + P], g.square("L3_Wv"),
                                              start=True, stop=True)
                    mm.then_inc(s["mm"].sem, 1)

            for c in range(3):
                project(0, c)
            for b in range(B + 1):
                for f in range(F):
                    if b < B:
                        n = F * b + f
                        if f == 0:
                            pe.wait_ge(s["evac"].sem, s["evac"].at(3 * (b + 1)))
                        pe.wait_ge(s["feat"].sem, s["feat"].at(n - 3))
                        if f < 4:
                            nc.tensor.matmul(f_ps[:, n % 4], qk[:, b % 2, 1, f * P:(f + 1) * P], pm,
                                             start=True, stop=True).then_inc(s["up"].sem, 1)
                        else:
                            nc.tensor.matmul(f_ps[:, n % 4], pm[:, (f - 4) * P:(f - 3) * P], qk[:, b % 2, 0],
                                             start=True, stop=True).then_inc(s["up"].sem, 1)
                    if b > 0 and f < 2:
                        pe.wait_ge(s["feat"].sem, s["feat"].at(F * (b - 1) + KT))
                        pe.wait_ge(s["kb"].sem, s["kb"].at(b - 1))
                        for hg in (2 * f, 2 * f + 1):
                            for t in range(KT):
                                mm = nc.tensor.matmul(
                                    kv_ps[:, hg, 0:4 * OUT], feat[:, 8 * ((b - 1) % 2) + t, hg * P:(hg + 1) * P],
                                    vo[:, (b - 1) % 2, t, 4 * hg:4 * hg + 4].rearrange("p j d -> p (j d)"),
                                    start=t == 0, stop=t == KT - 1)
                        if f == 1:
                            mm.then_inc(s["pv"].sem, 1)
                    elif b > 0 and f >= HG:
                        t = f - HG
                        pe.wait_ge(s["feat"].sem, s["feat"].at(F * b))
                        pe.wait_ge(s["kb"].sem, s["kb"].at(b))
                        pe.wait_ge(s["divide"].sem, s["divide"].at(b - 1))
                        for hg in range(HG):
                            mm = nc.tensor.matmul(
                                o_ps[:, t, hg * 4 * OUT:(hg + 1) * 4 * OUT],
                                feat[:, 8 * ((b - 1) % 2) + KT + hg, t * P:(t + 1) * P],
                                kv[:, (b - 1) % 2, hg].rearrange("p j d -> p (j d)"), start=True, stop=True)
                        if t == KT - 1:
                            mm.then_inc(s["down"].sem, 1)
                    if b + 1 < B and f in (1, 3, 5):
                        project(b + 1, f // 2)

        @block.scalar
        def _(act):
            def evacuate(b, c):
                act.wait_ge(s["mm"].sem, s["mm"].at(3 * b + c + 1))
                if c < 2:
                    act.wait_ge(s["up"].sem, s["up"].at(F * (b - 1)))
                    nc.scalar.activation(qk[:, b % 2, c], pj[:], ACT.Copy).then_inc(s["evac"].sem, 1)
                else:
                    act.wait_ge(s["ones"].sem, s["ones"].at(1))
                    act.wait_ge(s["pv"].sem, s["pv"].at(b - 1))
                    nc.scalar.activation(vo[:, b % 2, :, :, 0:8],
                                         pj[:].rearrange("p (t h d) -> p t h d", h=16, d=8), ACT.Copy
                                         ).then_inc(s["evac"].sem, 1)

            for c in range(3):
                evacuate(0, c)
            for b in range(B):
                for f in range(F):
                    n = F * b + f
                    act.wait_ge(s["clip"].sem, s["clip"].at(n + 1))
                    nc.scalar.activation(ex[:, n % 4], ex[:, n % 4], ACT.Exp).then_inc(s["exp"].sem, 1)
                    if b + 1 < B and f in (1, 3, 5):
                        evacuate(b + 1, f // 2)

        @block.gpsimd
        def _(pool):
            nc.gpsimd.memset(vo[:], 1.0).then_inc(s["ones"].sem, 1)

        @block.vector
        def _(dve):
            dve.wait_ge(s["dma"].sem, s["dma"].at(16))
            def mask(b):
                dve.wait_ge(s["pv"].sem, s["pv"].at(b + 1))
                nc.vector.tensor_tensor(kv[:, b % 2], kv_mask[:].unsqueeze(1).broadcast_to([P, HG, 4, OUT]),
                                        kv_ps[:, :, 0:4 * OUT].rearrange("p g (j d) -> p g j d", d=OUT),
                                        ALU.mult).then_inc(s["kb"].sem, 1)

            def divide(b):
                o = o_ps[:, :, 0:16 * OUT].rearrange("p t (h d) -> p t h d", d=OUT)
                dve.wait_ge(s["down"].sem, s["down"].at(b + 1))
                nc.vector.tensor_scalar(recip[:, 0], o[:, :, :, 8], 1e-8, None, ALU.add
                                        ).then_inc(s["recip"].sem, 1)
                dve.wait_ge(s["recip"].sem, s["recip"].at(2 * b + 1))
                nc.vector.reciprocal(recip[:, 1], recip[:, 0]).then_inc(s["recip"].sem, 1)
                dve.wait_ge(s["recip"].sem, s["recip"].at(2 * b + 2))
                for t in range(KT):
                    done = s["divide"] if t == KT - 1 else s["vec"]
                    nc.vector.tensor_tensor(
                        g.att_tok[:].rearrange("p (n h d) -> p n h d", h=16, d=8)[:, b * KT + t],
                        o[:, t, :, 0:8], recip[:, 1, t].unsqueeze(2).broadcast_to([P, 16, 8]), ALU.mult
                    ).then_inc(done.sem, 1)

            for b in range(B + 1):
                for f in range(F + 1):
                    n = F * b + f
                    if f < F and b < B:
                        dve.wait_ge(s["up"].sem, s["up"].at(n + 1))
                        dve.wait_ge(s["feat"].sem, s["feat"].at(n - 3))
                        nc.vector.tensor_scalar(ex[:, n % 4], f_ps[:, n % 4], 0.0, None, ALU.min
                                                ).then_inc(s["clip"].sem, 1)
                    if f and b < B:
                        dve.wait_ge(s["exp"].sem, s["exp"].at(n))
                        dve.wait_ge(s["down"].sem, s["down"].at(b - 1))
                        nc.vector.scalar_tensor_tensor(feat[:, 8 * (b % 2) + f - 1], f_ps[:, (n - 1) % 4], 0.0,
                                                       ex[:, (n - 1) % 4], ALU.max, ALU.add
                                                       ).then_inc(s["feat"].sem, 1)
                    if b > 0 and f == HG - 1:
                        mask(b - 1)
                if b > 0:
                    divide(b - 1)

    s["dma"].end(16)
    s["mm"].end(3 * B)
    s["evac"].end(3 * B)
    for name in ("up", "exp", "clip", "feat"):
        s[name].end(F * B)
    for name in ("kb", "pv", "down", "divide"):
        s[name].end(B)
    s["recip"].end(2 * B)
    s["vec"].end(3 * B)
    s["ones"].end(1)


def residual_output(nc, g):
    s = g.s
    att = g.att_tok[:].rearrange("p (n d) -> p n d", d=P)
    with g.sb("attn", [P, B, T], F32) as attn, \
         g.pb("turn_ps", [P, B, T], F32) as turn_ps, \
         g.pb("out_ps", [P, B, T], F32) as ps, \
         nc.Block() as block:

        @block.tensor
        def _(pe):
            for b in range(B):
                for t in range(T // P):
                    mm = nc.tensor.transpose(turn_ps[:, b, t * P:(t + 1) * P], att[:, b * (T // P) + t],
                                             g.identity)
                mm.then_inc(s["rawT"].sem, 1)
            for b in range(B):
                pe.wait_ge(s["evac"].sem, s["evac"].at(b + 1))
                nc.tensor.matmul(ps[:, b], g.square("L3_Wo"), attn[:, b], start=True, stop=True
                                 ).then_inc(s["mm"].sem, 1)

        @block.scalar
        def _(act):
            for b in range(B):
                act.wait_ge(s["rawT"].sem, s["rawT"].at(b + 1))
                nc.scalar.activation(attn[:, b], turn_ps[:, b], ACT.Copy).then_inc(s["evac"].sem, 1)

        @block.vector
        def _(dve):
            for b in range(B):
                dve.wait_ge(s["mm"].sem, s["mm"].at(b + 1))
                nc.vector.scalar_tensor_tensor(g.hT[:, cols(b)], ps[:, b], g.col("L3_bo"), g.hT[:, cols(b)],
                                               ALU.add, ALU.add).then_inc(s["vec"].sem, 1)

    for name in ("rawT", "evac", "mm", "vec"):
        s[name].end(B)


def gelu_ffn(nc, g):
    s = g.s
    FT = 4
    w1, w2 = g.l3_w[:, 1], g.l3_w[:, 2].rearrange("p (t d) -> p t d", t=FT)
    with g.sb("hidden", [P, 2, FT, T], F32) as hid, \
         g.pb("up_ps", [P, 4, T], F32) as up_ps, \
         g.pb("down_ps", [P, 2, T], F32) as dn_ps, \
         nc.Block() as block:

        @block.tensor
        def _(pe):
            def up(c):
                for t in range(FT):
                    pe.wait_ge(s["hidden"].sem, s["hidden"].at(FT * (c - 1) + t + 1))
                    nc.tensor.matmul(up_ps[:, t], w1[:, t * P:(t + 1) * P], g.hT[:, cols(c)],
                                     start=True, stop=True).then_inc(s["up"].sem, 1)

            up(0)
            for c in range(B):
                if c + 1 < B:
                    up(c + 1)
                pe.wait_ge(s["hidden"].sem, s["hidden"].at(FT * (c + 1)))
                pe.wait_ge(s["vec"].sem, s["vec"].at(c - 1))
                for t in range(FT):
                    mm = nc.tensor.matmul(dn_ps[:, c % 2], w2[:, t], hid[:, c % 2, t], start=t == 0,
                                          stop=t == FT - 1)
                mm.then_inc(s["down"].sem, 1)

        @block.scalar
        def _(act):
            for c in range(B):
                act.wait_ge(s["down"].sem, s["down"].at(c - 1))
                for t in range(FT):
                    act.wait_ge(s["up"].sem, s["up"].at(FT * c + t + 1))
                    nc.scalar.activation(hid[:, c % 2, t], up_ps[:, t], ACT.Gelu, bias=g.col(f"L3_b1_{t}")
                                         ).then_inc(s["hidden"].sem, 1)

        @block.vector
        def _(dve):
            for c in range(B):
                dve.wait_ge(s["down"].sem, s["down"].at(c + 1))
                nc.vector.scalar_tensor_tensor(g.hT[:, cols(c)], dn_ps[:, c % 2], g.col("L3_b2"), g.hT[:, cols(c)],
                                               ALU.add, ALU.add).then_inc(s["vec"].sem, 1)

    s["up"].end(B * FT)
    s["hidden"].end(B * FT)
    s["down"].end(B)
    s["vec"].end(B)


def gated_add(nc, g, layer, gate):
    s = g.s
    with nc.Block() as block:
        @block.vector
        def _(dve):
            for c in range(B):
                nc.vector.scalar_tensor_tensor(g.xT[:, cols(c)], g.hT[:, cols(c)], g.mod[:, layer, gate, c:c + 1],
                                               g.xT[:, cols(c)], ALU.mult, ALU.add).then_inc(s["vec"].sem, 1)
    s["vec"].end(B)


class Program:

    def __init__(self, nc):
        self.nc, self.count = nc, 0

    def sb(self, name, shape, dtype):
        self.count += 1
        return self.nc.sbuf_tensor(f"{name}_{self.count}", shape, dtype)

    def pb(self, name, shape, dtype):
        self.count += 1
        return self.nc.psum_tensor(f"{name}_{self.count}", shape, dtype)


def build(nc, dram, debug=None):
    g = Program(nc)
    g.dram = dram
    names = ["dma", "vec", "act", "pe", "pool", "mean", "square", "var", "centre", "std", "norm", "mm",
             "evac", "split", "store", "scores", "st", "max", "exp", "max_split", "max_hi", "maxT", "raw",
             "rawT", "divide", "pv", "vg", "ones", "zeros"]
    names += [f"load{p}" for p in range(4)] + [f"rows{q}" for q in range(2)]
    names += MORE_SIGNALS
    g.s = {n: Signal(nc, n) for n in names}
    g.scratch = {n: nc.dram_tensor(f"scratch_{n}", shape, F32, kind="Internal").ap() for n, shape in
                 (("q", (B * 16 * 24, T)), ("k", (B * 16 * 24, T)), ("comb", (9, N)),
                  ("alibi", (16, 2, T)))}
    g.xT = nc.alloc_sbuf_tensor("x_keep", [P, N], F32)
    g.hT = nc.alloc_sbuf_tensor("h_keep", [P, N], F32)
    g.squares = nc.alloc_sbuf_tensor("squares_keep", [P, len(SQUARES), P], F32)
    g.columns = nc.alloc_sbuf_tensor("columns_keep", [P, len(COLUMNS)], F32)
    g.consts = nc.alloc_sbuf_tensor("consts_keep", [P, 6 * P + 16], F32)
    g.iota = g.consts[:, 6 * P + 8:6 * P + 16]
    g.gate_w = nc.alloc_sbuf_tensor("gate_w_keep", [P, 3, EXPERTS], F32)
    g.gate_b = nc.alloc_sbuf_tensor("gate_b_keep", [P, 2, EXPERTS], F32)
    g.l3_w = nc.alloc_sbuf_tensor("l3_w", [P, 3, 4 * P], F32)
    g.wo2 = nc.alloc_sbuf_tensor("wo2", [P, P], F32)
    g.v_tok = nc.alloc_sbuf_tensor("v_tok", [P, N], F32)
    g.att_tok = nc.alloc_sbuf_tensor("att_tok", [P, N], F32)
    g.cs = nc.alloc_sbuf_tensor("silu_c", [P, 16], F32)
    g.mod = nc.alloc_sbuf_tensor("mod", [P, 4, 6, B], F32)
    g.gate_bias = nc.alloc_sbuf_tensor("gate_bias", [P, 2, B], F32)
    g.rms_w = nc.alloc_sbuf_tensor("rms_w", [P, 1], F32)
    g.neg_lam = nc.alloc_sbuf_tensor("neg_lam", [P, 1], F32)
    g.eps = nc.alloc_sbuf_tensor("eps", [P, 2], F32)
    const = lambda n: g.consts[:, n * P:(n + 1) * P]
    g.identity, g.mean_w, g.centre_w, g.tri, g.all_ones, g.before = (
        const(n) for n in range(6))
    g.den_eps = lambda hd: g.consts[:, 6 * P:6 * P + 1] if hd == 8 else g.eps[:, 1:2]
    g.square = lambda name: g.squares[:, SQUARES.index(name)]
    g.col = lambda name: g.columns[:, COLUMNS.index(name):COLUMNS.index(name) + 1]
    g.modcol = lambda layer, j: (lambda c: g.mod[:, layer, j, c:c + 1])

    with nc.Block() as block:
        @block.sync
        def _(sp):
            for signal in g.s.values():
                sp.sem_inc(signal.sem, START)

    def dump(name):
        if debug and name in debug:
            with nc.Block() as block:
                @block.sync
                def _(sp):
                    src = g.hT if name.startswith("h") else g.xT
                    sp.dma_start(debug[name], src[:]).then_inc(g.s["dma"].sem, 16)
                    sp.wait_ge(g.s["dma"].sem, g.s["dma"].at(16))
            g.s["dma"].end(16)

    setup_phase(nc, g)
    dump("h0")
    q_stack, k_stack, v_group = small_head_stacks(g)
    with q_stack as qs, k_stack as ks, v_group as vg:
        small_head_projections(nc, g, (qs, ks, vg), 8, "L0_Wq", "L0_Wk", "L0_Wv")
        small_head_attention(nc, g, (qs, ks, vg), 8, float(8 ** -0.5))
    attention_output(nc, g, 0, g.square("L0_Wo"), True)
    dump("x0")
    norm_phase(nc, g, g.xT, g.modcol(0, SCALE_B), g.modcol(0, SHIFT_B))
    dump("h1")
    experts_phase(nc, g, 0, "norm", 0, ["L0_w1"], "L0_w2", EXPERTS, 512, False, "L0_b1", "L0_b2")
    dump("x1")

    norm_phase(nc, g, g.xT, g.modcol(1, SCALE_A), g.modcol(1, SHIFT_A))
    dump("h2")
    with g.sb("att1", [P, N // P, 16 * 64], F32) as g.att1:
        alibi_attention(nc, g)
        alibi_output(nc, g)
    dump("x2")
    norm_phase(nc, g, g.xT, g.modcol(1, SCALE_B), g.modcol(1, SHIFT_B))
    experts_phase(nc, g, 1, "open", 1, ["L1_w1", "L1_w3"], "L1_w2", EXPERTS + 1, 256, True)
    dump("x3")

    norm_phase(nc, g, g.xT, g.modcol(2, SCALE_A), g.modcol(2, SHIFT_A))
    dump("h4")
    q_stack, k_stack, v_group = small_head_stacks(g)
    with q_stack as qs, k_stack as ks, v_group as vg:
        small_head_projections(nc, g, (qs, ks, vg), 4, "L2_Wq", "L2_Wk", "L2_Wv", "L2_Wqs", "L2_Wks")
        small_head_attention(nc, g, (qs, ks, vg), 4, 0.5, differential=True)
    head_rms_phase(nc, g)
    attention_output(nc, g, 2, g.wo2[:], False)
    dump("x4")
    norm_phase(nc, g, g.xT, g.modcol(2, SCALE_B), g.modcol(2, SHIFT_B))
    linear_chain_phase(nc, g)
    dump("x5")

    norm_phase(nc, g, g.xT, g.modcol(3, SCALE_A), g.modcol(3, SHIFT_A))
    dump("h6")
    linear_attention(nc, g)
    residual_output(nc, g)
    gamma, beta = (lambda c: g.col("L3_gamma")), (lambda c: g.col("L3_beta"))
    norm_phase(nc, g, g.hT, gamma, beta)
    gelu_ffn(nc, g)
    norm_phase(nc, g, g.hT, gamma, beta)
    gated_add(nc, g, 3, GATE_A)
    dump("x6")
    norm_phase(nc, g, g.xT, g.modcol(3, SCALE_B), g.modcol(3, SHIFT_B))
    dump("h7")
    experts_phase(nc, g, 3, "each", 2, ["L3_gate", "L3_up"], "L3_down", EXPERTS, 256, True)

    with nc.Block() as block:
        @block.sync
        def _(sp):
            sp.dma_start(dram["outT"], g.xT[:]).then_inc(g.s["dma"].sem, 16)
            sp.wait_ge(g.s["dma"].sem, g.s["dma"].at(16))


MORE_SIGNALS = ["lo0", "raw0", "bias_out", "weighted0", "dma_x", "dma_c", "late", "modulated", "primed", "mod_act", "mod_dve",
                "v_mm", "load_v", "h_hi", "logits", "totals", "counts", "route", "bias0", "bias1",
                "log", "full", "w_hi", "w_lo", "w_split", "comb0", "comb1", "chosen", "first", "up", "hidden", "silu", "down", "weighted", "added", "hi", "lo", "kb",
                "recip", "feat", "clip", "alibi0", "alibi1", "alibi2", "alibi3"]


def host_arrays(inp):
    a = {k: np.asarray(v) for k, v in inp.items()}
    t = np.transpose
    out = {"xT": np.ascontiguousarray(a["L0_attn_x"].reshape(N, P).T)}
    out["cT"] = np.ascontiguousarray(np.concatenate([a[f"L{i}_c"] for i in range(4)]).T)
    for i in range(4):
        out[f"L{i}_wmod"] = np.ascontiguousarray(a[f"L{i}_wmod"])
    out["lambdas"] = np.stack([a[f"L2_attn_lambda_{n}"] for n in ("q1", "k1", "q2", "k2")])
    swap = np.arange(P) ^ 1
    qkv3 = np.split(a["L3_attn_w_qkv"], 3)
    squares = [a["L0_attn_Wq"].T, a["L0_attn_Wk"].T, a["L0_attn_Wv"].T, a["L0_attn_Wo"].T,
               a["L2_attn_Wq"].T, a["L2_attn_Wq"][swap].T, a["L2_attn_Wk"].T, a["L2_attn_Wk"][swap].T,
               a["L2_attn_Wv"].T, a["L2_attn_Wo"].T,
               a["L2_ffn_weight"], a["L2_ffn_aux_weight1"], a["L2_ffn_aux_weight2"],
               qkv3[0].T, qkv3[1].T, qkv3[2].T, a["L3_attn_w_out"].T]
    out["squares"] = np.ascontiguousarray(np.stack(squares, axis=1))
    out["columns"] = np.ascontiguousarray(np.stack(
        [a["L0_attn_bo"], a["L1_attn_b_out"], np.tile(a["L2_attn_rms_weight"], 16), a["L2_ffn_bias"],
         a["L3_attn_b_out"], a["L3_attn_gamma"], a["L3_attn_beta"], a["L3_attn_b2"],
         *a["L3_attn_b1"].reshape(4, P)], axis=1))
    i = np.arange(P)
    tri = i[:, None] <= i[None, :]
    before = (i[:, None] // EXPERTS < i[None, :] // EXPERTS) & (i[:, None] % EXPERTS == i[None, :] % EXPERTS)
    den_eps = np.zeros((P, 16))
    den_eps[8::32, 0] = 1e-8
    den_eps[:, 8:16] = np.arange(EXPERTS) - EXPERTS
    out["consts"] = np.concatenate([np.eye(P), np.full((P, P), 1 / P), np.eye(P) - 1 / P, tri,
                                    np.ones((P, P)), before, den_eps], axis=1).astype(np.float32)
    angle = (1.0 / 10000.0 ** np.linspace(0.0, 1.0, 2)).astype(np.float32)
    f = np.arange(T, dtype=np.float32)[None, :] * angle[(i % 4) // 2][:, None]
    out["rope"] = np.stack([np.cos(f), np.sin(f) * np.where(i % 2, 1, -1)[:, None]], axis=1).astype(np.float32)
    bf = mybir.dt.np(BF16)
    above = np.where(i[None, :] > i[:, None], -1e30, 0.0)
    out["mask"] = np.stack([np.eye(P), above, above.T], axis=1).astype(bf)
    slope = np.array([(2 ** -0.5) ** (h + 1) for h in range(16)])
    al = (8 * slope[:, None] * np.arange(T)[None, :]).astype(np.float32)
    hi = (al.view(np.uint32) & np.uint32(0xFFFFF000)).view(np.float32)
    out["alibi"] = np.stack([hi, al - hi], axis=1)
    j = np.arange(4)
    out["kv_mask"] = np.broadcast_to((i[:, None] // 32 == j[None, :])[:, :, None], (P, 4, 9)).astype(np.float32)

    c = np.ascontiguousarray
    out["gate_w"] = c(np.stack([a["L0_ffn_gate_w"], a["L1_ffn_gate_w"].T, a["L3_ffn_gate_w"].T], axis=1))
    out["gate_b"] = c(np.stack([a["L0_ffn_gate_b"], a["L1_ffn_gate_bias"]]))
    out["L0_w1"], out["L0_w2"], out["L0_b2"] = a["L0_ffn_w1"], a["L0_ffn_w2"], a["L0_ffn_b2"]
    out["L0_b1"] = c(a["L0_ffn_b1"].reshape(EXPERTS, 4, P).transpose(0, 2, 1))
    wq = a["L1_attn_w_qkv"].reshape(P, 3, 16, 64)
    out["L1_wqk"] = c(wq.transpose(2, 0, 1, 3)[:, :, [0, 0, 1, 1]])
    out["L1_wv"] = c(wq[:, 2].reshape(P, 8, 2 * 64).transpose(1, 0, 2))
    out["L1_wout"] = c(a["L1_attn_w_out"].reshape(8, P, P).transpose(1, 0, 2))
    for n in ("w1", "w2", "w3"):
        both = np.concatenate([a[f"L1_ffn_{n}"], a[f"L1_ffn_s{n}"][None]])
        out[f"L1_{n}"] = c(both.transpose(0, 2, 1))
    pm = np.zeros((P, 16, 32), np.float32)
    for h in range(16):
        pm[8 * h:8 * h + 8, h] = a["L3_attn_proj"][h]
    out["L3_w"] = c(np.stack([pm.reshape(P, 512), a["L3_attn_w1"].T,
                              a["L3_attn_w2"].T.reshape(4, P, P).transpose(1, 0, 2).reshape(P, 512)], axis=1))
    for n, m in (("gate", "gate_proj_w"), ("up", "up_proj_w"), ("down", "down_proj_w")):
        out[f"L3_{n}"] = c(a[f"L3_ffn_{m}"].transpose(0, 2, 1))
    return out


def kernel(**inputs):
    import concourse.bacc as bacc
    from concourse.bass_utils import run_bass_kernel_spmd as run

    arrays = host_arrays(inputs)
    nc = bacc.Bacc("TRN2", target_bir_lowering=False, num_devices=1)
    dram = {k: nc.dram_tensor(f"in_{k}", v.shape, mybir.dt.from_np(v.dtype), kind="ExternalInput").ap()
            for k, v in arrays.items()}
    dram["outT"] = nc.dram_tensor("outT", (P, N), F32, kind="ExternalOutput").ap()
    build(nc, dram)
    r = run(nc, [{f"in_{k}": v for k, v in arrays.items()}], core_ids=[0])
    return np.ascontiguousarray(r.results[0]["outT"].T).reshape(B, T, P)
```
